# Optimizing a Trainium2 kernel written in Bass

```python
import numpy as np
import jax
import jax.numpy as jnp

def _softmax(x, axis=-1):
    return jax.nn.softmax(x, axis=axis)

def _gelu(x):
    return jax.nn.gelu(x, approximate=True)

def _silu(x):
    return jax.nn.silu(x)

def _sigmoid(x):
    return jax.nn.sigmoid(x)

def _layernorm(x, axis=-1, eps=1e-05):
    m = jnp.mean(x, axis=axis, keepdims=True)
    v = jnp.var(x, axis=axis, keepdims=True)
    return (x - m) / jnp.sqrt(v + eps)

def _scatter_add(tgt, idx, src, axis=0):
    return tgt.at[idx].add(src)

def _segment_sum(src, seg, n):
    return jax.ops.segment_sum(src, seg, n)
kernel_name = 'mk_early_fusion_d1_tok_img1024_r4_0dfabd'

def setup_inputs(seed: int=0):
    np.random.seed(seed)
    _w = jnp.asarray

    def _rec_inputs():
        import jax
        import jax.numpy as jnp
        _rk = jax.random.key(seed)
        x = -0.00016672 + 0.999947 * jax.random.normal(jax.random.fold_in(_rk, 1), (16, 3, 128, 128), jnp.float32)
        txt = -1.57589e-10 + 0.999995 * jax.random.normal(jax.random.fold_in(_rk, 2), (16, 77, 256), jnp.float32)
        return (x, txt)
    x, txt = _rec_inputs()

    def _L0_tok_setup():
        import jax, jax.numpy as jnp
        import numpy as np
        P = 16
        EPS = 1e-05

        def _layernorm(x, g, b):
            mu = jnp.mean(x, axis=-1, keepdims=True)
            var = jnp.mean(jnp.square(x - mu), axis=-1, keepdims=True)
            return (x - mu) * jax.lax.rsqrt(var + EPS) * g + b
        key = jax.random.key(seed)
        k1, k2 = jax.random.split(key)
        B, C, H, Wd = (64, 3, 96, 96)
        patch_dim, dim = (P * P * C, 256)
        return {'x': jax.random.normal(k1, (B, C, H, Wd), dtype=jnp.float32), 'ln1_g': jnp.ones((patch_dim,), jnp.float32), 'ln1_b': jnp.zeros((patch_dim,), jnp.float32), 'W': jax.random.normal(k2, (dim, patch_dim), dtype=jnp.float32) * patch_dim ** (-0.5), 'b': jnp.zeros((dim,), jnp.float32), 'ln2_g': jnp.ones((dim,), jnp.float32), 'ln2_b': jnp.zeros((dim,), jnp.float32)}
    _L0_tok_all = _L0_tok_setup()
    _L0_tok_in = {k: v for k, v in _L0_tok_all.items() if k in ('ln1_g', 'ln1_b', 'W', 'b', 'ln2_g', 'ln2_b')}
    del _L0_tok_all

    def _L0_attn_setup():
        import jax, jax.numpy as jnp
        import numpy as np
        B, T, G, H = (4, 512, 256, 16)
        HD = G // H
        key = jax.random.key(seed)
        ks = jax.random.split(key, 5)
        s = 1.0 / np.sqrt(G).astype(np.float32)
        return {'x': jax.random.normal(ks[0], (B, T, G), jnp.float32), 'wq': jax.random.normal(ks[1], (G, G), jnp.float32) * s, 'bq': jnp.zeros((G,), jnp.float32), 'wk': jax.random.normal(ks[2], (G, G), jnp.float32) * s, 'bk': jnp.zeros((G,), jnp.float32), 'wv': jax.random.normal(ks[3], (G, G), jnp.float32) * s, 'bv': jnp.zeros((G,), jnp.float32), 'wp': jax.random.normal(ks[4], (G, G), jnp.float32) * s, 'bp': jnp.zeros((G,), jnp.float32)}
    _L0_attn_all = _L0_attn_setup()
    _L0_attn_in = {k: v for k, v in _L0_attn_all.items() if k in ('wq', 'bq', 'wk', 'bk', 'wv', 'bv', 'wp', 'bp')}
    del _L0_attn_all

    def _L0_ffn_setup():
        import jax, jax.numpy as jnp
        import numpy as np
        DIM = 256
        HID = 512
        OUT = 256
        NE = 8
        TOPK = 2

        def _xavier(key, shape):
            fan_in, fan_out = (shape[-2], shape[-1])
            lim = jnp.sqrt(6.0 / (fan_in + fan_out))
            return jax.random.uniform(key, shape, jnp.float32, -lim, lim)
        key = jax.random.key(seed)
        ks = jax.random.split(key, 8)
        X = jax.random.normal(ks[0], (4, 256, DIM), jnp.float32)
        W1 = _xavier(ks[1], (NE, DIM, HID))
        W3 = _xavier(ks[2], (NE, DIM, HID))
        W2 = _xavier(ks[3], (NE, HID, OUT))
        b1 = jnp.zeros((NE, HID), jnp.float32)
        b3 = jnp.zeros((NE, HID), jnp.float32)
        b2 = jnp.zeros((NE, OUT), jnp.float32)
        Wg = _xavier(ks[4], (DIM, NE))
        bg = jnp.zeros((NE,), jnp.float32)
        Wf = _xavier(ks[5], (OUT, OUT))
        bf = jnp.zeros((OUT,), jnp.float32)
        return {'X': X, 'W1': W1, 'b1': b1, 'W3': W3, 'b3': b3, 'W2': W2, 'b2': b2, 'Wg': Wg, 'bg': bg, 'Wf': Wf, 'bf': bf}
    _L0_ffn_all = _L0_ffn_setup()
    _L0_ffn_in = {k: v for k, v in _L0_ffn_all.items() if k in ('W1', 'b1', 'W3', 'b3', 'W2', 'b2', 'Wg', 'bg', 'Wf', 'bf')}
    del _L0_ffn_all
    return {'x': x, 'txt': txt, 'L0_tok_ln1_g': _L0_tok_in['ln1_g'], 'L0_tok_ln1_b': _L0_tok_in['ln1_b'], 'L0_tok_W': _L0_tok_in['W'], 'L0_tok_b': _L0_tok_in['b'], 'L0_tok_ln2_g': _L0_tok_in['ln2_g'], 'L0_tok_ln2_b': _L0_tok_in['ln2_b'], 'L0_attn_wq': _L0_attn_in['wq'], 'L0_attn_bq': _L0_attn_in['bq'], 'L0_attn_wk': _L0_attn_in['wk'], 'L0_attn_bk': _L0_attn_in['bk'], 'L0_attn_wv': _L0_attn_in['wv'], 'L0_attn_bv': _L0_attn_in['bv'], 'L0_attn_wp': _L0_attn_in['wp'], 'L0_attn_bp': _L0_attn_in['bp'], 'L0_ffn_W1': _L0_ffn_in['W1'], 'L0_ffn_b1': _L0_ffn_in['b1'], 'L0_ffn_W3': _L0_ffn_in['W3'], 'L0_ffn_b3': _L0_ffn_in['b3'], 'L0_ffn_W2': _L0_ffn_in['W2'], 'L0_ffn_b2': _L0_ffn_in['b2'], 'L0_ffn_Wg': _L0_ffn_in['Wg'], 'L0_ffn_bg': _L0_ffn_in['bg'], 'L0_ffn_Wf': _L0_ffn_in['Wf'], 'L0_ffn_bf': _L0_ffn_in['bf']}

def reference(x, txt, L0_tok_ln1_g, L0_tok_ln1_b, L0_tok_W, L0_tok_b, L0_tok_ln2_g, L0_tok_ln2_b, L0_attn_wq, L0_attn_bq, L0_attn_wk, L0_attn_bk, L0_attn_wv, L0_attn_bv, L0_attn_wp, L0_attn_bp, L0_ffn_W1, L0_ffn_b1, L0_ffn_W3, L0_ffn_b3, L0_ffn_W2, L0_ffn_b2, L0_ffn_Wg, L0_ffn_bg, L0_ffn_Wf, L0_ffn_bf):
    import jax
    import jax.numpy as jnp

    def _L0_tok_ref(x, ln1_g, ln1_b, W, b, ln2_g, ln2_b):
        import jax, jax.numpy as jnp
        import numpy as np
        P = 16
        EPS = 1e-05

        def _layernorm(x, g, b):
            mu = jnp.mean(x, axis=-1, keepdims=True)
            var = jnp.mean(jnp.square(x - mu), axis=-1, keepdims=True)
            return (x - mu) * jax.lax.rsqrt(var + EPS) * g + b
        B, C, H, Wd = x.shape
        h, w = (H // P, Wd // P)
        t = x.reshape(B, C, h, P, w, P)
        t = t.transpose(0, 2, 4, 3, 5, 1).reshape(B, h * w, P * P * C)
        t = _layernorm(t, ln1_g, ln1_b)
        t = jnp.einsum('bnp,dp->bnd', t, W) + b
        return _layernorm(t, ln2_g, ln2_b)

    def _L0_attn_ref(x, wq, bq, wk, bk, wv, bv, wp, bp):
        import jax, jax.numpy as jnp
        import numpy as np
        B, T, G, H = (4, 512, 256, 16)
        HD = G // H
        b, t, g = x.shape

        def split_heads(y):
            return y.reshape(b, t, H, HD).transpose(0, 2, 1, 3)
        q = split_heads(x @ wq + bq)
        k = split_heads(x @ wk + bk)
        v = split_heads(x @ wv + bv)
        scale = 1.0 / np.sqrt(HD).astype(np.float32)
        att = jnp.einsum('bhqd,bhkd->bhqk', q, k) * scale
        causal = jnp.tril(jnp.ones((t, t), bool))
        att = jnp.where(causal[None, None], att, -jnp.inf)
        att = jax.nn.softmax(att, axis=-1)
        y = jnp.einsum('bhqk,bhkd->bhqd', att, v)
        y = y.transpose(0, 2, 1, 3).reshape(b, t, g)
        return y @ wp + bp

    def _L0_ffn_ref(X, W1, b1, W3, b3, W2, b2, Wg, bg, Wf, bf):
        import jax, jax.numpy as jnp
        import numpy as np
        DIM = 256
        HID = 512
        OUT = 256
        NE = 8
        TOPK = 2

        def _xavier(key, shape):
            fan_in, fan_out = (shape[-2], shape[-1])
            lim = jnp.sqrt(6.0 / (fan_in + fan_out))
            return jax.random.uniform(key, shape, jnp.float32, -lim, lim)
        gating = jax.nn.softmax(X @ Wg + bg, axis=-1)
        top_k_indices = jnp.argsort(gating, axis=-1)[..., -TOPK:]
        h1 = jnp.einsum('bsd,edh->bseh', X, W1) + b1
        h3 = jnp.einsum('bsd,edh->bseh', X, W3) + b3
        h = jax.nn.silu(h1 * h3)
        expert_outputs = jnp.einsum('bseh,eho->bseo', h, W2) + b2
        topk_out = jnp.take_along_axis(expert_outputs, top_k_indices[..., None], axis=2)
        topk_w = jnp.take_along_axis(gating, top_k_indices, axis=-1)
        mixed = jnp.sum(topk_w[..., None] * topk_out, axis=2)
        return mixed @ Wf + bf
    h = _L0_tok_ref(x, L0_tok_ln1_g, L0_tok_ln1_b, L0_tok_W, L0_tok_b, L0_tok_ln2_g, L0_tok_ln2_b)
    h = jnp.concatenate([h, txt], axis=1)
    h = h + _L0_attn_ref(_layernorm(h, axis=-1), L0_attn_wq, L0_attn_bq, L0_attn_wk, L0_attn_bk, L0_attn_wv, L0_attn_bv, L0_attn_wp, L0_attn_bp)
    h = h + _L0_ffn_ref(_layernorm(h, axis=-1), L0_ffn_W1, L0_ffn_b1, L0_ffn_W3, L0_ffn_b3, L0_ffn_W2, L0_ffn_b2, L0_ffn_Wg, L0_ffn_bg, L0_ffn_Wf, L0_ffn_bf)
    return h

_drawn_inputs = setup_inputs


def setup_inputs(seed=0):
    import zlib

    import numpy as np

    out = dict(_drawn_inputs(seed))
    spreads = {'L0_tok_ln1_g': (1.0, 0.2),
     'L0_tok_ln1_b': (0.0, 0.1),
     'L0_tok_b': (0.0, 0.1),
     'L0_tok_ln2_g': (1.0, 0.2),
     'L0_tok_ln2_b': (0.0, 0.1),
     'L0_attn_bq': (0.0, 0.334),
     'L0_attn_bk': (0.0, 0.8),
     'L0_attn_bv': (0.0, 0.1),
     'L0_attn_bp': (0.0, 0.1),
     'L0_ffn_b1': (0.0, 0.286),
     'L0_ffn_b3': (0.0, 0.284),
     'L0_ffn_b2': (0.0, 0.1),
     'L0_ffn_bg': (0.0, 0.295),
     'L0_ffn_bf': (0.0, 0.1)}
    factors = {}
    for name, (base, spread) in spreads.items():
        noise = np.random.default_rng([zlib.crc32(name.encode()), seed]).standard_normal(out[name].shape)
        drawn = base * np.exp(spread * noise) if base else spread * noise
        out[name] = jnp.asarray(drawn.astype(out[name].dtype))
    for name, factor in factors.items():
        out[name] = (out[name] * factor).astype(out[name].dtype)
    return out
```

```python
import concourse.bass as bass
from concourse import mybir
from contextlib import ExitStack


def early_fusion_block(nc, A, out):
    fp32 = mybir.dt.float32
    bf16 = mybir.dt.bfloat16
    fp16 = mybir.dt.float16
    ALU = mybir.AluOpType
    ACT = mybir.ActivationFunctionType
    AX = mybir.AxisListType

    P = 128
    B = 16
    C, PS = 3, 16
    G = 8
    IMG = G * G
    TXT = 77
    T = IMG + TXT
    TL = T - P
    N = B * T
    D = 256
    KD = D // P
    H, HD = 16, 16
    E, HID = 8, 512
    MH = HID // P
    NI = G
    NT = NI + (TXT + 7) // 8
    LAST = TXT - 8 * (NT - NI - 1)
    NP = NT * P
    EPS = 1e-5
    BIG = -1e30
    SCALE = HD ** -0.5
    FC = C * PS * PS // P
    QG = [(0, 0, 8), (0, 8, 8), (1, 0, 6), (1, 6, 5), (1, 11, 5), (2, 0, 16)]
    PART = [(0, IMG), (IMG, T - LAST), (T - LAST, T)]
    SROWS = 3 * HD
    TS = 160

    def tile_rows(i):
        return P if i < NT - 1 else B * LAST

    def flat_cols(v, g):
        part, b0, n = g
        return v.rearrange("p (b t) -> p b t", t=T)[:, b0:b0 + n, PART[part][0]:PART[part][1]]

    def tile_cols(v, g):
        part, b0, n = g
        if part == 0:
            return v[:, 0:NI * P].rearrange("p (w b hh) -> p b hh w", w=NI, b=B)[:, b0:b0 + n]
        if part == 1:
            return v[:, NI * P:(NT - 1) * P].rearrange("p (j b t) -> p b j t", b=B, t=8)[:, b0:b0 + n]
        o = (NT - 1) * P
        return v[:, o + LAST * b0:o + LAST * (b0 + n)].rearrange("p (b t) -> p b t", t=LAST)

    def tile_order(v, b, part):
        if part == 0:
            return v[:, :, 0:NI * P].rearrange("p k (w c) -> p k w c", c=P)[:, :, :, 8 * b:8 * b + 8].rearrange(
                "p k w hh -> p k hh w")
        if part == 1:
            return v[:, :, NI * P:(NT - 1) * P].rearrange("p k (j c) -> p k j c", c=P)[:, :, :, 8 * b:8 * b + 8]
        o = (NT - 1) * P + LAST * b
        return v[:, :, o:o + LAST]

    def dram_tile(v, i):
        if i < NI:
            return v[:, i:IMG:G, :]
        a = IMG + 8 * (i - NI)
        return v[:, a:min(a + 8, T), :]

    qk_dram = nc.dram_tensor("qk_scratch", (2, 2, D, N), fp16, kind="Internal").ap()
    v_dram = nc.dram_tensor("v_scratch", (B, T, H * (HD + 1)), fp32, kind="Internal").ap()

    ctx = ExitStack()
    with ctx:
        def sb(name, shape, dt=fp32):
            return ctx.enter_context(nc.sbuf_tensor(name, shape, dt))

        def sem(name):
            return ctx.enter_context(nc.semaphore(name))

        ident = sb("ident", [P, P])
        identb = sb("identb", [P, P], bf16)
        identh = sb("identh", [P, P], fp16)
        mask_q = sb("mask_q", [P, P], bf16)
        mask_k = sb("mask_k", [P, P], bf16)
        mask_l = sb("mask_l", [32, T], bf16)
        tri = sb("tri", [P, E, E])
        ones = sb("ones", [P, P])

        h = sb("h", [P, NT, D])
        shared_a = sb("shared_a", [P, 6144])
        shared_b = sb("shared_b", [P, 9024])
        shared_c = sb("shared_c", [P, 4608])
        img = shared_a[:, :].rearrange("p (c y x) -> p c y x", c=C, y=PS)
        qk = shared_b[:, :].bitcast(fp16).rearrange("p (w s n) -> p w s n", w=4, s=2)
        xnT = shared_c[:, :].rearrange("p (k n) -> p k n", k=KD)
        mixed = shared_b[:, 0:NT * D].rearrange("p (t d) -> p t d", t=NT)
        WE = 2 * KD * HID + MH * D
        stage = shared_b[:, NT * D:NT * D + WE]
        wbuf = shared_a[:, :].bitcast(fp16).rearrange("p (b s n) -> p b s n", b=2, s=2)
        xh = shared_c[:, 0:NP].bitcast(fp16).rearrange("p (k n) -> p k n", k=KD)
        xl = shared_c[:, NP:2 * NP].bitcast(fp16).rearrange("p (k n) -> p k n", k=KD)

        shared_d = sb("shared_d", [P, 6144])
        wtok, wT, wTg, wTb = (shared_d[:, 1536 * k:1536 * (k + 1)] for k in range(4))
        wtok = wtok.rearrange("p (k f) -> p k f", k=KD)
        wT, wTg, wTb = (w.rearrange("p (f d) -> p f d", f=FC) for w in (wT, wTg, wTb))
        crow = sb("crow", [P, D])
        tokn = sb("tokn", [P, 2, FC * P])
        tT = sb("tT", [P, 2, FC * P])
        rows = sb("rows", [P, 6, D])
        BTOK, G2, B2, BV, BP, BF = range(6)
        bg_row = sb("bg_row", [P, E])
        wqkv = sb("wqkv", [P, 4, KD, D])
        wf = sb("wf", [P, KD, D])
        wg = sb("wg", [P, KD, E])
        b2e = sb("b2e", [E, D])
        NB13 = 2 * E * MH
        lnraw = sb("lnraw", [4, C * P])
        b13raw = sb("b13raw", [NB13 + 4, P])
        cols = sb("cols", [P, NB13 + 4 + 4 * C])
        b13 = cols[:, 0:NB13]
        bqk = cols[:, NB13:NB13 + 4]

        def ln1(f, w):
            k = NB13 + 4 + 4 * (f % C) + 2 * w + f // C
            return cols[:, k:k + 1]

        st = sb("st", [P, NT, 3, 6])
        mv = sb("mv", [P, NT, 2])
        ve = sb("ve", [P, NT])
        sd = sb("sd", [P, NT])
        rstd = sb("rstd", [P, NT])
        xn = sb("xn", [P, 2, D])
        vt = sb("vt", [P, 2, H, HD + 1])

        Qs = sb("Qs", [64, 2, H, TS], fp16)
        Ks = sb("Ks", [64, 2, H, TS], fp16)
        Vm = sb("Vm", [P, 2, H, HD + 1])
        Vl = sb("Vl", [TL, 2, H, HD + 1])
        mx = sb("mx", [P, H + 4])
        mcat = sb("mcat", [P, 2, H + 4], fp16)
        mT = sb("mT", [2 * (H + 4), 2, P], fp16)
        pm = sb("pm", [P, H, P])
        pl = sb("pl", [P, H, TL])
        pr = sb("pr", [TL, H, TL])
        rd = sb("rd", [P, H])
        rdl = sb("rdl", [TL, H])
        at = sb("at", [P, H, HD])
        atl = sb("atl", [TL, H, HD])
        aT = xnT

        x2f = sb("x2f", [P, 2, KD, P])
        lg = sb("lg", [P, NT, E])
        gs = sb("gs", [P, NT])
        cmp1 = sb("cmp1", [P, NT, E, E], bf16)
        cmp2 = sb("cmp2", [P, NT, E, E], bf16)
        gwT = sb("gwT", [E, 2, P])
        t3 = pm[:, 0:4, :].rearrange("p a b -> p (a b)")
        t3 = pm[:, 0:8, :].rearrange("p (c a) b -> p c (a b)", c=2)
        uu = pm[:, 8:16, :].rearrange("p (c a) b -> p c (a b)", c=2)
        ss = shared_d[:, 4096:5120].rearrange("p (b n) -> p b n", b=2)
        sh = shared_d[:, 0:2048].bitcast(fp16).rearrange("p (b m n) -> p b m n", b=2, m=MH)
        sl = shared_d[:, 2048:4096].bitcast(fp16).rearrange("p (b m n) -> p b m n", b=2, m=MH)
        fT = shared_d[:, 5120:5632].rearrange("p (b k n) -> p b k n", b=2, k=KD)
        ot = sb("ot", [P, 2, D])

        ps = ctx.enter_context(nc.psum_tensor("ps", [P, 8 * 512], fp32))

        def bank(k, n=512):
            return ps[:, 512 * k:512 * k + n]

        s_ws = sem("wtok_in"); s_img = sem("image_in"); s_par = sem("params_in"); s_wt2 = sem("weights_in")
        s_txt = sem("text_in"); s_vout = [sem("v_out0"), sem("v_out1")]
        s_qkout = sem("qk_out")
        s_stack = [sem("stack_in0"), sem("stack_in1")]; s_mrow = [sem("mrow_in0"), sem("mrow_in1")]
        s_we = sem("expert_w_in"); s_out = [sem("out_done0"), sem("out_done1")]
        c_const = sem("consts_ready"); c_i0 = sem("ident_zeroed"); c_hb = sem("h_plus_bp"); c_hf = sem("h_plus_bf")
        c_hi = sem("w_hi"); c_w = sem("w_split"); c_sh = sem("s_hi")
        d_ = sem("vector_steps"); d_h0 = sem("h_tail_zeroed")
        d_ve = sem("var_ready"); d_wg = sem("wT_scaled"); d_crow = sem("crow_ready")
        d_tok = sem("patch_normed"); d_emb = sem("embed_taken"); d_xn = sem("xn_ready"); d_v = sem("v_ready")
        d_lo = sem("qk_lo"); d_hdone = sem("h_ln_done"); d_mx = sem("max_taken"); d_mc = sem("mcat_ready")
        d_mT = sem("mT_ready"); d_at = sem("attn_normed"); d_pr = sem("proj_added"); d_x2 = sem("xn2_ready")
        d_xl = sem("x_lo"); d_lg = sem("logits_ready"); d_gw = sem("gates_ready"); d_mix0 = sem("mix_init")
        d_u = sem("u_ready"); d_sl = sem("s_lo"); d_acc = sem("out_taken"); d_o = sem("o_ready"); d_gt = sem("gwT_taken")
        a_wt = sem("wT_copied"); a_sd = sem("std_ready"); a_tT = sem("patchT_copied"); a_xT = sem("xnT_copied")
        a_hi = sem("qk_hi"); a_ex = sem("exp_done"); a_aT = sem("attnT_copied"); a_x2 = sem("x2f_copied")
        a_xh = sem("x_hi"); a_ge = sem("gate_exp"); a_t3 = sem("h3_biased"); a_s = sem("silu_done")
        a_b = sem("biases_copied"); a_fT = sem("mixT_copied")
        p_wt = sem("wT_done"); p_cr = sem("crow_done"); p_tT = sem("patchT_done"); p_emb = sem("embed_done")
        p_xT = sem("xnT_done"); p_v = sem("v_done"); p_qk = sem("qk_done"); p_S = sem("S_done"); p_St = sem("St_done")
        p_mT = sem("mT_done"); p_pv = sem("pv_done"); p_aT = sem("attnT_done"); p_pj = sem("proj_done")
        p_x2 = sem("x2T_done"); p_lg = sem("logits_done"); p_gT = sem("gwT_done"); p_m0 = sem("mix0_done")
        p_h = sem("h13_done"); p_o = sem("expert_out_done"); p_b = sem("b13_done"); p_fT = sem("mixT_done")
        p_f = sem("final_done")

        NPAR = 14
        NE_BLK = [(n * 512, min(512, NP - n * 512)) for n in range((NP + 511) // 512)]
        NBLK = len(NE_BLK)

        block = ctx.enter_context(nc.Block())

        def qk_bank(u):
            part, _, n = QG[u % len(QG)]
            m = PART[part][1] - PART[part][0]
            return bank(u % 4, n * m).rearrange("p (b t) -> p b t", b=n)

        @block.sync
        def _(sp):
            sp.dma_start(wtok[:, :, :], A["L0_tok_W"].rearrange("(m p) f -> p m f", p=P)).then_inc(s_ws, 16)
            for c in range(C):
                sp.dma_start(shared_a[:, 2048 * c:2048 * (c + 1)],
                             A["x"][:, c, :, :].rearrange("b (hh y) x -> b hh (y x)", y=PS)).then_inc(s_img, 16)
            sp.wait_ge(d_h0, 1)
            for j in range(NT - NI):
                i = NI + j
                sp.dma_start(h[0:tile_rows(i), i, :], A["txt"][:, 8 * j:min(8 * j + 8, TXT), :]).then_inc(s_txt, 16)
            for w, name in enumerate(("wq", "wk", "wv", "wp")):
                sp.dma_start(wqkv[:, w, :, :], A["L0_attn_" + name].rearrange("(k p) n -> p k n", p=P)).then_inc(s_wt2, 16)
            sp.dma_start(wf[:, :, :], A["L0_ffn_Wf"].rearrange("(k p) n -> p k n", p=P)).then_inc(s_wt2, 16)
            sp.dma_start(wg[:, :, :], A["L0_ffn_Wg"].rearrange("(k p) n -> p k n", p=P)).then_inc(s_wt2, 16)
            for i in range(NT):
                sp.wait_ge(d_v, i + 1)
                sp.dma_start(dram_tile(v_dram, i), vt[0:tile_rows(i), i % 2, :, :].rearrange("p h d -> p (h d)")
                             ).then_inc(s_vout[i % 2], 16)
            for w in range(4):
                sp.wait_ge(d_lo, len(QG) * (w + 1))
                for k in range(2):
                    sp.dma_start(qk_dram[w // 2, k, P * (w % 2):P * (w % 2) + P, :], qk[:, w, k, :]).then_inc(s_qkout, 16)
            sp.wait_ge(s_vout[0], 16 * (NT // 2))
            sp.wait_ge(s_vout[1], 16 * (NT // 2))

            def load_stack(b):
                sp.wait_ge(s_qkout, 16 * 8)
                if b >= 2:
                    sp.wait_ge(p_pv, b - 1)
                t0 = b * T
                for w, dst, parts in ((0, Qs, (0, 1, 0)), (1, Ks, (0, 0, 1))):
                    for r, s in enumerate(parts):
                        sp.dma_start(dst[HD * r:HD * (r + 1), b % 2, :, 0:T],
                                     qk_dram[w, s, :, t0:t0 + T].rearrange("(h d) t -> d h t", d=HD)
                                     ).then_inc(s_stack[b % 2], 16)
                sp.dma_start(Vm[:, b % 2, :, :].rearrange("p h d -> p (h d)"), v_dram[b, 0:P, :]).then_inc(s_stack[b % 2], 16)
                sp.dma_start(Vl[:, b % 2, :, :].rearrange("p h d -> p (h d)"), v_dram[b, P:T, :]).then_inc(s_stack[b % 2], 16)

            def load_mrow(b):
                sp.wait_ge(d_mT, b + 1)
                z = b % 2
                for s in range(2):
                    r = (H + 4) * s
                    sp.dma_start(Qs[SROWS + s:SROWS + s + 1, z, :, 0:P], mT[r:r + H, z, :]).then_inc(s_mrow[z], 16)
                    sp.dma_start(Qs[SROWS + s:SROWS + s + 1, z, :, P:T],
                                 mT[r + H:r + H + 4, z, :].rearrange("p (j t) -> p j t", j=4)[:, :, 0:TL]
                                 ).then_inc(s_mrow[z], 16)

            load_stack(0)
            load_stack(1)
            load_mrow(0)
            for b in range(B):
                if b + 1 < B:
                    load_mrow(b + 1)
                if b + 2 < B:
                    load_stack(b + 2)
            for e in range(E):
                if e:
                    sp.wait_ge(c_w, e)
                src = (A["L0_ffn_W1"], A["L0_ffn_W3"])
                for w in range(2):
                    sp.dma_start(stage[:, KD * HID * w:KD * HID * (w + 1)].rearrange("p (k n) -> p k n", k=KD),
                                 src[w][e].rearrange("(k p) n -> p k n", p=P)).then_inc(s_we, 16)
                sp.dma_start(stage[:, 2 * KD * HID:WE].rearrange("p (k n) -> p k n", k=MH),
                             A["L0_ffn_W2"][e].rearrange("(k p) n -> p k n", p=P)).then_inc(s_we, 16)
            for i in range(NT):
                sp.wait_ge(d_o, i + 1)
                sp.dma_start(dram_tile(out, i), ot[0:tile_rows(i), i % 2, :]).then_inc(s_out[i % 2], 16)
            sp.wait_ge(s_out[0], 16 * (NT // 2))
            sp.wait_ge(s_out[1], 16 * (NT // 2))

        @block.gpsimd
        def _(pool):
            for k, name in ((BTOK, "L0_tok_b"), (G2, "L0_tok_ln2_g"), (B2, "L0_tok_ln2_b"), (BV, "L0_attn_bv"),
                            (BP, "L0_attn_bp"), (BF, "L0_ffn_bf")):
                pool.dma_start(rows[:, k, :], A[name].rearrange("(o n) -> o n", o=1).to_broadcast([P, D])).then_inc(s_par, 16)
            pool.dma_start(bg_row[:, :], A["L0_ffn_bg"].rearrange("(o n) -> o n", o=1).to_broadcast([P, E])).then_inc(s_par, 16)
            for w, name in enumerate(("L0_tok_ln1_g", "L0_tok_ln1_b")):
                pool.dma_start(lnraw[2 * w:2 * w + 2, :], A[name].rearrange("(hf n) -> hf n", hf=2)).then_inc(s_par, 16)
            for w, name in enumerate(("L0_attn_bq", "L0_attn_bk")):
                pool.dma_start(b13raw[NB13 + 2 * w:NB13 + 2 * w + 2, :], A[name].rearrange("(m p) -> m p", p=P)).then_inc(s_par, 16)
            pool.dma_start(b2e[:, :], A["L0_ffn_b2"]).then_inc(s_par, 16)
            for w, name in enumerate(("L0_ffn_b1", "L0_ffn_b3")):
                pool.dma_start(b13raw[E * MH * w:E * MH * (w + 1), :], A[name].rearrange("e (m p) -> (e m) p", p=P)).then_inc(s_par, 16)
            z = [nc.gpsimd.memset(t[:, :], v) for t, v in
                 ((ident, 0.0), (identb, 0.0), (identh, 0.0), (mask_q, 0.0), (mask_k, 0.0), (mask_l, 0.0), (ones, 1.0))]
            z.append(nc.gpsimd.memset(tri[:, :, :], 1.0))
            z.append(nc.gpsimd.memset(Qs[:, :, :, :], 0.0))
            z.append(nc.gpsimd.memset(Ks[:, :, :, :], 1.0))
            z.append(nc.gpsimd.memset(vt[:, :, :, :], 1.0))
            z[-1].then_inc(c_i0, 1)
            pool.wait_ge(c_i0, 1)
            for m in (ident, identb, identh):
                nc.gpsimd.affine_select(out=m[:, :], in_=m[:, :], compare_op=ALU.not_equal, fill=1.0, base=0,
                                        pattern=[[-1, P]], channel_multiplier=1)
            nc.gpsimd.affine_select(out=mask_q[:, :], in_=mask_q[:, :], compare_op=ALU.is_ge, fill=BIG, base=0,
                                    pattern=[[-1, P]], channel_multiplier=1)
            nc.gpsimd.affine_select(out=mask_k[:, :], in_=mask_k[:, :], compare_op=ALU.is_ge, fill=BIG, base=0,
                                    pattern=[[1, P]], channel_multiplier=-1)
            nc.gpsimd.affine_select(out=mask_l[:, :], in_=mask_l[:, :], compare_op=ALU.is_ge, fill=BIG, base=P,
                                    pattern=[[-1, T]], channel_multiplier=1)
            nc.gpsimd.affine_select(out=tri[:, :, :], in_=tri[:, :, :], compare_op=ALU.is_gt, fill=0.0, base=0,
                                    pattern=[[-1, E], [1, E]], channel_multiplier=0).then_inc(c_const, 1)
            pool.wait_ge(d_xn, NT)
            pool.wait_ge(s_par, 16 * NPAR)
            nc.gpsimd.tensor_tensor(h[:, :, :], h[:, :, :], rows[:, BP:BP + 1, :].to_broadcast([P, NT, D]), ALU.add).then_inc(c_hb, 1)
            for e in range(E):
                pool.wait_ge(s_we, 48 * (e + 1))
                if e >= 2:
                    pool.wait_ge(p_o, NBLK * (e - 1))
                nc.gpsimd.tensor_copy(wbuf[:, e % 2, 0, :], stage).then_inc(c_hi, 1)
                pool.wait_ge(c_hi, e + 1)
                nc.gpsimd.tensor_tensor(wbuf[:, e % 2, 1, :], stage, wbuf[:, e % 2, 0, :], ALU.subtract).then_inc(c_w, 1)
                if e == 1:
                    pool.wait_ge(d_x2, NT)
                    nc.gpsimd.tensor_tensor(h[:, :, :], h[:, :, :], rows[:, BF:BF + 1, :].to_broadcast([P, NT, D]),
                                            ALU.add).then_inc(c_hf, 1)

        @block.scalar
        def _(act):
            for g in range(3):
                act.wait_ge(p_wt, g + 1)
                nc.scalar.copy(wT[:, 2 * g:2 * g + 2, :].rearrange("p a b -> p (a b)"), bank(g)).then_inc(a_wt, 1)
            act.wait_ge(p_b, 1)
            nc.scalar.copy(cols[:, :], bank(3)[:, 256:256 + NB13 + 4 + 4 * C]).then_inc(a_b, 1)
            act.wait_ge(d_ve, 1)
            nc.scalar.activation(sd[:, 0:NI], ve[:, 0:NI], ACT.Sqrt).then_inc(a_sd, 1)
            for i in range(NI):
                act.wait_ge(p_tT, i + 1)
                if i >= 2:
                    act.wait_ge(p_emb, i - 1)
                nc.scalar.copy(tT[:, i % 2, :], ps[:, 2048 + 1024 * (i % 2):2048 + 1024 * (i % 2) + FC * P]).then_inc(a_tT, 1)
            act.wait_ge(d_ve, 2)
            nc.scalar.activation(sd[:, 0:NI], ve[:, 0:NI], ACT.Sqrt).then_inc(a_sd, 1)
            act.wait_ge(d_ve, 3)
            nc.scalar.activation(sd[:, :], ve[:, :], ACT.Sqrt).then_inc(a_sd, 1)
            for i in range(NT):
                act.wait_ge(p_xT, i + 1)
                r = tile_rows(i)
                nc.scalar.copy(xnT[:, :, P * i:P * i + r], bank(4 + i % 2, D).rearrange("p (k t) -> p k t", k=KD)[:, :, 0:r]
                               ).then_inc(a_xT, 1)
            act.wait_ge(s_par, 16 * NPAR)
            for u in range(4 * len(QG)):
                w, g = u // len(QG), QG[u % len(QG)]
                act.wait_ge(p_qk, u + 1)
                nc.scalar.activation(flat_cols(qk[:, w, 0, :], g), qk_bank(u), ACT.Identity,
                                     bias=bqk[:, w:w + 1]).then_inc(a_hi, 1)
            for b in range(B):
                for hf in range(2):
                    act.wait_ge(p_St, 3 * b + hf + 1)
                    if b:
                        act.wait_ge(p_pv, b)
                    nc.scalar.activation(pm[:, 8 * hf:8 * hf + 8, :].rearrange("p h q -> p (h q)"), ps[:, 1024:2048],
                                         ACT.Exp, scale=SCALE).then_inc(a_ex, 1)
                act.wait_ge(p_St, 3 * b + 3)
                nc.scalar.activation(pl[:, :, :].rearrange("p h q -> p (h q)"), bank(4, H * TL), ACT.Exp, scale=SCALE)
                nc.scalar.activation(pr[:, :, :].rearrange("p h q -> p (h q)"), ps[0:TL, 2048 + H * TL:2048 + 2 * H * TL],
                                     ACT.Exp, scale=SCALE).then_inc(a_ex, 1)
                act.wait_ge(p_aT, b + 1)
                o = bank(7, KD * T).rearrange("p (k t) -> p k t", k=KD)
                nc.scalar.copy(tile_order(aT, b, 0), o[:, :, 0:IMG].rearrange("p k (hh w) -> p k hh w", w=G))
                nc.scalar.copy(tile_order(aT, b, 1), o[:, :, IMG:T - LAST].rearrange("p k (j t) -> p k j t", t=8))
                nc.scalar.copy(tile_order(aT, b, 2), o[:, :, T - LAST:T]).then_inc(a_aT, 1)
            act.wait_ge(d_ve, 4)
            nc.scalar.activation(sd[:, :], ve[:, :], ACT.Sqrt).then_inc(a_sd, 1)
            for i in range(NT):
                act.wait_ge(p_x2, i + 1)
                if i >= 2:
                    act.wait_ge(p_lg, i - 1)
                    act.wait_ge(d_xl, i - 1)
                nc.scalar.copy(x2f[:, i % 2, :, :].rearrange("p k n -> p (k n)"), bank(2 + i % 2, D)).then_inc(a_x2, 1)
                nc.scalar.copy(xh[:, :, P * i:P * (i + 1)], bank(2 + i % 2, D).rearrange("p (k n) -> p k n", k=KD)).then_inc(a_xh, 1)
            act.wait_ge(d_lg, 1)
            nc.scalar.activation(lg[:, :, :], lg[:, :, :], ACT.Exp).then_inc(a_ge, 1)
            step = 0
            for e in range(E):
                for n, (c0, cn) in enumerate(NE_BLK):
                    for m in range(MH):
                        act.wait_ge(p_h, step + 1)
                        if step >= 2:
                            act.wait_ge(d_u, step - 1)
                        nc.scalar.activation(t3[:, step % 2, 0:cn], bank(2 + step % 2, cn), ACT.Identity,
                                             bias=b13[:, E * MH + e * MH + m:E * MH + e * MH + m + 1]).then_inc(a_t3, 1)
                        act.wait_ge(d_u, step + 1)
                        if step >= 2:
                            act.wait_ge(d_sl, step - 1)
                        if step >= 8:
                            act.wait_ge(p_o, (step - 4) // 4)
                        nc.scalar.activation(ss[:, step % 2, 0:cn], uu[:, step % 2, 0:cn], ACT.Silu).then_inc(a_s, 1)
                        act.wait_ge(a_s, step + 1)
                        nc.scalar.copy(sh[:, (step // 4) % 2, m, 0:cn], ss[:, step % 2, 0:cn]).then_inc(c_sh, 1)
                        step += 1
            for i in range(NT):
                act.wait_ge(p_fT, i + 1)
                if i >= 2:
                    act.wait_ge(p_f, i - 1)
                nc.scalar.copy(fT[:, i % 2, :, :].rearrange("p k n -> p (k n)"), bank(i % 2, D)).then_inc(a_fT, 1)

        @block.vector
        def _(dve):
            V = nc.vector
            steps = [0]

            def link(ins):
                steps[0] += 1
                ins.then_inc(d_, 1)
                dve.wait_ge(d_, steps[0])

            V.memset(h[:, NT - 1, :], 0.0).then_inc(d_h0, 1)
            dve.wait_ge(s_img, 16 * C)
            for i in range(NI):
                for c in range(C):
                    last = V.bn_stats(st[:, i, c, :], img[:, c, :, PS * i:PS * (i + 1)])
            link(last)
            for i in range(NI):
                last = V.bn_aggr(mv[:, i, :], st[:, i, :, :].rearrange("p a b -> p (a b)"))
            link(last)
            V.tensor_scalar(ve[:, 0:NI], mv[:, 0:NI, 1], EPS, None, ALU.add).then_inc(d_ve, 1)
            dve.wait_ge(s_par, 16 * NPAR)
            dve.wait_ge(a_wt, 3)
            dve.wait_ge(a_b, 1)
            for f in range(FC):
                V.tensor_scalar(wTb[:, f, :], wT[:, f, :], ln1(f, 1), None, ALU.mult).then_inc(d_wg, 1)
                V.tensor_scalar(wTg[:, f, :], wT[:, f, :], ln1(f, 0), None, ALU.mult).then_inc(d_wg, 1)
            dve.wait_ge(a_sd, 1)
            link(V.reciprocal(rstd[:, 0:NI], sd[:, 0:NI]))
            dve.wait_ge(p_cr, 1)
            link(V.tensor_tensor(crow[:, :], bank(3, D), rows[:, BTOK, :], ALU.add))

            def take_embed(i):
                dve.wait_ge(p_emb, i + 1)
                link(V.tensor_tensor(h[:, i, :], bank(i % 2, D), crow[:, :], ALU.add))
                last = V.bn_stats(st[:, i, 0, :], h[:, i, :])
                last.then_inc(d_emb, 1)

            for i in range(NI):
                if i >= 2:
                    dve.wait_ge(p_tT, i - 1)
                V.tensor_scalar(tokn[:, i % 2, :].rearrange("p (c y x) -> p c y x", c=C, y=PS),
                                img[:, :, :, PS * i:PS * (i + 1)],
                                mv[:, i, 0:1], rstd[:, i:i + 1], ALU.subtract, ALU.mult).then_inc(d_tok, 1)
                if i:
                    take_embed(i - 1)
            take_embed(NI - 1)

            def norm_stats(lo, hi, wait):
                for i in range(lo, hi):
                    last = V.bn_aggr(mv[:, i, :], st[:, i, 0, :])
                link(last)
                V.tensor_scalar(ve[:, lo:hi], mv[:, lo:hi, 1], EPS, None, ALU.add).then_inc(d_ve, 1)
                dve.wait_ge(a_sd, wait)
                link(V.reciprocal(rstd[:, lo:hi], sd[:, lo:hi]))

            dve.wait_ge(d_emb, NI)
            norm_stats(0, NI, 2)
            for i in range(NI):
                last = V.tensor_scalar(h[:, i, :], h[:, i, :], mv[:, i, 0:1], rstd[:, i:i + 1], ALU.subtract, ALU.mult)
            link(last)
            link(V.tensor_tensor(h[:, 0:NI, :], h[:, 0:NI, :], rows[:, G2:G2 + 1, :].to_broadcast([P, NI, D]), ALU.mult))
            link(V.tensor_tensor(h[:, 0:NI, :], h[:, 0:NI, :], rows[:, B2:B2 + 1, :].to_broadcast([P, NI, D]), ALU.add))
            dve.wait_ge(s_txt, 16 * (NT - NI))
            for i in range(NT):
                last = V.bn_stats(st[:, i, 0, :], h[:, i, :])
            link(last)
            norm_stats(0, NT, 3)

            dve.wait_ge(c_const, 1)

            def take_v(i):
                dve.wait_ge(p_v, i + 1)
                if i >= 2:
                    dve.wait_ge(s_vout[i % 2], 16 * (i // 2))
                r = tile_rows(i)
                V.tensor_tensor(vt[0:r, i % 2, :, 0:HD], bank(6 + i % 2, D)[0:r, :].rearrange("p (h d) -> p h d", h=H),
                                rows[0:r, BV, :].rearrange("p (h d) -> p h d", h=H), ALU.add).then_inc(d_v, 1)

            for i in range(NT):
                if i >= 2:
                    dve.wait_ge(p_xT, i - 1)
                V.tensor_scalar(xn[:, i % 2, :], h[:, i, :], mv[:, i, 0:1], rstd[:, i:i + 1],
                                ALU.subtract, ALU.mult).then_inc(d_xn, 1)
                if i:
                    take_v(i - 1)
            take_v(NT - 1)
            for u in range(4 * len(QG)):
                w, g = u // len(QG), QG[u % len(QG)]
                dve.wait_ge(a_hi, u + 1)
                V.scalar_tensor_tensor(out=flat_cols(qk[:, w, 1, :], g), in0=qk_bank(u), scalar=bqk[:, w:w + 1],
                                       in1=flat_cols(qk[:, w, 0, :], g), op0=ALU.add, op1=ALU.subtract).then_inc(d_lo, 1)

            def maxima(b, part):
                dve.wait_ge(p_S, 3 * b + part + 1)
                if part < 2:
                    V.reduce_max(mx[:, 8 * part:8 * part + 8], ps[:, 0:1024].rearrange("p (h k) -> p h k", h=8), AX.X
                                 ).then_inc(d_mx, 1)
                    return
                V.reduce_max(mx[:, H:H + 3], bank(0, 3 * T).rearrange("p (h k) -> p h k", h=3), AX.X)
                V.reduce_max(mx[:, H + 3:H + 4], bank(1, T), AX.X).then_inc(d_mx, 1)
                dve.wait_ge(d_mx, 3 * b + 3)
                if b:
                    dve.wait_ge(p_mT, b)
                link(V.tensor_scalar(mcat[:, 0, :], mx[:, :], -1.0, None, ALU.mult))
                V.scalar_tensor_tensor(out=mcat[:, 1, :], in0=mx[:, :], scalar=-1.0, in1=mcat[:, 0, :],
                                       op0=ALU.mult, op1=ALU.subtract).then_inc(d_mc, 1)
                dve.wait_ge(p_mT, b + 1)
                if b >= 2:
                    dve.wait_ge(s_mrow[b % 2], 64 * (b // 2))
                V.tensor_copy(mT[:, b % 2, :], bank(0)[0:2 * (H + 4), 0:P // 2].bitcast(fp16)).then_inc(d_mT, 1)

            def normalise(b):
                dve.wait_ge(p_pv, b + 1)
                main = bank(5, H * (HD + 1)).rearrange("p (h d) -> p h d", h=H)
                rest = bank(6, H * (HD + 1))[0:TL, :].rearrange("p (h d) -> p h d", h=H)
                V.reciprocal(rd[:, :], main[:, :, HD])
                link(V.reciprocal(rdl[:, :], rest[:, :, HD]))
                if b:
                    dve.wait_ge(p_aT, b)
                V.tensor_tensor(at[:, :, :], main[:, :, 0:HD], rd[:, :].unsqueeze(2).to_broadcast([P, H, HD]), ALU.mult)
                V.tensor_tensor(atl[:, :, :], rest[:, :, 0:HD], rdl[:, :].unsqueeze(2).to_broadcast([TL, H, HD]),
                                ALU.mult).then_inc(d_at, 1)

            for part in range(3):
                maxima(0, part)
            for b in range(B):
                if b + 1 < B:
                    for part in range(3):
                        maxima(b + 1, part)
                normalise(b)

            dve.wait_ge(c_hb, 1)
            for i in range(NT):
                dve.wait_ge(p_pj, i + 1)
                r = tile_rows(i)
                link(V.tensor_tensor(h[0:r, i, :], bank(i % 2, D)[0:r, :], h[0:r, i, :], ALU.add))
                V.bn_stats(st[:, i, 0, :], h[:, i, :]).then_inc(d_pr, 1)
            dve.wait_ge(d_pr, NT)
            norm_stats(0, NT, 4)

            def take_lo(i):
                dve.wait_ge(a_xh, i + 1)
                V.tensor_tensor(xl[:, :, P * i:P * (i + 1)], x2f[:, i % 2, :, :], xh[:, :, P * i:P * (i + 1)],
                                ALU.subtract).then_inc(d_xl, 1)

            for i in range(NT):
                if i >= 2:
                    dve.wait_ge(p_x2, i - 1)
                V.tensor_scalar(xn[:, i % 2, :], h[:, i, :], mv[:, i, 0:1], rstd[:, i:i + 1],
                                ALU.subtract, ALU.mult).then_inc(d_x2, 1)
                if i:
                    take_lo(i - 1)
            take_lo(NT - 1)
            dve.wait_ge(p_lg, NT)
            link(V.tensor_tensor(lg[:, :, :], bank(4, NT * E).rearrange("p (t e) -> p t e", e=E),
                                 bg_row[:, :].unsqueeze(1).to_broadcast([P, NT, E]), ALU.add))
            link(V.reduce_max(gs[:, :], lg[:, :, :], AX.X))
            V.tensor_tensor(lg[:, :, :], lg[:, :, :], gs[:, :].unsqueeze(2).to_broadcast([P, NT, E]), ALU.subtract).then_inc(d_lg, 1)
            dve.wait_ge(a_ge, 1)
            link(V.reduce_sum(gs[:, :], lg[:, :, :], AX.X))
            link(V.reciprocal(gs[:, :], gs[:, :]))
            link(V.tensor_tensor(lg[:, :, :], lg[:, :, :], gs[:, :].unsqueeze(2).to_broadcast([P, NT, E]), ALU.mult))
            for i in range(NT):
                this = lg[:, i, :].unsqueeze(2).to_broadcast([P, E, E])
                other = lg[:, i, :].unsqueeze(1).to_broadcast([P, E, E])
                V.tensor_tensor(cmp1[:, i, :, :], other, this, ALU.is_gt)
                last = V.tensor_tensor(cmp2[:, i, :, :], other, this, ALU.is_equal)
            link(last)
            link(V.tensor_tensor(cmp2[:, :, :, :], cmp2[:, :, :, :], tri[:, :, :].unsqueeze(1).to_broadcast([P, NT, E, E]), ALU.mult))
            link(V.tensor_tensor(cmp1[:, :, :, :], cmp1[:, :, :, :], cmp2[:, :, :, :], ALU.add))
            rank = cmp2[:, :, 0, :]
            link(V.reduce_sum(ss[:, 0, 0:NT * E].rearrange("p (t e) -> p t e", e=E), cmp1[:, :, :, :], AX.X))
            V.scalar_tensor_tensor(out=lg[:, :, :], in0=ss[:, 0, 0:NT * E].rearrange("p (t e) -> p t e", e=E), scalar=2.0,
                                   in1=lg[:, :, :], op0=ALU.is_lt, op1=ALU.mult).then_inc(d_gw, 1)
            dve.wait_ge(d_gw, 1)
            for i in range(NT):
                dve.wait_ge(p_gT, i + 1)
                if i >= 2:
                    dve.wait_ge(p_m0, i - 1)
                V.tensor_copy(gwT[:, i % 2, :], bank(4 + i % 2)[0:E, 0:P]).then_inc(d_gt, 1)
                dve.wait_ge(p_m0, i + 1)
                V.tensor_copy(mixed[:, i, :], bank(6 + i % 2, D)).then_inc(d_mix0, 1)
            dve.wait_ge(d_mix0, NT)

            def take_out(blk):
                e, n = blk // NBLK, blk % NBLK
                dve.wait_ge(p_o, blk + 1)
                for t in range(NE_BLK[n][1] // P):
                    i = 4 * n + t
                    last = V.scalar_tensor_tensor(out=mixed[:, i, :], in0=bank(4 + t, D), scalar=lg[:, i, e:e + 1],
                                                  in1=mixed[:, i, :], op0=ALU.mult, op1=ALU.add)
                last.then_inc(d_acc, 1)

            step = 0
            for e in range(E):
                for n, (c0, cn) in enumerate(NE_BLK):
                    for m in range(MH):
                        dve.wait_ge(a_t3, step + 1)
                        if step >= 2:
                            dve.wait_ge(a_s, step - 1)
                        V.scalar_tensor_tensor(out=uu[:, step % 2, 0:cn], in0=bank(step % 2, cn),
                                               scalar=b13[:, e * MH + m:e * MH + m + 1], in1=t3[:, step % 2, 0:cn],
                                               op0=ALU.add, op1=ALU.mult).then_inc(d_u, 1)
                        if m == 2 and step >= 4:
                            take_out(step // 4 - 1)
                            if step // 4 - 1 >= 0:
                                dve.wait_ge(d_acc, step // 4)
                        dve.wait_ge(c_sh, step + 1)
                        V.tensor_tensor(sl[:, (step // 4) % 2, m, 0:cn], ss[:, step % 2, 0:cn],
                                        sh[:, (step // 4) % 2, m, 0:cn], ALU.subtract).then_inc(d_sl, 1)
                        step += 1
            take_out(E * NBLK - 1)
            dve.wait_ge(c_hf, 1)
            for i in range(NT):
                dve.wait_ge(p_f, i + 1)
                if i >= 2:
                    dve.wait_ge(s_out[i % 2], 16 * (i // 2))
                V.tensor_tensor(ot[:, i % 2, :], bank(2 + i % 2, D), h[:, i, :], ALU.add).then_inc(d_o, 1)

        @block.tensor
        def _(pe):
            mm = nc.tensor.matmul
            tr = nc.tensor.transpose
            pe.wait_ge(c_const, 1)
            pe.wait_ge(s_ws, 16)
            for g in range(3):
                for f in (2 * g, 2 * g + 1):
                    off = (f // C) * (C * P) + f % C
                    for m in range(KD):
                        last = tr(bank(g)[:, D * (f % 2) + P * m:D * (f % 2) + P * (m + 1)],
                                  wtok[:, m, off:off + C * (P - 1) + 1:C], ident[:, :])
                last.then_inc(p_wt, 1)
            pe.wait_ge(s_par, 16 * NPAR)
            tr(bank(3)[:, 256:256 + NB13 + 4], b13raw[:, :], ident[0:NB13 + 4, 0:NB13 + 4])
            for c in range(C):
                o = 256 + NB13 + 4 + 4 * c
                last = tr(bank(3)[:, o:o + 4], lnraw[:, c:c + C * (P - 1) + 1:C], ident[0:4, 0:4])
            last.then_inc(p_b, 1)
            pe.wait_ge(d_wg, 2 * FC)
            for f in range(FC):
                last = mm(bank(3, D), ones[:, :], wTb[:, f, :], start=(f == 0), stop=(f == FC - 1))
            last.then_inc(p_cr, 1)

            def embed(i):
                pe.wait_ge(a_tT, i + 1)
                if i >= 2:
                    pe.wait_ge(d_emb, i - 1)
                for f in range(FC):
                    ch = f * P
                    last = mm(bank(i % 2, D), tT[:, i % 2, ch:ch + P], wTg[:, f, :], start=(f == 0), stop=(f == FC - 1))
                last.then_inc(p_emb, 1)

            for i in range(NI):
                pe.wait_ge(d_tok, i + 1)
                if i >= 2:
                    pe.wait_ge(a_tT, i - 1)
                for f in range(FC):
                    src = (f % C) * (PS * PS) + (f // C) * P
                    o = 2048 + 1024 * (i % 2) + P * f
                    last = tr(ps[:, o:o + P], tokn[:, i % 2, src:src + P], ident[:, :])
                last.then_inc(p_tT, 1)
                if i:
                    embed(i - 1)
            embed(NI - 1)

            pe.wait_ge(s_wt2, 16 * 6)

            def values(i):
                pe.wait_ge(a_xT, i + 1)
                if i >= 2:
                    pe.wait_ge(d_v, i - 1)
                r = tile_rows(i)
                for k in range(KD):
                    last = mm(bank(6 + i % 2, D)[0:r, :], xnT[:, k, P * i:P * i + r], wqkv[:, 2, k, :],
                              start=(k == 0), stop=(k == KD - 1))
                last.then_inc(p_v, 1)

            for i in range(NT):
                pe.wait_ge(d_xn, i + 1)
                if i >= 2:
                    pe.wait_ge(a_xT, i - 1)
                else:
                    pe.wait_ge(a_tT, NI)
                for k in range(KD):
                    last = tr(bank(4 + i % 2)[:, P * k:P * (k + 1)], xn[:, i % 2, P * k:P * (k + 1)], ident[:, :])
                last.then_inc(p_xT, 1)
                if i:
                    values(i - 1)
            values(NT - 1)
            for u in range(4 * len(QG)):
                w, g = u // len(QG), QG[u % len(QG)]
                o = qk_bank(u)
                if g[0] < 2:
                    o = o.rearrange("p b (x y) -> p b x y", y=8)
                if u >= 4:
                    pe.wait_ge(d_lo, u - 3)
                for k in range(KD):
                    last = mm(o, wqkv[:, w // 2, k, P * (w % 2):P * (w % 2) + P], tile_cols(xnT[:, k, :], g),
                              start=(k == 0), stop=(k == KD - 1))
                last.then_inc(p_qk, 1)

            def scores(b, part):
                z = b % 2
                if part == 0:
                    pe.wait_ge(s_stack[z], 16 * 8 * (b // 2 + 1))
                if part:
                    pe.wait_ge(d_mx, 3 * b + part)
                elif b:
                    pe.wait_ge(d_mT, b)
                else:
                    pe.wait_ge(d_lo, 4 * len(QG))
                if part < 2:
                    for q in range(2):
                        mm(bank(q), identb[:, :], mask_q[:, :].unsqueeze(1).to_broadcast([P, 4, P]), start=True, stop=False)
                        for j in range(4):
                            hd = 8 * part + 4 * q + j
                            last = mm(bank(q)[:, P * j:P * (j + 1)], Qs[0:SROWS, z, hd, 0:P], Ks[0:SROWS, z, hd, 0:P],
                                      start=False, stop=(j == 3))
                    last.then_inc(p_S, 1)
                    return
                for g, (s0, sn) in enumerate(((0, 3), (3, 1))):
                    for j in range(4):
                        o = ps[32 * j:32 * j + 32, 512 * g:512 * g + sn * T]
                        mm(o, identb[0:32, 0:32], mask_l[:, :].unsqueeze(1).to_broadcast([32, sn, T]), start=True, stop=False,
                           tile_position=(0, 32 * j))
                        for s in range(sn):
                            hd = 4 * (s0 + s) + j
                            last = mm(o[:, T * s:T * (s + 1)], Qs[0:SROWS, z, hd, P:P + 32], Ks[0:SROWS, z, hd, 0:T],
                                      start=False, stop=(s == sn - 1), tile_position=(0, 32 * j))
                last.then_inc(p_S, 1)

            def shifted(b, part):
                z = b % 2
                R = SROWS + 2
                if part == 0:
                    pe.wait_ge(s_mrow[z], 64 * (b // 2 + 1))
                if 3 * b + part:
                    pe.wait_ge(a_ex, 3 * b + part)
                if part < 2:
                    for q in range(2):
                        mm(bank(2 + q), identb[:, :], mask_k[:, :].unsqueeze(1).to_broadcast([P, 4, P]), start=True, stop=False)
                        for j in range(4):
                            hd = 8 * part + 4 * q + j
                            last = mm(bank(2 + q)[:, P * j:P * (j + 1)], Ks[0:R, z, hd, 0:P], Qs[0:R, z, hd, 0:P],
                                      start=False, stop=(j == 3))
                    last.then_inc(p_St, 1)
                    return
                for hd in range(H):
                    mm(bank(4)[:, TL * hd:TL * (hd + 1)], Ks[0:R, z, hd, 0:P], Qs[0:R, z, hd, P:T], start=(hd == 0),
                       stop=(hd == H - 1))
                o = ps[0:TL, 2048 + H * TL:2048 + 2 * H * TL]
                mm(o, identb[0:TL, 0:TL], mask_k[0:TL, 0:TL].unsqueeze(1).to_broadcast([TL, H, TL]), start=True, stop=False)
                for hd in range(H):
                    last = mm(o[:, TL * hd:TL * (hd + 1)], Ks[0:R, z, hd, P:T], Qs[0:R, z, hd, P:T], start=False,
                              stop=(hd == H - 1))
                last.then_inc(p_St, 1)

            def maxrows(b):
                pe.wait_ge(d_mc, b + 1)
                if b:
                    pe.wait_ge(d_mT, b)
                tr(bank(0)[0:2 * (H + 4), 0:P // 2].bitcast(fp16), mcat[:, :, :].rearrange("p a b -> p (a b)"),
                   identh[:, :]).then_inc(p_mT, 1)

            def weigh(b):
                z = b % 2
                pe.wait_ge(a_ex, 3 * b + 3)
                if b:
                    pe.wait_ge(d_at, b)
                main = bank(5, H * (HD + 1)).rearrange("p (h d) -> p h d", h=H)
                rest = bank(6, H * (HD + 1))[0:TL, :].rearrange("p (h d) -> p h d", h=H)
                for hd in range(H):
                    mm(main[:, hd, :], pm[:, hd, :], Vm[:, z, hd, :], start=(hd == 0), stop=(hd == H - 1))
                for hd in range(H):
                    mm(rest[:, hd, :], pl[:, hd, :], Vm[:, z, hd, :], start=(hd == 0), stop=False)
                    last = mm(rest[:, hd, :], pr[:, hd, :], Vl[:, z, hd, :], start=False, stop=(hd == H - 1))
                last.then_inc(p_pv, 1)

            def attended(b):
                pe.wait_ge(d_at, b + 1)
                if b:
                    pe.wait_ge(a_aT, b)
                o = bank(7, KD * T).rearrange("p (k t) -> p k t", k=KD)
                for k in range(KD):
                    tr(o[:, k, 0:P], at[:, :, :].rearrange("p h d -> p (h d)")[:, P * k:P * (k + 1)], ident[:, :])
                    last = tr(o[:, k, P:T], atl[:, :, :].rearrange("p h d -> p (h d)")[:, P * k:P * (k + 1)], ident[0:TL, 0:TL])
                last.then_inc(p_aT, 1)

            for part in range(3):
                scores(0, part)
            maxrows(0)
            for b in range(B):
                if b + 1 < B:
                    scores(b + 1, 0)
                if b:
                    attended(b - 1)
                shifted(b, 0)
                if b + 1 < B:
                    scores(b + 1, 1)
                shifted(b, 1)
                if b + 1 < B:
                    scores(b + 1, 2)
                shifted(b, 2)
                if b + 1 < B:
                    maxrows(b + 1)
                weigh(b)
            attended(B - 1)

            pe.wait_ge(a_aT, B)
            for i in range(NT):
                if i >= 2:
                    pe.wait_ge(d_pr, i - 1)
                r = tile_rows(i)
                for k in range(KD):
                    last = mm(bank(i % 2, D)[0:r, :], aT[:, k, P * i:P * i + r], wqkv[:, 3, k, :], start=(k == 0),
                              stop=(k == KD - 1))
                last.then_inc(p_pj, 1)

            def logits(i):
                pe.wait_ge(a_x2, i + 1)
                for k in range(KD):
                    last = mm(bank(4)[:, E * i:E * (i + 1)], x2f[:, i % 2, k, :], wg[:, k, :], start=(k == 0), stop=(k == KD - 1))
                last.then_inc(p_lg, 1)

            for i in range(NT):
                pe.wait_ge(d_x2, i + 1)
                if i >= 2:
                    pe.wait_ge(a_xh, i - 1)
                for k in range(KD):
                    last = tr(bank(2 + i % 2)[:, P * k:P * (k + 1)], xn[:, i % 2, P * k:P * (k + 1)], ident[:, :])
                last.then_inc(p_x2, 1)
                if i:
                    logits(i - 1)
            logits(NT - 1)
            pe.wait_ge(d_gw, 1)
            for i in range(NT):
                if i >= 2:
                    pe.wait_ge(d_gt, i - 1)
                tr(bank(4 + i % 2)[0:E, 0:P], lg[:, i, :], ident[:, :]).then_inc(p_gT, 1)
                pe.wait_ge(d_gt, i + 1)
                if i >= 2:
                    pe.wait_ge(d_mix0, i - 1)
                mm(bank(6 + i % 2, D), gwT[:, i % 2, :], b2e[:, :], start=True, stop=True).then_inc(p_m0, 1)
            pe.wait_ge(d_mix0, NT)
            pe.wait_ge(d_xl, NT)

            def expert_out(blk):
                e, n = blk // NBLK, blk % NBLK
                pe.wait_ge(d_sl, 4 * (blk + 1))
                if blk:
                    pe.wait_ge(d_acc, blk)
                w2 = wbuf[:, e % 2, :, 2 * KD * HID:WE].rearrange("p s (m d) -> p s m d", m=MH)
                z = blk % 2
                for t in range(NE_BLK[n][1] // P):
                    k = 0
                    for m in range(MH):
                        for a, s in ((sh, 0), (sh, 1), (sl, 0)):
                            last = mm(bank(4 + t, D), a[:, z, m, P * t:P * (t + 1)], w2[:, s, m, :], start=(k == 0), stop=(k == 11))
                            k += 1
                last.then_inc(p_o, 1)

            step = 0
            for e in range(E):
                pe.wait_ge(c_w, e + 1)
                w1 = wbuf[:, e % 2, :, 0:KD * HID].rearrange("p s (k n) -> p s k n", k=KD)
                w3 = wbuf[:, e % 2, :, KD * HID:2 * KD * HID].rearrange("p s (k n) -> p s k n", k=KD)
                for n, (c0, cn) in enumerate(NE_BLK):
                    for m in range(MH):
                        if step >= 2:
                            pe.wait_ge(d_u, step - 1)
                        for w, o in ((w3, bank(2 + step % 2, cn)), (w1, bank(step % 2, cn))):
                            q = 0
                            for k in range(KD):
                                for s, x in ((0, xh), (0, xl), (1, xh)):
                                    last = mm(o, w[:, s, k, P * m:P * (m + 1)], x[:, k, c0:c0 + cn], start=(q == 0), stop=(q == 5))
                                    q += 1
                        last.then_inc(p_h, 1)
                        if m == 1 and step >= 4:
                            expert_out(step // 4 - 1)
                        step += 1
            expert_out(E * NBLK - 1)
            pe.wait_ge(d_acc, E * NBLK)

            def final(i):
                pe.wait_ge(a_fT, i + 1)
                if i >= 2:
                    pe.wait_ge(d_o, i - 1)
                for k in range(KD):
                    last = mm(bank(2 + i % 2, D), fT[:, i % 2, k, :], wf[:, k, :], start=(k == 0), stop=(k == KD - 1))
                last.then_inc(p_f, 1)

            for i in range(NT):
                if i >= 2:
                    pe.wait_ge(a_fT, i - 1)
                for k in range(KD):
                    last = tr(bank(i % 2)[:, P * k:P * (k + 1)], mixed[:, i, P * k:P * (k + 1)], ident[:, :])
                last.then_inc(p_fT, 1)
                if i:
                    final(i - 1)
            final(NT - 1)


_INS = ['x', 'txt', 'L0_tok_ln1_g', 'L0_tok_ln1_b', 'L0_tok_W', 'L0_tok_b', 'L0_tok_ln2_g', 'L0_tok_ln2_b',
        'L0_attn_wq', 'L0_attn_bq', 'L0_attn_wk', 'L0_attn_bk', 'L0_attn_wv', 'L0_attn_bv', 'L0_attn_wp', 'L0_attn_bp',
        'L0_ffn_W1', 'L0_ffn_b1', 'L0_ffn_W3', 'L0_ffn_b3', 'L0_ffn_W2', 'L0_ffn_b2', 'L0_ffn_Wg', 'L0_ffn_bg',
        'L0_ffn_Wf', 'L0_ffn_bf']


def kernel(**inputs):
    import numpy as _np
    import concourse.bacc as _bacc
    from concourse import mybir as _mybir
    from concourse.bass_utils import run_bass_kernel_spmd as _run

    nc = _bacc.Bacc("TRN2", target_bir_lowering=False, num_devices=1)
    arrays, args = {}, {}
    for name in _INS:
        a = _np.ascontiguousarray(inputs[name])
        arrays[f"in_{name}"] = a
        args[name] = nc.dram_tensor(f"in_{name}", a.shape, _mybir.dt.from_np(a.dtype), kind="ExternalInput").ap()
    out = nc.dram_tensor("out_0", (16, 141, 256), _mybir.dt.float32, kind="ExternalOutput").ap()
    early_fusion_block(nc, args, out)
    r = _run(nc, [arrays], core_ids=[0])
    return r.results[0]["out_0"]
```

```python
import concourse.bass as bass
from concourse import mybir
from contextlib import ExitStack
import math


def early_fusion_block(nc, A, out):
    fp32 = mybir.dt.float32
    bf16 = mybir.dt.bfloat16
    fp16 = mybir.dt.float16
    ALU = mybir.AluOpType
    ACT = mybir.ActivationFunctionType
    AX = mybir.AxisListType

    P = 128
    B = 16
    C, PS = 3, 16
    G = 8
    IMG = G * G
    TXT = 77
    T = IMG + TXT
    TL = T - P
    N = B * T
    D = 256
    KD = D // P
    H, HD = 16, 16
    E, HID = 8, 512
    MH = HID // P
    NI = G
    NT = NI + (TXT + 7) // 8
    LAST = TXT - 8 * (NT - NI - 1)
    NP = NT * P
    EPS = 1e-5
    BIG = -1e30
    SCALE = HD ** -0.5
    FC = C * PS * PS // P
    QG = [(0, 0, 8), (0, 8, 8), (1, 0, 6), (1, 6, 5), (1, 11, 5), (2, 0, 16)]
    PART = [(0, IMG), (IMG, T - LAST), (T - LAST, T)]
    SROWS = 3 * HD
    TS = 160
    NS = 4
    WM = KD * HID
    WE = 2 * KD * HID + MH * D
    RP = NT * P + P
    NST = (2 * N + E * (P - 1)) // P
    GG = [(0, 6), (6, 6), (12, 6)]
    QR = H // KD * TL

    def tile_rows(i):
        return P if i < NT - 1 else B * LAST

    def flat_cols(v, g):
        part, b0, n = g
        return v.rearrange("p (b t) -> p b t", t=T)[:, b0:b0 + n, PART[part][0]:PART[part][1]]

    def tile_cols(v, g):
        part, b0, n = g
        if part == 0:
            return v[:, 0:NI * P].rearrange("p (w b hh) -> p b hh w", w=NI, b=B)[:, b0:b0 + n]
        if part == 1:
            return v[:, NI * P:(NT - 1) * P].rearrange("p (j b t) -> p b j t", b=B, t=8)[:, b0:b0 + n]
        o = (NT - 1) * P
        return v[:, o + LAST * b0:o + LAST * (b0 + n)].rearrange("p (b t) -> p b t", t=LAST)

    def tile_order(v, b, part):
        if part == 0:
            return v[:, :, 0:NI * P].rearrange("p k (w c) -> p k w c", c=P)[:, :, :, 8 * b:8 * b + 8].rearrange(
                "p k w hh -> p k hh w")
        if part == 1:
            return v[:, :, NI * P:(NT - 1) * P].rearrange("p k (j c) -> p k j c", c=P)[:, :, :, 8 * b:8 * b + 8]
        o = (NT - 1) * P + LAST * b
        return v[:, :, o:o + LAST]

    def dram_tile(v, i):
        if i < NI:
            return v[:, i:IMG:G, :]
        a = IMG + 8 * (i - NI)
        return v[:, a:min(a + 8, T), :]

    qk_dram = nc.dram_tensor("qk_scratch", (2, 2, D, N), fp16, kind="Internal").ap()
    xs_dram = nc.dram_tensor("xs_scratch", (E * RP, D), fp32, kind="Internal").ap()
    y_dram = nc.dram_tensor("y_scratch", (NST * P, D), fp32, kind="Internal").ap()
    v_dram = nc.dram_tensor("v_scratch", (B, T, 2 * H * (HD + 1)), fp16, kind="Internal").ap()

    ctx = ExitStack()
    with ctx:
        def sb(name, shape, dt=fp32):
            return ctx.enter_context(nc.sbuf_tensor(name, shape, dt))

        def sem(name):
            return ctx.enter_context(nc.semaphore(name))

        ident = sb("ident", [P, P])
        identb = sb("identb", [P, P], bf16)
        identh = sb("identh", [P, P], fp16)
        mask_q = sb("mask_q", [P, P], bf16)
        mask_k = sb("mask_k", [P, P], bf16)
        mask_l = sb("mask_l", [32, T], bf16)
        tri = sb("tri", [P, E, E])
        ones = sb("ones", [P, P])
        onesb = sb("onesb", [P, P], bf16)
        before = sb("before", [P, P], bf16)
        jmask = sb("jmask", [P, 4])
        qsel = sb("qsel", [P, TL], fp16)
        bmask = sb("bmask", [P, H // KD])
        qtmp = sb("qtmp", [P, H // KD, TL])
        qsel2 = sb("qsel2", [P, TL])
        sel = sb("sel", [P, E, P], fp16)
        brow = sb("brow", [P, 2 * HID + D], fp16)
        iota_i = sb("iota_i", [P, 64 + NT + E], mybir.dt.int32)
        iota_f = sb("iota_f", [P, 64 + NT + E])
        jv = iota_f[:, 0:NST]
        tv = iota_f[:, 64:64 + NT]
        eoff = iota_f[:, 64 + NT:64 + NT + E]
        eoff0 = sb("eoff0", [P, E])

        h = sb("h", [P, NT, D])
        weights = sb("weights", [P, 2 * E * WE // 2])
        wres = weights[:, :].bitcast(fp16).rearrange("p (s e n) -> p s e n", s=2, e=E)
        shared_a = weights[:, 0:6144]
        shared_d = weights[:, 6144:12288]
        shared_b = weights[:, 12288:12288 + 9024]
        shared_c = sb("shared_c", [P, KD * NP])
        img = shared_a.rearrange("p (c y x) -> p c y x", c=C, y=PS)
        qk = shared_b.bitcast(fp16).rearrange("p (w s n) -> p w s n", w=4, s=2)
        xnT = shared_c[:, :].rearrange("p (k n) -> p k n", k=KD)
        stage = sb("stage", [P, 2, WM])
        spare = weights[:, 21312:24576]
        SQ, SK = H * TS, H * (T + 3)
        arena = sb("arena", [P, SQ + SK + H * P])

        wtok, wT, wTg, wTb = (shared_d[:, 1536 * k:1536 * (k + 1)] for k in range(4))
        wtok = wtok.rearrange("p (k f) -> p k f", k=KD)
        wT, wTg, wTb = (w.rearrange("p (f d) -> p f d", f=FC) for w in (wT, wTg, wTb))
        tokn = arena[:, 0:2 * FC * P].rearrange("p (b n) -> p b n", b=2)
        tT = arena[:, 2 * FC * P:4 * FC * P].rearrange("p (b n) -> p b n", b=2)
        crow = shared_c[:, 0:D]
        lnraw = shared_c[0:4, D:D + C * P]
        NB = 6
        bqkv_raw = shared_c[0:NB, 1024:1024 + P]
        cols = sb("cols", [P, NB + 4 * C])
        bqk = cols[:, 0:4]
        bv = cols[:, 4:6]

        def ln1(f, w):
            k = NB + 4 * (f % C) + 2 * w + f // C
            return cols[:, k:k + 1]

        rows = spare[:, 0:4 * D].rearrange("p (r d) -> p r d", d=D)
        BTOK, G2, B2 = range(3)
        rows_h = sb("rows_h", [P, 2, D])
        BP, BF = range(2)
        bg_row = sb("bg_row", [P, E])
        wqkv = spare[:, 4 * D:10 * D].rearrange("p (w k d) -> p w k d", w=3, k=KD)
        wp = sb("wp", [P, KD, D])
        wf = sb("wf", [P, KD, D])
        wg = sb("wg", [P, KD, E])
        st = sb("st", [P, NT, 3, 6])
        mv = sb("mv", [P, NT, 2])
        ve = sb("ve", [P, NT])
        sd = sb("sd", [P, NT])
        rstd = sb("rstd", [P, NT])
        xn = sb("xn", [P, 2, D])
        vt = spare[:, 10 * D:10 * D + 2 * H * (HD + 1)].bitcast(fp16).rearrange("p (b s h d) -> p b s h d", b=2, s=2, h=H)

        Qs = arena[:, 0:SQ].bitcast(fp16).rearrange("p (z h t) -> p z h t", z=2, h=H)
        Ks = arena[:, SQ:SQ + SK].bitcast(fp16).rearrange("p (z h t) -> p z h t", z=2, h=H)

        def stack(t, b, n, heads, cols, first=0):
            p0 = 64 * (b % 2)
            return t[p0 + first:p0 + n, b % NS // 2, heads, cols]

        pw = arena[:, SQ + SK:SQ + SK + H * P].bitcast(fp16).rearrange("p (s h q) -> p s h q", s=2, h=H)
        HQ = H // 4
        pm = [t.rearrange("p k d -> p (k d)") for t in (xn[:, :, :], wf[:, :, :])]
        braw = arena[:, SQ + SK:SQ + SK + 2 * HID + D]
        Vm = sb("Vm", [P, NS, 2, H, HD + 1], fp16)
        Vl = sb("Vl", [TL, NS, 2, H, HD + 1], fp16)
        mx = sb("mx", [P, 2, H])
        mxl = sb("mxl", [P, 4])
        mall = sb("mall", [P, 2, 2, H], fp16)
        mT = sb("mT", [2 * H, 2, T], fp16)
        pl_words = sb("pl", [P, 2 * H * TL])
        plw = sb("plw", [P, 2, 2, H, TL], fp16)
        shift = sb("shift", [P, 1])
        rd = sb("rd", [P, H])
        rdl = sb("rdl", [P, KD])
        attended = sb("attended", [P, 2 * D])
        at = attended[:, 0:D].rearrange("p (h d) -> p h d", h=H)
        atl = attended[:, D:2 * D].rearrange("p (k n) -> p k n", k=KD)
        aT = xnT

        xn2 = arena[:, 0:NT * D].rearrange("p (t d) -> p t d", t=NT)
        at_word = [0]

        def part_of(n, dt=fp32):
            a = at_word[0]
            at_word[0] += n
            return shared_c[:, a:a + n] if dt == fp32 else shared_c[:, a:a + n].bitcast(dt)

        xg = part_of(2 * D).rearrange("p (z d) -> p z d", z=2)
        xh = part_of(D, fp16).rearrange("p (z n) -> p z n", z=2)
        xl = part_of(D, fp16).rearrange("p (z n) -> p z n", z=2)
        t3 = part_of(HID)
        uu = part_of(HID)
        ss = part_of(2 * HID).rearrange("p (z n) -> p z n", z=2)
        sh = part_of(HID, fp16).rearrange("p (z n) -> p z n", z=2)
        sl = part_of(HID, fp16).rearrange("p (z n) -> p z n", z=2)
        yt = part_of(2 * D).rearrange("p (z d) -> p z d", z=2)
        x2f = xg.rearrange("p z (k n) -> p z k n", k=KD)
        NG = 4
        gy = shared_c[:, 0:NG * 2 * D].rearrange("p (z k d) -> p z k d", z=NG, k=2)
        fT = shared_c[:, 2048:2048 + 2 * D].rearrange("p (z k n) -> p z k n", z=2, k=KD)
        mt = shared_c[:, 2560:2560 + 2 * D].rearrange("p (z d) -> p z d", z=2)
        ot = shared_c[:, 3072:3072 + 2 * D].rearrange("p (z d) -> p z d", z=2)
        i32 = mybir.dt.int32
        lg = sb("lg", [P, NT, E])
        rk = sb("rk", [P, NT, E])
        chosen = sb("chosen", [P, NT, E], bf16)
        tally = sb("tally", [P, NT, E], bf16)
        addr = sb("addr", [P, NT, E])
        gs = sb("gs", [P, NT])
        cmp1 = sb("cmp1", [P, 6, E, E], bf16)
        cmp2 = sb("cmp2", [P, 6, E, E], bf16)
        pick = sb("pick", [P, 2, NT, E])
        slot_f = sb("slot_f", [P, 2, NT])
        slot_i = sb("slot_i", [P, 2, NT], i32)
        gate = sb("gate", [P, 2, NT])
        yslot_i = sb("yslot_i", [P, 2, NT], i32)
        pad_f = sb("pad_f", [P, E])
        pad_i = sb("pad_i", [P, E], i32)
        zero_rows = xn[:, 0, :]
        more = sb("more", [P, E, NT], bf16)
        tiles_of = sb("tiles_of", [P, E])
        before_e = sb("before_e", [P, E, E])
        tbase = sb("tbase", [P, E])
        tend = sb("tend", [P, E])
        jeff = pl_words[:, 0:4 * NST].rearrange("p (r j) -> p r j", j=NST)
        jge = attended[:, 0:NST * E].rearrange("p (j e) -> p j e", e=E)
        tab = sb("tab", [P, 2, NST], i32)

        ps = ctx.enter_context(nc.psum_tensor("ps", [P, 8 * 512], fp32))

        def bank(k, n=512):
            return ps[:, 512 * k:512 * k + n]

        s_ws = sem("wtok_in"); s_img = sem("image_in"); s_par = sem("params_in"); s_wt2 = sem("weights_in")
        s_txt = sem("text_in"); s_wf = sem("wf_in"); s_vout = [sem("v_out0"), sem("v_out1")]; s_qkout = sem("qk_out")
        s_stack = [sem(f"stack_in{z}") for z in range(NS)]; s_mrow = [sem("mrow_in0"), sem("mrow_in1")]
        s_we = [sem("expert_w_in0"), sem("expert_w_in1")]; s_out = [sem("out_done0"), sem("out_done1")]
        s_sort = sem("sorted_out"); s_xg = [sem("xg_in0"), sem("xg_in1")]; s_y = [sem("y_out0"), sem("y_out1")]
        s_gy = [sem(f"gathered{z}") for z in range(NG)]
        c_const = sem("consts_ready"); c_i0 = sem("consts_step"); c_hb = sem("h_plus_bp"); c_hf = sem("h_plus_bf")
        c_w = sem("w_split"); c_br = sem("brow_step")
        d_ = sem("vector_steps"); d_h0 = sem("h_tail_zeroed")
        d_ve = sem("var_ready"); d_wg = sem("wT_scaled"); d_crow = sem("crow_ready")
        d_tok = sem("patch_normed"); d_emb = sem("embed_taken"); d_xn = sem("xn_ready"); d_v = sem("v_ready")
        d_lo = sem("qk_lo"); d_pl = sem("exp_lo"); d_bp = sem("bp_ready"); d_mx = sem("max_taken"); d_mc = sem("max_rows_split")
        d_mT = sem("mT_ready"); d_at = sem("attn_normed"); d_pr = sem("proj_added"); d_x2 = sem("xn2_ready")
        d_lg = sem("logits_shifted"); d_ch = sem("choice_ready"); d_slot = sem("slots_ready"); d_pad = sem("pad_ready")
        d_tab = sem("table_ready"); d_ys = sem("yslots_ready")
        d_xl = sem("x_lo"); d_u = sem("u_ready"); d_sl = sem("s_lo"); d_y = sem("y_ready")
        d_mt = sem("mixed_ready"); d_o = sem("o_ready")
        a_wt = sem("wT_copied"); a_sd = sem("std_ready"); a_tT = sem("patchT_copied"); a_xT = sem("xnT_copied")
        a_hi = sem("qk_hi"); a_vh = sem("v_hi"); a_ph = sem("exp_hi"); a_ex = sem("exp_done"); a_aT = sem("attnT_copied"); a_wh = sem("w_hi")
        a_x2 = sem("x2f_copied"); a_ge = sem("gate_exp"); a_xh = sem("x_hi"); a_t3 = sem("h3_copied")
        a_s = sem("silu_done"); a_sh = sem("s_hi"); a_b = sem("biases_copied"); a_fT = sem("mixT_copied")
        p_wt = sem("wT_done"); p_cr = sem("crow_done"); p_tT = sem("patchT_done"); p_emb = sem("embed_done")
        p_xT = sem("xnT_done"); p_v = sem("v_done"); p_qk = sem("qk_done"); p_S = sem("S_done"); p_St = sem("St_done")
        p_mT = sem("mT_done"); p_pv = sem("pv_done"); p_aT = sem("attnT_done"); p_pj = sem("proj_done")
        p_x2 = sem("x2T_done"); p_lg = sem("logits_done"); p_rk = sem("rows_done"); p_cnt = sem("counts_done")
        p_X = sem("xT_done"); p_H3 = sem("h3_done"); p_H1 = sem("h1_done"); p_T = sem("sT_done"); p_O = sem("y_done")
        p_b = sem("biasT_done"); p_bv = sem("bvWp_done"); p_fT = sem("mixT_done"); p_f = sem("final_done")

        NPAR = 17
        NSC = 2 * NT + E

        def at_least(eng, s, n):
            if not (isinstance(n, int) and n <= 0):
                eng.wait_ge(s, n)

        def over_tiles(eng, body):
            for j in range(3):
                body(j, j // 2, j % 2)
            with eng.Fori(0, (NST - 5) // 2) as i:
                body(i * 2 + 3, i + 1, 1)
                body(i * 2 + 4, i + 2, 0)
            for j in range(NST - 2, NST):
                body(j, j // 2, j % 2)

        block = ctx.enter_context(nc.Block())

        def qk_bank(u):
            part, _, n = QG[u % len(QG)]
            m = PART[part][1] - PART[part][0]
            return bank(u % 4, n * m).rearrange("p (b t) -> p b t", b=n)

        @block.sync
        def _(sp):
            sp.dma_start(wtok[:, :, :], A["L0_tok_W"].rearrange("(m p) f -> p m f", p=P)).then_inc(s_ws, 16)
            for c in range(C):
                sp.dma_start(shared_a[:, 2048 * c:2048 * (c + 1)],
                             A["x"][:, c, :, :].rearrange("b (hh y) x -> b hh (y x)", y=PS)).then_inc(s_img, 16)
            sp.wait_ge(d_h0, 1)
            for j in range(NT - NI):
                i = NI + j
                sp.dma_start(h[0:tile_rows(i), i, :], A["txt"][:, 8 * j:min(8 * j + 8, TXT), :]).then_inc(s_txt, 16)
            for w, name in enumerate(("wq", "wk", "wv", "wp")):
                sp.dma_start(wqkv[:, w, :, :] if w < 3 else wp[:, :, :], A["L0_attn_" + name].rearrange("(k p) n -> p k n", p=P)).then_inc(s_wt2, 16)
            sp.dma_start(wg[:, :, :], A["L0_ffn_Wg"].rearrange("(k p) n -> p k n", p=P)).then_inc(s_wt2, 16)
            for i in range(NT):
                sp.wait_ge(d_v, i + 1)
                sp.dma_start(dram_tile(v_dram, i), vt[0:tile_rows(i), i % 2, :, :, :].rearrange("p s h d -> p (s h d)")
                             ).then_inc(s_vout[i % 2], 16)
            for w in range(4):
                sp.wait_ge(d_lo, len(QG) * (w + 1))
                for k in range(2):
                    sp.dma_start(qk_dram[w // 2, k, P * (w % 2):P * (w % 2) + P, :], qk[:, w, k, :]).then_inc(s_qkout, 16)
            sp.wait_ge(s_vout[0], 16 * (NT // 2))
            sp.wait_ge(s_vout[1], 16 * (NT // 2))
            sp.wait_ge(s_qkout, 16 * 8)
            sp.wait_ge(c_br, 4)

            def load_stack(b):
                z = b % NS
                if b >= NS:
                    sp.wait_ge(p_pv, b - NS + 1)
                t0 = b * T
                for w, dst, parts in ((0, Qs, (0, 1, 0)), (1, Ks, (0, 0, 1))):
                    for r, s in enumerate(parts):
                        sp.dma_start(stack(dst, b, HD * (r + 1), slice(0, H), slice(0, T), HD * r),
                                     qk_dram[w, s, :, t0:t0 + T].rearrange("(h d) t -> d h t", d=HD)
                                     ).then_inc(s_stack[z], 16)
                sp.dma_start(Vm[:, z, :, :, :].rearrange("p s h d -> p (s h d)"), v_dram[b, 0:P, :]).then_inc(s_stack[z], 16)
                sp.dma_start(Vl[:, z, :, :, :].rearrange("p s h d -> p (s h d)"), v_dram[b, P:T, :]).then_inc(s_stack[z], 16)

            def load_mrow(b):
                sp.wait_ge(d_mT, b + 1)
                sp.dma_start(stack(Qs, b, SROWS + 2, slice(0, H), slice(0, T), SROWS), mT[:, b % 2, :]).then_inc(s_mrow[b % 2], 16)

            for b in range(NS):
                load_stack(b)
            load_mrow(0)
            for b in range(B):
                if b + 1 < B:
                    load_mrow(b + 1)
                if b + NS < B:
                    load_stack(b + NS)

            sp.wait_ge(d_pl, 5 * B)
            sp.dma_start(wf[:, :, :], A["L0_ffn_Wf"].rearrange("(k p) n -> p k n", p=P)).then_inc(s_wf, 16)
            sp.wait_ge(s_sort, 16 * NSC)
            sp.wait_ge(d_tab, 1)

            def load_x(j, half, z):
                row = sp.value_load(tab[0:1, 1, bass.ds(j, 1)], min_val=0, max_val=E * RP - P)
                at_least(sp, p_X, j - 1)
                sp.dma_start(xg[:, z, :], xs_dram[bass.ds(row, P), :]).then_inc(s_xg[z], 16)

            def store_y(j, z):
                sp.wait_ge(d_y, j + 1)
                sp.dma_start(y_dram[bass.ds(j * P, P), :], yt[:, z, :]).then_inc(s_y[z], 16)

            def move(j, half, z):
                load_x(j, half, z)
                if not (isinstance(j, int) and j < 3):
                    store_y(j - 3, 1 - z)

            over_tiles(sp, move)
            for j in range(NST - 3, NST):
                store_y(j, j % 2)
            for i in range(NT):
                sp.wait_ge(d_o, i + 1)
                sp.dma_start(dram_tile(out, i), ot[0:tile_rows(i), i % 2, :]).then_inc(s_out[i % 2], 16)
            sp.wait_ge(s_out[0], 16 * (NT // 2))
            sp.wait_ge(s_out[1], 16 * (NT // 2))

        @block.gpsimd
        def _(pool):
            for k, name in ((BTOK, "L0_tok_b"), (G2, "L0_tok_ln2_g"), (B2, "L0_tok_ln2_b"),
                            (4 + BP, "L0_attn_bp"), (4 + BF, "L0_ffn_bf")):
                pool.dma_start(rows[:, k, :] if k < 4 else rows_h[:, k - 4, :], A[name].rearrange("(o n) -> o n", o=1).to_broadcast([P, D])).then_inc(s_par, 16)
            pool.dma_start(bg_row[:, :], A["L0_ffn_bg"].rearrange("(o n) -> o n", o=1).to_broadcast([P, E])).then_inc(s_par, 16)
            for w, name in enumerate(("L0_tok_ln1_g", "L0_tok_ln1_b")):
                pool.dma_start(lnraw[2 * w:2 * w + 2, :], A[name].rearrange("(hf n) -> hf n", hf=2)).then_inc(s_par, 16)
            for w, name in enumerate(("L0_attn_bq", "L0_attn_bk", "L0_attn_bv")):
                pool.dma_start(bqkv_raw[2 * w:2 * w + 2, :], A[name].rearrange("(m p) -> m p", p=P)).then_inc(s_par, 16)
            for p0 in (0, 32):
                for name, o, n in (("b1", 0, HID), ("b3", HID, HID), ("b2", 2 * HID, D)):
                    pool.dma_start(braw[p0:p0 + E, o:o + n], A["L0_ffn_" + name]).then_inc(s_par, 16)
            for t, v in ((ident, 0.0), (identb, 0.0), (identh, 0.0), (mask_q, 0.0), (mask_k, 0.0), (mask_l, 0.0), (ones, 1.0),
                         (onesb, 1.0), (before, 0.0), (jmask, 1.0), (qsel, 0.0), (bmask, 1.0), (brow, 0.0)):
                nc.gpsimd.memset(t[:, :], v)
            for t, v in ((tri, 1.0), (sel, 0.0), (qtmp, 0.0)):
                nc.gpsimd.memset(t[:, :, :], v)
            nc.gpsimd.memset(vt[:, :, 0, :, :], 1.0)
            nc.gpsimd.memset(vt[:, :, 1, :, :], 0.0)
            nc.gpsimd.memset(pl_words[:, :], 0.0)
            nc.gpsimd.memset(shift[:, :], 10.0 * math.log(2.0))
            nc.gpsimd.iota(iota_i[:, 0:64], [[1, 64]], base=0, channel_multiplier=0)
            nc.gpsimd.iota(iota_i[:, 64:64 + NT], [[P, NT]], base=0, channel_multiplier=0)
            nc.gpsimd.iota(iota_i[:, 64 + NT:64 + NT + E], [[RP, E]], base=0, channel_multiplier=1).then_inc(c_i0, 1)
            pool.wait_ge(c_i0, 1)

            def select(t, op, fill, base, pattern, cm):
                return nc.gpsimd.affine_select(out=t, in_=t, compare_op=op, fill=fill, base=base, pattern=pattern,
                                               channel_multiplier=cm)

            for m in (ident, identb, identh):
                select(m[:, :], ALU.not_equal, 1.0, 0, [[-1, P]], 1)
            select(mask_q[:, :], ALU.is_ge, BIG, 0, [[-1, P]], 1)
            select(mask_k[:, :], ALU.is_ge, BIG, 0, [[1, P]], -1)
            select(mask_l[:, :], ALU.is_ge, BIG, P, [[-1, T]], 1)
            select(before[:, :], ALU.is_ge, 1.0, 0, [[-1, P]], 1)
            select(tri[:, :, :], ALU.is_gt, 0.0, 0, [[-1, E], [1, E]], 0)
            select(sel[:, :, :], ALU.not_equal, 1.0, 0, [[-1, E], [0, P]], 1)
            select(bmask[:, :], ALU.is_ge, 0.0, 0, [[-TL, H // KD]], 1)
            select(qtmp[:, :, :], ALU.not_equal, 1.0, 0, [[-TL, H // KD], [-1, TL]], 1)
            select(jmask[:, :], ALU.is_ge, 0.0, 0, [[-32, 4]], 1)
            select(qsel[:, :], ALU.not_equal, 1.0, 0, [[-1, TL]], 1)
            nc.gpsimd.tensor_copy(iota_f[:, :], iota_i[:, :]).then_inc(c_i0, 1)
            pool.wait_ge(c_i0, 2)
            select(sel[:, :, :], ALU.not_equal, 1.0, -32, [[-1, E], [0, P]], 1)
            select(bmask[:, :], ALU.is_ge, 0.0, TL - 1, [[TL, H // KD]], -1)
            nc.gpsimd.tensor_scalar(eoff0[:, :], jv[:, 0:E], float(RP), 0.0, ALU.mult, ALU.add)
            select(jmask[:, :], ALU.is_ge, 0.0, 31, [[32, 4]], -1)
            select(qsel[:, :], ALU.not_equal, 1.0, -32, [[-1, TL]], 1).then_inc(c_i0, 1)
            pool.wait_ge(c_i0, 3)
            select(qsel[:, :], ALU.not_equal, 1.0, -64, [[-1, TL]], 1).then_inc(c_i0, 1)
            pool.wait_ge(c_i0, 4)
            select(qsel[:, :], ALU.not_equal, 1.0, -96, [[-1, TL]], 1).then_inc(c_const, 1)
            pool.wait_ge(s_par, 16 * NPAR)
            nc.gpsimd.tensor_copy(brow[0:E, :], braw[0:E, :]).then_inc(c_br, 1)
            pool.wait_ge(c_br, 1)
            nc.gpsimd.tensor_copy(brow[32:32 + E, :], braw[32:32 + E, :]).then_inc(c_br, 1)
            pool.wait_ge(c_br, 2)
            nc.gpsimd.tensor_tensor(brow[32:32 + E, :], braw[32:32 + E, :], brow[32:32 + E, :], ALU.subtract).then_inc(c_br, 1)
            pool.wait_ge(c_br, 3)
            pool.wait_ge(p_emb, NI)
            nc.gpsimd.memset(Qs, 0.0)
            nc.gpsimd.memset(Ks, 1.0).then_inc(c_br, 1)
            pool.wait_ge(d_xn, NT)
            pool.wait_ge(d_bp, 1)
            nc.gpsimd.tensor_tensor(h[:, :, :], h[:, :, :], rows_h[:, BP:BP + 1, :].to_broadcast([P, NT, D]), ALU.add).then_inc(c_hb, 1)

            def load_w(u):
                w = A["L0_ffn_W" + "132"[u % 3]][u // 3].rearrange("(k p) n -> p k n", p=P)
                pool.dma_start(stage[:, u % 2, :].rearrange("p (k n) -> p k n", k=w.shape[1]), w).then_inc(s_we[u % 2], 16)

            load_w(0)
            load_w(1)
            for u in range(3 * E):
                pool.wait_ge(a_wh, u + 1)
                o = WM * (u % 3)
                nc.gpsimd.tensor_tensor(wres[:, 1, u // 3, o:o + WM], stage[:, u % 2, :], wres[:, 0, u // 3, o:o + WM],
                                        ALU.subtract).then_inc(c_w, 1)
                if u + 2 < 3 * E:
                    pool.wait_ge(c_w, u + 1)
                    load_w(u + 2)
            pool.wait_ge(d_pl, 5 * B)
            nc.gpsimd.memset(zero_rows, 0.0).then_inc(c_w, 1)
            pool.wait_ge(c_w, 3 * E + 1)

            for g, (t0, n) in enumerate(GG):
                pool.wait_ge(d_slot, g + 1)
                for i in range(t0, t0 + n):
                    m = tile_rows(i)
                    for k in range(2):
                        pool.indirect_dma_start(out=xs_dram[:, :],
                                                out_offset=bass.IndirectOffsetOnAxis(ap=slot_i[0:m, k, i:i + 1], axis=0),
                                                in_=xn2[0:m, i, :], in_offset=None).then_inc(s_sort, 16)
            pool.wait_ge(d_pad, 1)
            for e in range(E):
                pool.indirect_dma_start(out=xs_dram[:, :], out_offset=bass.IndirectOffsetOnAxis(ap=pad_i[:, e:e + 1], axis=0),
                                        in_=zero_rows, in_offset=None).then_inc(s_sort, 16)
            pool.wait_ge(d_x2, NT)
            nc.gpsimd.tensor_tensor(h[:, :, :], h[:, :, :], rows_h[:, BF:BF + 1, :].to_broadcast([P, NT, D]), ALU.add).then_inc(c_hf, 1)
            pool.wait_ge(d_ys, 1)
            pool.wait_ge(s_y[0], 16 * ((NST + 1) // 2))
            pool.wait_ge(s_y[1], 16 * (NST // 2))
            for i in range(NT):
                m = tile_rows(i)
                if i >= NG:
                    pool.wait_ge(d_mt, i - NG + 1)
                for k in range(2):
                    pool.indirect_dma_start(out=gy[0:m, i % NG, k, :], out_offset=None, in_=y_dram[:, :],
                                            in_offset=bass.IndirectOffsetOnAxis(ap=yslot_i[0:m, k, i:i + 1], axis=0)
                                            ).then_inc(s_gy[i % NG], 16)

        @block.scalar
        def _(act):
            for g in range(3):
                act.wait_ge(p_wt, g + 1)
                nc.scalar.copy(wT[:, 2 * g:2 * g + 2, :].rearrange("p a b -> p (a b)"), bank(g)).then_inc(a_wt, 1)
            act.wait_ge(p_b, 1)
            nc.scalar.copy(cols[:, :], bank(3)[:, 256:256 + NB + 4 * C]).then_inc(a_b, 1)
            act.wait_ge(d_ve, 1)
            nc.scalar.activation(sd[:, 0:NI], ve[:, 0:NI], ACT.Sqrt).then_inc(a_sd, 1)
            for i in range(NI):
                act.wait_ge(p_tT, i + 1)
                if i >= 2:
                    act.wait_ge(p_emb, i - 1)
                nc.scalar.copy(tT[:, i % 2, :], ps[:, 2048 + 1024 * (i % 2):2048 + 1024 * (i % 2) + FC * P]).then_inc(a_tT, 1)
            act.wait_ge(d_ve, 2)
            nc.scalar.activation(sd[:, 0:NI], ve[:, 0:NI], ACT.Sqrt).then_inc(a_sd, 1)
            act.wait_ge(d_ve, 3)
            nc.scalar.activation(sd[:, :], ve[:, :], ACT.Sqrt).then_inc(a_sd, 1)

            def values_hi(i):
                act.wait_ge(p_v, i + 1)
                if i >= 2:
                    act.wait_ge(s_vout[i % 2], 16 * (i // 2))
                m = tile_rows(i)
                nc.scalar.copy(vt[0:m, i % 2, 0, :, 0:HD], bank(6 + i % 2, D)[0:m, :].rearrange("p (h d) -> p h d", h=H)).then_inc(a_vh, 1)

            act.wait_ge(c_const, 1)
            for i in range(NT):
                act.wait_ge(p_xT, i + 1)
                r = tile_rows(i)
                nc.scalar.copy(xnT[:, :, P * i:P * i + r], bank(4 + i % 2, D).rearrange("p (k t) -> p k t", k=KD)[:, :, 0:r]
                               ).then_inc(a_xT, 1)
                if i:
                    values_hi(i - 1)
            values_hi(NT - 1)
            act.wait_ge(s_par, 16 * NPAR)
            for u in range(4 * len(QG)):
                w, g = u // len(QG), QG[u % len(QG)]
                act.wait_ge(p_qk, u + 1)
                nc.scalar.activation(flat_cols(qk[:, w, 0, :], g), qk_bank(u), ACT.Identity,
                                     bias=bqk[:, w:w + 1]).then_inc(a_hi, 1)

            def keep_attended(b):
                act.wait_ge(p_aT, b + 1)
                o = bank(7, KD * T).rearrange("p (k t) -> p k t", k=KD)
                nc.scalar.copy(tile_order(aT, b, 0), o[:, :, 0:IMG].rearrange("p k (hh w) -> p k hh w", w=G))
                nc.scalar.copy(tile_order(aT, b, 1), o[:, :, IMG:T - LAST].rearrange("p k (j t) -> p k j t", t=8))
                nc.scalar.copy(tile_order(aT, b, 2), o[:, :, T - LAST:T]).then_inc(a_aT, 1)

            for b in range(B):
                for hf in range(2):
                    act.wait_ge(p_St, 3 * b + hf + 1)
                    for q in range(2):
                        if 4 * b + 2 * hf >= 2:
                            act.wait_ge(d_pl, 5 * b + 2 * hf + q - 1 if hf else 5 * b - 2 + q)
                        nc.scalar.activation(pm[q], bank(2 + q), ACT.Exp, bias=shift[:, 0:1], scale=SCALE).then_inc(a_ex, 1)
                    if b and not hf:
                        act.wait_ge(p_pv, b)
                    for q in range(2):
                        act.wait_ge(a_ex, 5 * b + 2 * hf + q + 1)
                        nc.scalar.copy(pw[:, 0, HQ * (2 * hf + q):HQ * (2 * hf + q + 1), :].rearrange("p h q -> p (h q)"), pm[q]
                                       ).then_inc(a_ph, 1)
                act.wait_ge(p_St, 3 * b + 3)
                if b:
                    act.wait_ge(d_pl, 5 * b)
                nc.scalar.activation(pl_words[:, 0:H * TL], bank(4, H * TL), ACT.Exp, bias=shift[:, 0:1], scale=SCALE)
                nc.scalar.activation(pl_words[0:TL, H * TL:2 * H * TL], ps[0:TL, 2048 + H * TL:2048 + 2 * H * TL],
                                     ACT.Exp, bias=shift[0:TL, 0:1], scale=SCALE).then_inc(a_ex, 1)
                act.wait_ge(a_ex, 5 * b + 5)
                nc.scalar.copy(plw[:, 0, :, :, :].rearrange("p k h q -> p (k h q)"), pl_words[:, :]).then_inc(a_ph, 1)
                if b:
                    keep_attended(b - 1)
                for u in range(3 * b // 2, 3 * (b + 1) // 2):
                    act.wait_ge(s_we[u % 2], 16 * (u // 2 + 1))
                    o = WM * (u % 3)
                    nc.scalar.copy(wres[:, 0, u // 3, o:o + WM], stage[:, u % 2, :]).then_inc(a_wh, 1)
            keep_attended(B - 1)
            act.wait_ge(d_ve, 4)
            nc.scalar.activation(sd[:, :], ve[:, :], ACT.Sqrt).then_inc(a_sd, 1)
            for i in range(NT):
                act.wait_ge(p_x2, i + 1)
                if i >= 2:
                    act.wait_ge(p_lg, i - 1)
                nc.scalar.copy(x2f[:, i % 2, :, :].rearrange("p k n -> p (k n)"), bank(2 + i % 2, D)).then_inc(a_x2, 1)
                if i % 6 == 1 and i > 6:
                    g = i // 6 - 1
                    act.wait_ge(d_lg, g + 1)
                    t0, n = GG[g]
                    nc.scalar.activation(lg[:, t0:t0 + n, :], lg[:, t0:t0 + n, :], ACT.Exp).then_inc(a_ge, 1)
            act.wait_ge(d_lg, len(GG))
            t0, n = GG[-1]
            nc.scalar.activation(lg[:, t0:t0 + n, :], lg[:, t0:t0 + n, :], ACT.Exp).then_inc(a_ge, 1)

            def split_x(j, z):
                act.wait_ge(p_X, j + 1)
                at_least(act, p_H1, j - 1)
                nc.scalar.copy(xh[:, z, :], bank(3, D)).then_inc(a_xh, 1)

            def split_s(j, z):
                act.wait_ge(p_T, j + 1)
                at_least(act, p_O, j - 1)
                nc.scalar.copy(sh[:, z, :], bank(2)).then_inc(a_sh, 1)

            def expert(j, half, z):
                act.wait_ge(p_H3, j + 1)
                at_least(act, d_u, j)
                nc.scalar.copy(t3, bank(0)).then_inc(a_t3, 1)
                if not (isinstance(j, int) and j < 1):
                    split_s(j - 1, 1 - z)
                act.wait_ge(d_u, j + 1)
                at_least(act, p_T, j - 1)
                nc.scalar.activation(ss[:, z, :], uu, ACT.Silu).then_inc(a_s, 1)
                if not (isinstance(j, int) and j == NST - 1):
                    split_x(j + 1, 1 - z)

            split_x(0, 0)
            over_tiles(act, expert)
            split_s(NST - 1, (NST - 1) % 2)
            for i in range(NT):
                act.wait_ge(p_fT, i + 1)
                if i >= 2:
                    act.wait_ge(p_f, i - 1)
                m = tile_rows(i)
                nc.scalar.copy(fT[:, i % 2, :, 0:m], bank(i % 2, D).rearrange("p (k n) -> p k n", k=KD)[:, :, 0:m]).then_inc(a_fT, 1)

        @block.vector
        def _(dve):
            V = nc.vector
            steps = [0]

            def link(ins):
                steps[0] += 1
                ins.then_inc(d_, 1)
                dve.wait_ge(d_, steps[0])

            V.memset(h[:, NT - 1, :], 0.0).then_inc(d_h0, 1)
            dve.wait_ge(s_img, 16 * C)
            for i in range(NI):
                for c in range(C):
                    last = V.bn_stats(st[:, i, c, :], img[:, c, :, PS * i:PS * (i + 1)])
            link(last)
            for i in range(NI):
                last = V.bn_aggr(mv[:, i, :], st[:, i, :, :].rearrange("p a b -> p (a b)"))
            link(last)
            V.tensor_scalar(ve[:, 0:NI], mv[:, 0:NI, 1], EPS, None, ALU.add).then_inc(d_ve, 1)
            dve.wait_ge(s_par, 16 * NPAR)
            dve.wait_ge(a_wt, 3)
            dve.wait_ge(a_b, 1)
            for f in range(FC):
                V.tensor_scalar(wTb[:, f, :], wT[:, f, :], ln1(f, 1), None, ALU.mult).then_inc(d_wg, 1)
                V.tensor_scalar(wTg[:, f, :], wT[:, f, :], ln1(f, 0), None, ALU.mult).then_inc(d_wg, 1)
            dve.wait_ge(a_sd, 1)
            link(V.reciprocal(rstd[:, 0:NI], sd[:, 0:NI]))
            dve.wait_ge(p_cr, 1)
            link(V.tensor_tensor(crow[:, :], bank(3, D), rows[:, BTOK, :], ALU.add))

            def take_embed(i):
                dve.wait_ge(p_emb, i + 1)
                link(V.tensor_tensor(h[:, i, :], bank(i % 2, D), crow[:, :], ALU.add))
                last = V.bn_stats(st[:, i, 0, :], h[:, i, :])
                last.then_inc(d_emb, 1)

            for i in range(NI):
                if i >= 2:
                    dve.wait_ge(p_tT, i - 1)
                V.tensor_scalar(tokn[:, i % 2, :].rearrange("p (c y x) -> p c y x", c=C, y=PS),
                                img[:, :, :, PS * i:PS * (i + 1)],
                                mv[:, i, 0:1], rstd[:, i:i + 1], ALU.subtract, ALU.mult).then_inc(d_tok, 1)
                if i:
                    take_embed(i - 1)
            take_embed(NI - 1)

            def norm_stats(lo, hi, wait):
                for i in range(lo, hi):
                    last = V.bn_aggr(mv[:, i, :], st[:, i, 0, :])
                link(last)
                V.tensor_scalar(ve[:, lo:hi], mv[:, lo:hi, 1], EPS, None, ALU.add).then_inc(d_ve, 1)
                dve.wait_ge(a_sd, wait)
                link(V.reciprocal(rstd[:, lo:hi], sd[:, lo:hi]))

            dve.wait_ge(d_emb, NI)
            norm_stats(0, NI, 2)
            for i in range(NI):
                last = V.tensor_scalar(h[:, i, :], h[:, i, :], mv[:, i, 0:1], rstd[:, i:i + 1], ALU.subtract, ALU.mult)
            link(last)
            link(V.tensor_tensor(h[:, 0:NI, :], h[:, 0:NI, :], rows[:, G2:G2 + 1, :].to_broadcast([P, NI, D]), ALU.mult))
            link(V.tensor_tensor(h[:, 0:NI, :], h[:, 0:NI, :], rows[:, B2:B2 + 1, :].to_broadcast([P, NI, D]), ALU.add))
            dve.wait_ge(s_txt, 16 * (NT - NI))
            for i in range(NT):
                last = V.bn_stats(st[:, i, 0, :], h[:, i, :])
            link(last)
            norm_stats(0, NT, 3)

            def take_v(i):
                dve.wait_ge(a_vh, i + 1)
                m = tile_rows(i)
                V.tensor_tensor(vt[0:m, i % 2, 1, :, 0:HD], bank(6 + i % 2, D)[0:m, :].rearrange("p (h d) -> p h d", h=H),
                                vt[0:m, i % 2, 0, :, 0:HD], ALU.subtract).then_inc(d_v, 1)

            for i in range(NT):
                if i >= 2:
                    dve.wait_ge(p_xT, i - 1)
                V.tensor_scalar(xn[:, i % 2, :], h[:, i, :], mv[:, i, 0:1], rstd[:, i:i + 1],
                                ALU.subtract, ALU.mult).then_inc(d_xn, 1)
                if i:
                    take_v(i - 1)
            take_v(NT - 1)
            for u in range(4 * len(QG)):
                w, g = u // len(QG), QG[u % len(QG)]
                dve.wait_ge(a_hi, u + 1)
                V.scalar_tensor_tensor(out=flat_cols(qk[:, w, 1, :], g), in0=qk_bank(u), scalar=bqk[:, w:w + 1],
                                       in1=flat_cols(qk[:, w, 0, :], g), op0=ALU.add, op1=ALU.subtract).then_inc(d_lo, 1)

            dve.wait_ge(p_bv, 1)
            V.tensor_tensor(rows_h[:, BP, :], bank(6, D), rows_h[:, BP, :], ALU.add).then_inc(d_bp, 1)

            def maxima(b, part):
                dve.wait_ge(p_S, 3 * b + part + 1)
                if b and part == 0:
                    dve.wait_ge(d_mc, b)
                if part < 2:
                    V.reduce_max(mx[:, 0, 8 * part:8 * part + 8], ps[:, 0:1024].rearrange("p (h k) -> p h k", h=8), AX.X
                                 ).then_inc(d_mx, 1)
                    return
                dve.wait_ge(d_mx, 2 * b + 2)
                V.reduce_max(mxl[:, 0:3], bank(0, 3 * T).rearrange("p (h k) -> p h k", h=3), AX.X)
                link(V.reduce_max(mxl[:, 3:4], bank(1, T), AX.X))
                link(V.tensor_tensor(mx[:, 1, :].rearrange("p (a j) -> p a j", j=4), mxl[:, :].unsqueeze(2).to_broadcast([P, 4, 4]),
                                     jmask[:, :].unsqueeze(1).to_broadcast([P, 4, 4]), ALU.mult))
                if b:
                    dve.wait_ge(p_mT, b)
                link(V.tensor_scalar(mall[:, :, 0, :], mx[:, :, :], -1.0, None, ALU.mult))
                V.scalar_tensor_tensor(out=mall[:, :, 1, :], in0=mx[:, :, :], scalar=-1.0, in1=mall[:, :, 0, :],
                                       op0=ALU.mult, op1=ALU.subtract).then_inc(d_mc, 1)
                dve.wait_ge(p_mT, b + 1)
                if b >= 2:
                    dve.wait_ge(s_mrow[b % 2], 16 * (b // 2))
                V.tensor_copy(mT[:, b % 2, :], bank(5)[0:2 * H, 512 - T:512]).then_inc(d_mT, 1)

            def normalise(b):
                dve.wait_ge(p_pv, b + 1)
                main = bank(5, H * (HD + 1)).rearrange("p (h d) -> p h d", h=H)
                rest = bank(6, H * (HD + 1))[0:QR, :].rearrange("p (k h d) -> p k h d", k=KD, d=HD + 1)
                V.reciprocal(rd[:, :], main[:, :, HD])
                link(V.reciprocal(rdl[0:QR, :], rest[:, :, 0, HD]))
                if b:
                    dve.wait_ge(p_aT, b)
                V.tensor_tensor(at[:, :, :], main[:, :, 0:HD], rd[:, :].unsqueeze(2).to_broadcast([P, H, HD]), ALU.mult)
                for k in range(KD):
                    last = V.scalar_tensor_tensor(out=atl[0:QR, k, :].rearrange("p (h d) -> p h d", d=HD), in0=rest[:, k, :, 0:HD],
                                                  scalar=rdl[0:QR, k:k + 1],
                                                  in1=bmask[0:QR, :].unsqueeze(2).to_broadcast([QR, H // KD, HD]),
                                                  op0=ALU.mult, op1=ALU.mult)
                last.then_inc(d_at, 1)

            def exp_lo(b, u):
                dve.wait_ge(a_ph, 5 * b + u + 1)
                if u < 4:
                    hs = slice(HQ * u, HQ * (u + 1))
                    V.tensor_tensor(pw[:, 1, hs, :].rearrange("p h q -> p (h q)"), pm[u % 2],
                                    pw[:, 0, hs, :].rearrange("p h q -> p (h q)"), ALU.subtract).then_inc(d_pl, 1)
                else:
                    V.tensor_tensor(plw[:, 1, :, :, :].rearrange("p k h q -> p (k h q)"), pl_words[:, :],
                                    plw[:, 0, :, :, :].rearrange("p k h q -> p (k h q)"), ALU.subtract).then_inc(d_pl, 1)

            dve.wait_ge(c_const, 1)
            link(V.reduce_sum(qsel2[:, :], qtmp[:, :, :].rearrange("p h q -> p q h"), AX.X))
            for part in range(3):
                maxima(0, part)
            for b in range(B):
                if b + 1 < B:
                    maxima(b + 1, 0)
                if b:
                    normalise(b - 1)
                if b + 1 < B:
                    maxima(b + 1, 1)
                exp_lo(b, 0)
                exp_lo(b, 1)
                if b + 1 < B:
                    maxima(b + 1, 2)
                for u in range(2, 5):
                    exp_lo(b, u)
            normalise(B - 1)

            dve.wait_ge(c_hb, 1)
            for i in range(NT):
                dve.wait_ge(p_pj, i + 1)
                r = tile_rows(i)
                link(V.tensor_tensor(h[0:r, i, :], bank(i % 2, D)[0:r, :], h[0:r, i, :], ALU.add))
                V.bn_stats(st[:, i, 0, :], h[:, i, :]).then_inc(d_pr, 1)
            dve.wait_ge(d_pr, NT)
            norm_stats(0, NT, 4)

            for i in range(NT):
                V.tensor_scalar(xn2[:, i, :], h[:, i, :], mv[:, i, 0:1], rstd[:, i:i + 1],
                                ALU.subtract, ALU.mult).then_inc(d_x2, 1)

            V.memset(tally[:, 0, :], 0.0).then_inc(d_, 1)
            steps[0] += 1
            for g, (t0, n) in enumerate(GG):
                t1 = t0 + n
                ln = lg[:, t0:t1, :]
                gn = gs[:, t0:t1]
                dve.wait_ge(p_lg, t1)
                link(V.tensor_tensor(ln, bank(4 + g % 2, n * E).rearrange("p (t e) -> p t e", e=E),
                                     bg_row[:, :].unsqueeze(1).to_broadcast([P, n, E]), ALU.add))
                link(V.reduce_max(gn, ln, AX.X))
                V.tensor_tensor(ln, ln, gn.unsqueeze(2).to_broadcast([P, n, E]), ALU.subtract).then_inc(d_lg, 1)
                dve.wait_ge(a_ge, g + 1)
                link(V.reduce_sum(gn, ln, AX.X))
                link(V.reciprocal(gn, gn))
                link(V.tensor_tensor(ln, ln, gn.unsqueeze(2).to_broadcast([P, n, E]), ALU.mult))
                this = ln.unsqueeze(3).to_broadcast([P, n, E, E])
                other = ln.unsqueeze(2).to_broadcast([P, n, E, E])
                V.tensor_tensor(cmp1[:, :, :, :], other, this, ALU.is_gt)
                link(V.tensor_tensor(cmp2[:, :, :, :], other, this, ALU.is_equal))
                link(V.tensor_tensor(cmp2[:, :, :, :], cmp2[:, :, :, :], tri[:, :, :].unsqueeze(1).to_broadcast([P, n, E, E]), ALU.mult))
                link(V.tensor_tensor(cmp1[:, :, :, :], cmp1[:, :, :, :], cmp2[:, :, :, :], ALU.add))
                link(V.reduce_sum(rk[:, t0:t1, :], cmp1[:, :, :, :], AX.X))
                link(V.tensor_scalar(chosen[:, t0:t1, :], rk[:, t0:t1, :], 2.0, None, ALU.is_lt))
                for i in range(t0 + 1, min(t1 + 1, NT)):
                    link(V.tensor_tensor(tally[:, i, :], tally[:, i - 1, :], chosen[:, i - 1, :], ALU.add))
                dve.nop().then_inc(d_ch, 1)
                dve.wait_ge(p_rk, g + 1)
                link(V.tensor_tensor(addr[:, t0:t1, :], bank(6 + g % 2, n * E).rearrange("p (t e) -> p t e", e=E),
                                     eoff0[:, :].unsqueeze(1).to_broadcast([P, n, E]), ALU.add))
                for k in range(2):
                    last = V.scalar_tensor_tensor(out=pick[:, k, t0:t1, :], in0=rk[:, t0:t1, :], scalar=float(k),
                                                  in1=addr[:, t0:t1, :], op0=ALU.is_equal, op1=ALU.mult)
                link(last)
                link(V.reduce_sum(slot_f[:, :, t0:t1], pick[:, :, t0:t1, :], AX.X))
                V.tensor_copy(slot_i[:, :, t0:t1], slot_f[:, :, t0:t1]).then_inc(d_slot, 1)

            dve.wait_ge(p_cnt, 1)
            counts = bank(0, E)
            link(V.tensor_tensor(pad_f[:, :], counts, eoff, ALU.add))
            V.tensor_copy(pad_i[:, :], pad_f[:, :]).then_inc(d_pad, 1)
            link(V.tensor_copy(tend[:, :], counts))
            link(V.tensor_tensor(more[:, :, :], tend[:, :].unsqueeze(2).to_broadcast([P, E, NT]),
                                 tv.unsqueeze(1).to_broadcast([P, E, NT]), ALU.is_gt))
            link(V.reduce_sum(tiles_of[:, :], more[:, :, :], AX.X))
            link(V.tensor_tensor(before_e[:, :, :], tiles_of[:, :].unsqueeze(1).to_broadcast([P, E, E]),
                                 tri[:, :, :].rearrange("p a b -> p b a"), ALU.mult))
            link(V.reduce_sum(tbase[:, :], before_e[:, :, :], AX.X))
            link(V.tensor_tensor(tend[:, :], tbase[:, :], tiles_of[:, :], ALU.add))
            one = slice(0, 1)
            link(V.tensor_scalar(gs[one, 0:1], tend[one, E - 1:E], 1.0, None, ALU.subtract))
            link(V.tensor_scalar(jeff[one, 0, :], jv[one, :], gs[one, 0:1], None, ALU.min))
            link(V.tensor_tensor(jge[one, :, :], jeff[one, 0, :].unsqueeze(2).to_broadcast([1, NST, E]),
                                 tend[one, :].unsqueeze(1).to_broadcast([1, NST, E]), ALU.is_ge))
            link(V.reduce_sum(jeff[one, 1, :], jge[one, :, :], AX.X))
            link(V.tensor_tensor(jge[one, :, :], jge[one, :, :], tend[one, :].unsqueeze(1).to_broadcast([1, NST, E]), ALU.mult))
            link(V.reduce_max(jeff[one, 2, :], jge[one, :, :], AX.X))
            link(V.tensor_tensor(jeff[one, 2, :], jeff[one, 0, :], jeff[one, 2, :], ALU.subtract))
            link(V.tensor_scalar(jeff[one, 2, :], jeff[one, 2, :], float(P), None, ALU.mult))
            link(V.scalar_tensor_tensor(out=jeff[one, 3, :], in0=jeff[one, 1, :], scalar=float(RP), in1=jeff[one, 2, :],
                                        op0=ALU.mult, op1=ALU.add))
            V.tensor_copy(tab[one, 0, :], jeff[one, 1, :])
            V.tensor_copy(tab[one, 1, :], jeff[one, 3, :]).then_inc(d_tab, 1)

            def split_x(j, z):
                dve.wait_ge(a_xh, j + 1)
                at_least(dve, p_H1, j - 1)
                V.tensor_tensor(xl[:, z, :], bank(3, D), xh[:, z, :], ALU.subtract).then_inc(d_xl, 1)

            def split_s(j, z):
                dve.wait_ge(a_sh, j + 1)
                at_least(dve, p_O, j - 1)
                V.tensor_tensor(sl[:, z, :], bank(2), sh[:, z, :], ALU.subtract).then_inc(d_sl, 1)

            def take_y(j, half, z):
                dve.wait_ge(p_O, j + 1)
                at_least(dve, s_y[z], half * 16)
                V.tensor_copy(yt[:, z, :], bank(4 + z, D)).then_inc(d_y, 1)

            def expert(j, half, z):
                if not (isinstance(j, int) and j < 1):
                    split_s(j - 1, 1 - z)
                dve.wait_ge(a_t3, j + 1)
                dve.wait_ge(p_H1, j + 1)
                at_least(dve, a_s, j)
                V.tensor_tensor(uu, bank(1), t3, ALU.mult).then_inc(d_u, 1)
                if not (isinstance(j, int) and j == NST - 1):
                    split_x(j + 1, 1 - z)
                if not (isinstance(j, int) and j < 1):
                    take_y(j - 1, half + z - 1, 1 - z)

            split_x(0, 0)
            for k in range(2):
                last = V.scalar_tensor_tensor(out=pick[:, k, :, :], in0=rk[:, :, :], scalar=float(k), in1=lg[:, :, :],
                                              op0=ALU.is_equal, op1=ALU.mult)
            link(last)
            link(V.reduce_sum(gate[:, :, :], pick[:, :, :, :], AX.X))
            link(V.scalar_tensor_tensor(out=pad_f[:, :], in0=tbase[:, :], scalar=float(P), in1=eoff0[:, :], op0=ALU.mult,
                                        op1=ALU.subtract))
            link(V.tensor_tensor(addr[:, :, :], addr[:, :, :], pad_f[:, :].unsqueeze(1).to_broadcast([P, NT, E]), ALU.add))
            for k in range(2):
                last = V.scalar_tensor_tensor(out=pick[:, k, :, :], in0=rk[:, :, :], scalar=float(k), in1=addr[:, :, :],
                                              op0=ALU.is_equal, op1=ALU.mult)
            link(last)
            link(V.reduce_sum(slot_f[:, :, :], pick[:, :, :, :], AX.X))
            V.tensor_copy(yslot_i[:, :, :], slot_f[:, :, :]).then_inc(d_ys, 1)
            over_tiles(dve, expert)
            split_s(NST - 1, (NST - 1) % 2)
            take_y(NST - 1, (NST - 1) // 2, (NST - 1) % 2)

            dve.wait_ge(c_hf, 1)

            def finish(i):
                dve.wait_ge(p_f, i + 1)
                if i >= 2:
                    dve.wait_ge(s_out[i % 2], 16 * (i // 2))
                m = tile_rows(i)
                V.tensor_tensor(ot[0:m, i % 2, :], bank(2 + i % 2, D)[0:m, :], h[0:m, i, :], ALU.add).then_inc(d_o, 1)

            for i in range(NT):
                m = tile_rows(i)
                dve.wait_ge(s_gy[i % NG], 32 * (i // NG + 1))
                if i >= 2:
                    dve.wait_ge(p_fT, i - 1)
                link(V.tensor_scalar(mt[0:m, i % 2, :], gy[0:m, i % NG, 0, :], gate[0:m, 0, i:i + 1], None, ALU.mult))
                V.scalar_tensor_tensor(out=mt[0:m, i % 2, :], in0=gy[0:m, i % NG, 1, :], scalar=gate[0:m, 1, i:i + 1],
                                       in1=mt[0:m, i % 2, :], op0=ALU.mult, op1=ALU.add).then_inc(d_mt, 1)
                if i:
                    finish(i - 1)
            finish(NT - 1)

        @block.tensor
        def _(pe):
            mm = nc.tensor.matmul
            tr = nc.tensor.transpose
            pe.wait_ge(c_const, 1)
            pe.wait_ge(s_ws, 16)
            for g in range(3):
                for f in (2 * g, 2 * g + 1):
                    off = (f // C) * (C * P) + f % C
                    for m in range(KD):
                        last = tr(bank(g)[:, D * (f % 2) + P * m:D * (f % 2) + P * (m + 1)],
                                  wtok[:, m, off:off + C * (P - 1) + 1:C], ident[:, :])
                last.then_inc(p_wt, 1)
            pe.wait_ge(s_par, 16 * NPAR)
            tr(bank(3)[:, 256:256 + NB], bqkv_raw, ident[0:NB, 0:NB])
            for c in range(C):
                o = 256 + NB + 4 * c
                last = tr(bank(3)[:, o:o + 4], lnraw[:, c:c + C * (P - 1) + 1:C], ident[0:4, 0:4])
            last.then_inc(p_b, 1)
            pe.wait_ge(d_wg, 2 * FC)
            for f in range(FC):
                last = mm(bank(3, D), ones[:, :], wTb[:, f, :], start=(f == 0), stop=(f == FC - 1))
            last.then_inc(p_cr, 1)

            def embed(i):
                pe.wait_ge(a_tT, i + 1)
                if i >= 2:
                    pe.wait_ge(d_emb, i - 1)
                for f in range(FC):
                    ch = f * P
                    last = mm(bank(i % 2, D), tT[:, i % 2, ch:ch + P], wTg[:, f, :], start=(f == 0), stop=(f == FC - 1))
                last.then_inc(p_emb, 1)

            for i in range(NI):
                pe.wait_ge(d_tok, i + 1)
                if i >= 2:
                    pe.wait_ge(a_tT, i - 1)
                for f in range(FC):
                    src = (f % C) * (PS * PS) + (f // C) * P
                    o = 2048 + 1024 * (i % 2) + P * f
                    last = tr(ps[:, o:o + P], tokn[:, i % 2, src:src + P], ident[:, :])
                last.then_inc(p_tT, 1)
                if i:
                    embed(i - 1)
            embed(NI - 1)

            pe.wait_ge(s_wt2, 16 * 5)

            def values(i):
                pe.wait_ge(a_xT, i + 1)
                if i >= 2:
                    pe.wait_ge(d_v, i - 1)
                r = tile_rows(i)
                for k in range(KD):
                    last = mm(bank(6 + i % 2, D)[0:r, :], xnT[:, k, P * i:P * i + r], wqkv[:, 2, k, :],
                              start=(k == 0), stop=(k == KD - 1))
                last.then_inc(p_v, 1)

            for i in range(NT):
                pe.wait_ge(d_xn, i + 1)
                if i >= 2:
                    pe.wait_ge(a_xT, i - 1)
                else:
                    pe.wait_ge(a_tT, NI)
                for k in range(KD):
                    last = tr(bank(4 + i % 2)[:, P * k:P * (k + 1)], xn[:, i % 2, P * k:P * (k + 1)], ident[:, :])
                last.then_inc(p_xT, 1)
                if i:
                    values(i - 1)
            values(NT - 1)
            pe.wait_ge(d_v, NT - 1)
            pe.wait_ge(a_b, 1)
            for k in range(KD):
                last = mm(bank(6, D), bv[:, k:k + 1].to_broadcast([P, P]), wp[:, k, :], start=(k == 0), stop=(k == KD - 1))
            last.then_inc(p_bv, 1)
            for u in range(4 * len(QG)):
                w, g = u // len(QG), QG[u % len(QG)]
                o = qk_bank(u)
                if g[0] < 2:
                    o = o.rearrange("p b (x y) -> p b x y", y=8)
                if u >= 4:
                    pe.wait_ge(d_lo, u - 3)
                for k in range(KD):
                    last = mm(o, wqkv[:, w // 2, k, P * (w % 2):P * (w % 2) + P], tile_cols(xnT[:, k, :], g),
                              start=(k == 0), stop=(k == KD - 1))
                last.then_inc(p_qk, 1)

            def scores(b, part):
                z = b % NS
                if part == 0:
                    pe.wait_ge(s_stack[z], 16 * 8 * (b // NS + 1))
                if part:
                    pe.wait_ge(d_mx, 2 * b + part)
                elif b:
                    pe.wait_ge(d_mc, b)
                else:
                    pe.wait_ge(d_lo, 4 * len(QG))
                if part < 2:
                    for q in range(2):
                        for j in range(4):
                            hd = 8 * part + 4 * q + j
                            mm(bank(q)[:, P * j:P * (j + 1)], stack(Qs, b, SROWS, hd, slice(0, P)), stack(Ks, b, SROWS, hd, slice(0, P)),
                               start=(j == 0), stop=False)
                        last = mm(bank(q), identb[:, :], mask_q[:, :].unsqueeze(1).to_broadcast([P, 4, P]), start=False, stop=True)
                    last.then_inc(p_S, 1)
                    return
                for g, (s0, sn) in enumerate(((0, 3), (3, 1))):
                    for j in range(4):
                        o = ps[32 * j:32 * j + 32, 512 * g:512 * g + sn * T]
                        for s in range(sn):
                            hd = 4 * (s0 + s) + j
                            mm(o[:, T * s:T * (s + 1)], stack(Qs, b, SROWS, hd, slice(P, P + 32)),
                               stack(Ks, b, SROWS, hd, slice(0, T)), start=(s == 0), stop=False,
                               tile_position=(64 * (b % 2), 32 * j))
                        last = mm(o.rearrange("p (s t) -> p s t", t=T)[:, :, P:T], identb[0:32, 0:32],
                                  mask_l[:, P:T].unsqueeze(1).to_broadcast([32, sn, TL]), start=False, stop=True,
                                  tile_position=(0, 32 * j))
                last.then_inc(p_S, 1)

            def shifted(b, part):
                z = b % NS
                R = SROWS + 2
                if part == 0:
                    pe.wait_ge(s_mrow[b % 2], 16 * (b // 2 + 1))
                if 5 * b + 2 * part:
                    pe.wait_ge(a_ex, 5 * b - 1 if part == 0 else 5 * b + (0, 2, 4)[part])
                if part < 2:
                    for q in range(2):
                        for j in range(4):
                            hd = 8 * part + 4 * q + j
                            mm(bank(2 + q)[:, P * j:P * (j + 1)], stack(Ks, b, R, hd, slice(0, P)), stack(Qs, b, R, hd, slice(0, P)),
                               start=(j == 0), stop=False)
                        last = mm(bank(2 + q), identb[:, :], mask_k[:, :].unsqueeze(1).to_broadcast([P, 4, P]), start=False, stop=True)
                    last.then_inc(p_St, 1)
                    return
                for hd in range(H):
                    mm(bank(4)[:, TL * hd:TL * (hd + 1)], stack(Ks, b, R, hd, slice(0, P)), stack(Qs, b, R, hd, slice(P, T)),
                       start=(hd == 0), stop=(hd == H - 1))
                o = ps[0:TL, 2048 + H * TL:2048 + 2 * H * TL]
                for hd in range(H):
                    mm(o[:, TL * hd:TL * (hd + 1)], stack(Ks, b, R, hd, slice(P, T)), stack(Qs, b, R, hd, slice(P, T)),
                       start=(hd == 0), stop=False)
                last = mm(o, identb[0:TL, 0:TL], mask_k[0:TL, 0:TL].unsqueeze(1).to_broadcast([TL, H, TL]), start=False, stop=True)
                last.then_inc(p_St, 1)

            def maxrows(b):
                pe.wait_ge(d_mc, b + 1)
                if b >= 2:
                    pe.wait_ge(d_at, b - 1)
                o = bank(5)[0:2 * H, 512 - T:512]
                mm(o[:, 0:P], mall[:, 0, :, :].rearrange("p s h -> p (s h)"), identh[:, :], start=True, stop=True)
                mm(o[:, P:T], mall[:, 1, :, :].rearrange("p s h -> p (s h)"), qsel[:, :], start=True, stop=True).then_inc(p_mT, 1)

            def weigh(b):
                z = b % NS
                pe.wait_ge(d_pl, 5 * b + 5)
                if b:
                    pe.wait_ge(d_at, b)
                pe.wait_ge(d_mT, min(b + 2, B))
                main = bank(5, H * (HD + 1)).rearrange("p (h d) -> p h d", h=H)
                terms = ((0, 0), (0, 1), (1, 0))
                for hd in range(H):
                    for x, y in terms:
                        mm(main[:, hd, :], pw[:, x, hd, :], Vm[:, z, y, hd, :], start=(hd == 0 and x + y == 0),
                           stop=(hd == H - 1 and x == 1))
                HK = H // KD
                for k in range(KD):
                    o = bank(6)[0:QR, HK * (HD + 1) * k:HK * (HD + 1) * (k + 1)]
                    hs = slice(HK * k, HK * (k + 1))
                    for x, y in terms:
                        mm(o, plw[:, x, 0, hs, :].rearrange("p h q -> p (h q)"),
                           Vm[:, z, y, hs, :].rearrange("p h d -> p (h d)"), start=(x + y == 0), stop=False)
                        last = mm(o, plw[0:TL, x, 1, hs, :].rearrange("p h q -> p (h q)"),
                                  Vl[:, z, y, hs, :].rearrange("p h d -> p (h d)"), start=False, stop=(x == 1))
                last.then_inc(p_pv, 1)

            def attended(b):
                pe.wait_ge(d_at, b + 1)
                if b:
                    pe.wait_ge(a_aT, b)
                o = bank(7, KD * T).rearrange("p (k t) -> p k t", k=KD)
                for k in range(KD):
                    tr(o[:, k, 0:P], at[:, :, :].rearrange("p h d -> p (h d)")[:, P * k:P * (k + 1)], ident[:, :])
                    last = mm(o[:, k, P:T], atl[0:QR, k, :], qsel2[0:QR, :], start=True, stop=True)
                last.then_inc(p_aT, 1)

            for part in range(3):
                scores(0, part)
            maxrows(0)
            for b in range(B):
                if b + 1 < B:
                    scores(b + 1, 0)
                if b:
                    weigh(b - 1)
                shifted(b, 0)
                if b + 1 < B:
                    scores(b + 1, 1)
                if b:
                    attended(b - 1)
                shifted(b, 1)
                if b + 1 < B:
                    scores(b + 1, 2)
                shifted(b, 2)
                if b + 1 < B:
                    maxrows(b + 1)
            weigh(B - 1)
            attended(B - 1)

            pe.wait_ge(a_aT, B)
            for i in range(NT):
                if i >= 2:
                    pe.wait_ge(d_pr, i - 1)
                r = tile_rows(i)
                for k in range(KD):
                    last = mm(bank(i % 2, D)[0:r, :], aT[:, k, P * i:P * i + r], wp[:, k, :], start=(k == 0),
                              stop=(k == KD - 1))
                last.then_inc(p_pj, 1)

            def logits(i):
                pe.wait_ge(a_x2, i + 1)
                g = i // 6
                for k in range(KD):
                    last = mm(bank(4 + g % 2)[:, E * (i % 6):E * (i % 6) + E], x2f[:, i % 2, k, :], wg[:, k, :], start=(k == 0),
                              stop=(k == KD - 1))
                last.then_inc(p_lg, 1)

            def rows_of(g):
                t0, n = GG[g]
                pe.wait_ge(d_ch, g + 1)
                o = bank(6 + g % 2, n * E).rearrange("p (t e) -> p t e", e=E)
                full = n if t0 + n < NT else n - 1
                mm(o, onesb[:, :], tally[:, t0:t0 + n, :], start=True, stop=False)
                last = mm(o[:, 0:full, :], before[:, :], chosen[:, t0:t0 + full, :], start=False, stop=(full == n))
                if full < n:
                    m = tile_rows(NT - 1)
                    last = mm(o[:, full, :], before[0:m, :], chosen[0:m, NT - 1, :], start=False, stop=True)
                last.then_inc(p_rk, 1)

            for i in range(NT):
                pe.wait_ge(d_x2, i + 1)
                if i >= 2:
                    pe.wait_ge(a_x2, i - 1)
                for k in range(KD):
                    last = tr(bank(2 + i % 2)[:, P * k:P * (k + 1)], xn2[:, i, P * k:P * (k + 1)], ident[:, :])
                last.then_inc(p_x2, 1)
                if i:
                    logits(i - 1)
                if i % 6 == 5 and i > 6:
                    rows_of(i // 6 - 1)
            logits(NT - 1)
            rows_of(len(GG) - 1)
            m = tile_rows(NT - 1)
            mm(bank(0, E), onesb[:, :], tally[:, NT - 1, :], start=True, stop=False)
            mm(bank(0, E), onesb[0:m, :], chosen[0:m, NT - 1, :], start=False, stop=True).then_inc(p_cnt, 1)

            def transpose_x(half, z):
                pe.wait_ge(s_xg[z], half * 16 + 16)
                for k in range(KD):
                    last = tr(bank(3)[:, P * k:P * (k + 1)], xg[:, z, P * k:P * (k + 1)], ident[:, :])
                last.then_inc(p_X, 1)

            def hidden(o, e, w, z, done):
                mm(o, sel[:, bass.ds(e, 1), :].rearrange("p e n -> p (e n)"), brow[:, HID * w:HID * (w + 1)], start=True, stop=False)
                for k in range(KD):
                    c = KD * HID * w + HID * k
                    for x, s in ((xh, 0), (xh, 1), (xl, 0)):
                        last = mm(o, x[:, z, P * k:P * (k + 1)],
                                  wres[:, s, bass.ds(e, 1), c:c + HID].rearrange("p e n -> p (e n)"), start=False,
                                  stop=(k == KD - 1 and x is xl))
                last.then_inc(done, 1)

            def transpose_s(j, z):
                pe.wait_ge(a_s, j + 1)
                at_least(pe, d_sl, j)
                for m in range(MH):
                    last = tr(bank(2)[:, P * m:P * (m + 1)], ss[:, z, P * m:P * (m + 1)], ident[:, :])
                last.then_inc(p_T, 1)

            def expert_out(j, e, z):
                pe.wait_ge(d_sl, j + 1)
                at_least(pe, d_y, j - 1)
                o = bank(4 + z, D)
                mm(o, sel[:, bass.ds(e, 1), :].rearrange("p e n -> p (e n)"), brow[:, 2 * HID:2 * HID + D], start=True, stop=False)
                for m in range(MH):
                    c = 2 * KD * HID + D * m
                    for x, s in ((sh, 0), (sh, 1), (sl, 0)):
                        last = mm(o, x[:, z, P * m:P * (m + 1)],
                                  wres[:, s, bass.ds(e, 1), c:c + D].rearrange("p e n -> p (e n)"), start=False,
                                  stop=(m == MH - 1 and x is sl))
                last.then_inc(p_O, 1)

            def expert_of(j):
                return pe.value_load(tab[0:1, 0, bass.ds(j, 1)], min_val=0, max_val=E - 1)

            def expert(j, half, z):
                e = expert_of(j)
                pe.wait_ge(d_xl, j + 1)
                at_least(pe, a_t3, j)
                hidden(bank(0), e, 1, z, p_H3)
                if not (isinstance(j, int) and j < 1):
                    transpose_s(j - 1, 1 - z)
                at_least(pe, d_u, j)
                hidden(bank(1), e, 0, z, p_H1)
                if not (isinstance(j, int) and j == NST - 1):
                    transpose_x(half + z, 1 - z)
                if not (isinstance(j, int) and j < 1):
                    expert_out(j - 1, expert_of(j - 1), 1 - z)

            pe.wait_ge(c_w, 3 * E)
            pe.wait_ge(d_tab, 1)
            transpose_x(0, 0)
            over_tiles(pe, expert)
            z = (NST - 1) % 2
            transpose_s(NST - 1, z)
            expert_out(NST - 1, expert_of(NST - 1), z)

            pe.wait_ge(s_wf, 16)

            def final(i):
                pe.wait_ge(a_fT, i + 1)
                if i >= 2:
                    pe.wait_ge(d_o, i - 1)
                m = tile_rows(i)
                for k in range(KD):
                    last = mm(bank(2 + i % 2, D)[0:m, :], fT[:, i % 2, k, 0:m], wf[:, k, :], start=(k == 0), stop=(k == KD - 1))
                last.then_inc(p_f, 1)

            pe.wait_ge(d_y, NST)
            for i in range(NT):
                m = tile_rows(i)
                pe.wait_ge(d_mt, i + 1)
                if i >= 2:
                    pe.wait_ge(a_fT, i - 1)
                for k in range(KD):
                    last = tr(bank(i % 2)[:, P * k:P * k + m], mt[0:m, i % 2, P * k:P * (k + 1)], ident[0:m, 0:m])
                last.then_inc(p_fT, 1)
                if i:
                    final(i - 1)
            final(NT - 1)


_INS = ['x', 'txt', 'L0_tok_ln1_g', 'L0_tok_ln1_b', 'L0_tok_W', 'L0_tok_b', 'L0_tok_ln2_g', 'L0_tok_ln2_b',
        'L0_attn_wq', 'L0_attn_bq', 'L0_attn_wk', 'L0_attn_bk', 'L0_attn_wv', 'L0_attn_bv', 'L0_attn_wp', 'L0_attn_bp',
        'L0_ffn_W1', 'L0_ffn_b1', 'L0_ffn_W3', 'L0_ffn_b3', 'L0_ffn_W2', 'L0_ffn_b2', 'L0_ffn_Wg', 'L0_ffn_bg',
        'L0_ffn_Wf', 'L0_ffn_bf']


def kernel(**inputs):
    import numpy as _np
    import concourse.bacc as _bacc
    from concourse import mybir as _mybir
    from concourse.bass_utils import run_bass_kernel_spmd as _run

    nc = _bacc.Bacc("TRN2", target_bir_lowering=False, num_devices=1)
    arrays, args = {}, {}
    for name in _INS:
        a = _np.ascontiguousarray(inputs[name])
        arrays[f"in_{name}"] = a
        args[name] = nc.dram_tensor(f"in_{name}", a.shape, _mybir.dt.from_np(a.dtype), kind="ExternalInput").ap()
    out = nc.dram_tensor("out_0", (16, 141, 256), _mybir.dt.float32, kind="ExternalOutput").ap()
    early_fusion_block(nc, args, out)
    r = _run(nc, [arrays], core_ids=[0])
    return r.results[0]["out_0"]
```

```python
import concourse.bass as bass
from concourse import mybir
from contextlib import ExitStack
from collections import namedtuple
import math

Step = namedtuple("Step", "j half quarter z x")


def early_fusion_block(nc, A, out):
    fp32 = mybir.dt.float32
    bf16 = mybir.dt.bfloat16
    fp16 = mybir.dt.float16
    ALU = mybir.AluOpType
    ACT = mybir.ActivationFunctionType
    AX = mybir.AxisListType

    P = 128
    B = 16
    C, PS = 3, 16
    G = 8
    IMG = G * G
    TXT = 77
    T = IMG + TXT
    TL = T - P
    N = B * T
    D = 256
    KD = D // P
    H, HD = 16, 16
    E, HID = 8, 512
    MH = HID // P
    NI = G
    NT = NI + (TXT + 7) // 8
    LAST = TXT - 8 * (NT - NI - 1)
    NP = NT * P
    EPS = 1e-5
    BIG = -1e30
    SCALE = HD ** -0.5
    FC = C * PS * PS // P
    QG = [(0, 0, 8), (0, 8, 8), (1, 0, 6), (1, 6, 5), (1, 11, 5), (2, 0, 16)]
    PART = [(0, IMG), (IMG, T - LAST), (T - LAST, T)]
    SROWS = 3 * HD
    TS = 160
    NS = 3
    WM = KD * HID
    WE = 2 * KD * HID + MH * D
    NST = (2 * N + E * (P - 1)) // P
    GG = [(0, 6), (6, 6), (12, 6)]
    GR = [(0, 12), (12, 6)]
    QR = H // KD * TL

    ORDER = list(range(NI, NT)) + list(range(NI))

    def tile_rows(i):
        return P if i < NT - 1 else B * LAST

    def flat_cols(v, g):
        part, b0, n = g
        return v.rearrange("p (b t) -> p b t", t=T)[:, b0:b0 + n, PART[part][0]:PART[part][1]]

    def tile_cols(v, g):
        part, b0, n = g
        if part == 0:
            return v[:, 0:NI * P].rearrange("p (w b hh) -> p b hh w", w=NI, b=B)[:, b0:b0 + n]
        if part == 1:
            return v[:, NI * P:(NT - 1) * P].rearrange("p (j b t) -> p b j t", b=B, t=8)[:, b0:b0 + n]
        o = (NT - 1) * P
        return v[:, o + LAST * b0:o + LAST * (b0 + n)].rearrange("p (b t) -> p b t", t=LAST)

    def tile_order(v, b, part):
        if part == 0:
            return v[:, :, 0:NI * P].rearrange("p k (w c) -> p k w c", c=P)[:, :, :, 8 * b:8 * b + 8].rearrange(
                "p k w hh -> p k hh w")
        if part == 1:
            return v[:, :, NI * P:(NT - 1) * P].rearrange("p k (j c) -> p k j c", c=P)[:, :, :, 8 * b:8 * b + 8]
        o = (NT - 1) * P + LAST * b
        return v[:, :, o:o + LAST]

    def dram_tile(v, i):
        if i < NI:
            return v[:, i:IMG:G, :]
        a = IMG + 8 * (i - NI)
        return v[:, a:min(a + 8, T), :]

    qk_dram = nc.dram_tensor("qk_scratch", (2, 2, D, N), fp16, kind="Internal").ap()
    x2_dram = nc.dram_tensor("x2_scratch", (NP, 2 * D), fp16, kind="Internal").ap()
    y_dram = nc.dram_tensor("y_scratch", (2 * NP + NST * P, D), fp32, kind="Internal").ap()
    v_dram = nc.dram_tensor("v_scratch", (B, T, 2 * H * (HD + 1)), fp16, kind="Internal").ap()

    ctx = ExitStack()
    with ctx:
        def sb(name, shape, dt=fp32):
            return ctx.enter_context(nc.sbuf_tensor(name, shape, dt))

        def sem(name):
            return ctx.enter_context(nc.semaphore(name))

        ident = sb("ident", [P, P])
        identb = sb("identb", [P, P], bf16)
        identh = sb("identh", [P, P], fp16)
        mask_q = sb("mask_q", [P, P], bf16)
        mask_k = sb("mask_k", [P, P], bf16)
        mask_l = sb("mask_l", [32, T], bf16)
        tri = sb("tri", [P, E, E])
        ones = sb("ones", [P, P])
        onesb = sb("onesb", [P, P], bf16)
        before = sb("before", [P, P], bf16)
        jmask = sb("jmask", [P, 4])
        qsel = sb("qsel", [P, TL], fp16)
        bmask = sb("bmask", [P, H // KD])
        qtmp = sb("qtmp", [P, H // KD, TL])
        qsel2 = sb("qsel2", [P, TL])
        sel = sb("sel", [P, E, P], fp16)
        brow = sb("brow", [P, 2 * HID + D], fp16)
        iota_i = sb("iota_i", [P, P + NT + 2 * NST], mybir.dt.int32)
        iota_f = sb("iota_f", [P, P + NT + 2 * NST])
        jv = iota_f[:, 0:NST]
        tv = iota_f[:, P:P + NT]
        empty = iota_f[:, P + NT:P + NT + NST]
        pv = iota_f[:, P + NT + NST:P + NT + NST + 1]
        posv = sb("posv", [P, P], fp16)

        h = sb("h", [P, NT, D])
        weights = sb("weights", [P, 2 * E * WE // 2])
        wres = weights[:, :].bitcast(fp16).rearrange("p (s e n) -> p s e n", s=2, e=E)
        shared_a = weights[:, 0:6144]
        shared_d = weights[:, 6144:12288]
        shared_b = weights[:, 12288:12288 + 9024]
        shared_c = sb("shared_c", [P, KD * NP])
        img = shared_a.rearrange("p (c y x) -> p c y x", c=C, y=PS)
        qk = shared_b.bitcast(fp16).rearrange("p (w s n) -> p w s n", w=4, s=2)
        xnT = shared_c[:, :].bitcast(fp16).rearrange("p (s k n) -> p s k n", s=2, k=KD)
        WU = WM // 2
        stage = sb("stage", [P, 2, WU])
        spare = weights[:, 21312:24576]
        SQ, SK = NS * H * TS // 2, NS * H * (T + 3) // 2
        arena = sb("arena", [P, SQ + SK + H * P])

        wtok, wT, wTg, wTb = (shared_d[:, 1536 * k:1536 * (k + 1)] for k in range(4))
        wtok = wtok.rearrange("p (k f) -> p k f", k=KD)
        wT, wTg, wTb = (w.rearrange("p (f d) -> p f d", f=FC) for w in (wT, wTg, wTb))
        tokn = arena[:, 0:2 * FC * P].rearrange("p (b n) -> p b n", b=2)
        tT = arena[:, 2 * FC * P:4 * FC * P].rearrange("p (b n) -> p b n", b=2)
        crow = shared_c[:, 0:D]
        lnraw = shared_c[0:4, D:D + C * P]
        NB = 6
        bqkv_raw = shared_c[0:NB, 1024:1024 + P]
        cols = sb("cols", [P, NB + 4 * C])
        bqk = cols[:, 0:4]
        bv = cols[:, 4:6]

        def ln1(f, w):
            k = NB + 4 * (f % C) + 2 * w + f // C
            return cols[:, k:k + 1]

        rows = spare[:, 0:4 * D].rearrange("p (r d) -> p r d", d=D)
        BTOK, G2, B2 = range(3)
        rows_h = sb("rows_h", [P, 2, D])
        BP, BF = range(2)
        bg_row = sb("bg_row", [P, E])
        wqkv = spare[:, 4 * D:10 * D].rearrange("p (w k d) -> p w k d", w=3, k=KD)
        wp = sb("wp", [P, KD, D])
        wf = sb("wf", [P, KD, D])
        wg = sb("wg", [P, KD, E])
        st = sb("st", [P, NT, 3, 6])
        mv = sb("mv", [P, NT, 2])
        ve = sb("ve", [P, NT])
        sd = sb("sd", [P, NT])
        rstd = sb("rstd", [P, NT])
        xn = sb("xn", [P, 2, D])
        vt = spare[:, 10 * D:10 * D + 2 * H * (HD + 1)].bitcast(fp16).rearrange("p (b s h d) -> p b s h d", b=2, s=2, h=H)

        Qs = arena[:, 0:SQ].bitcast(fp16).rearrange("p (z h t) -> p z h t", z=NS, h=H)
        Ks = arena[:, SQ:SQ + SK].bitcast(fp16).rearrange("p (z h t) -> p z h t", z=NS, h=H)

        def stack(t, b, heads, cols, first=0, end=P):
            return t[first:end, b % NS, heads, cols]

        pw = arena[:, SQ + SK:SQ + SK + H * P].bitcast(fp16).rearrange("p (s h q) -> p s h q", s=2, h=H)
        HQ = H // 4
        pm = [t.rearrange("p k d -> p (k d)") for t in (xn[:, :, :], wf[:, :, :])]
        w16 = arena[:, SQ + SK:SQ + SK + 6 * D].bitcast(fp16).rearrange("p (s w k d) -> p s w k d", s=2, w=3, k=KD)
        braw = arena[:, SQ + SK:SQ + SK + 2 * HID + D]
        VW = 2 * H * (HD + 1)
        Vm_flat = sb("Vm", [P, NS * VW], fp16)
        Vm = Vm_flat[:, :].rearrange("p (z s h d) -> p z s h d", z=NS, s=2, h=H)
        Vl = sb("Vl", [TL, NS, 2, H, HD + 1], fp16)
        mx = sb("mx", [P, 2, H])
        mxl = sb("mxl", [P, 4])
        mall = sb("mall", [P, 2, 2, H], fp16)
        mT = sb("mT", [2 * H, 2, T], fp16)
        pl_words = sb("pl", [P, 2 * H * TL])
        plw = sb("plw", [P, 2, 2, H, TL], fp16)
        shift = sb("shift", [P, 1])
        rd = sb("rd", [P, H])
        rdl = sb("rdl", [P, KD])
        attended = sb("attended", [P, 2 * D])
        at = attended[:, 0:D].rearrange("p (h d) -> p h d", h=H)
        atl = attended[:, D:2 * D].rearrange("p (k n) -> p k n", k=KD)
        aT = shared_c[:, :].rearrange("p (k n) -> p k n", k=KD)

        xn2 = arena[:, 0:NT * D].rearrange("p (t d) -> p t d", t=NT)
        x2hl = shared_c[:, :].bitcast(fp16).rearrange("p (t s d) -> p t s d", t=NT, s=2)
        X0 = NT * D
        ss = arena[:, X0:X0 + 2 * HID].rearrange("p (z n) -> p z n", z=2)
        x2f = arena[:, X0 + 2 * HID:X0 + 2 * HID + 2 * D].rearrange("p (z k n) -> p z k n", z=2, k=KD)
        pos_of = arena[:, 0:NT * P].bitcast(fp16).rearrange("p (m n) -> p m n", n=P)
        tile_of = arena[:, NT * P:NT * (P + 2 * NST)].bitcast(fp16).rearrange("p (m v j) -> p m v j", v=2, j=NST)
        sT = arena[:, 0:2 * HID].bitcast(fp16).rearrange("p (z s m n) -> p z s m n", z=2, s=2, m=MH)
        at_word = [0]

        def part_of(n, dt=fp32):
            a = at_word[0]
            at_word[0] += n
            return shared_c[:, a:a + n] if dt == fp32 else shared_c[:, a:a + n].bitcast(dt)

        NX = 4
        xg = part_of(NX * D, fp16).rearrange("p (z n) -> p z n", z=NX)
        xt = part_of(2 * D, fp16).rearrange("p (z s k n) -> p z s k n", z=2, s=2, k=KD)
        t3 = part_of(HID)
        uu = part_of(HID)
        sh = part_of(HID, fp16).rearrange("p (z n) -> p z n", z=2)
        sl = part_of(HID, fp16).rearrange("p (z n) -> p z n", z=2)
        yt = part_of(2 * D).rearrange("p (z d) -> p z d", z=2)
        gy = [t[:, 0:NT * D].rearrange("p (t d) -> p t d", t=NT) for t in (shared_c, arena)]
        fT = arena[:, X0:X0 + 2 * D].rearrange("p (z k n) -> p z k n", z=2, k=KD)
        NM = 4
        mt = arena[:, X0 + 2 * D:X0 + (2 + NM) * D].rearrange("p (z d) -> p z d", z=NM)
        ot = arena[:, X0 + (2 + NM) * D:X0 + (4 + NM) * D].rearrange("p (z d) -> p z d", z=2)
        i32 = mybir.dt.int32
        E0, EW = X0 + 9 * D, NT * E

        def per_expert(k, dt=fp32):
            t = arena[:, E0 + k * EW:E0 + (k + 1) * EW]
            return (t if dt == fp32 else t.bitcast(dt)[:, 0:EW]).rearrange("p (t e) -> p t e", e=E)

        lg, rk = per_expert(0), per_expert(1)
        chosen = per_expert(2, bf16)
        slots = per_expert(4)
        gs = sb("gs", [P, NT])
        CW = GR[0][1] * E * E
        cmp1, cmp2 = (Vm_flat[:, CW * k:CW * (k + 1)].bitcast(bf16).rearrange("p (t a b) -> p t a b", b=E, a=E) for k in range(2))
        pick = arena[:, E0 + 5 * EW:E0 + 7 * EW].rearrange("p (k t e) -> p k t e", k=2, t=NT)
        slot_f = sb("slot_f", [P, 2, NT])
        slot_i = sb("slot_i", [P, 2, NT], i32)
        tile_f = sb("tile_f", [P, 2, NT])
        tile_h = sb("tile_h", [P, 2, NT], fp16)
        place = sb("place", [P, 2, NT], fp16)
        jh = sb("jh", [P, NST], fp16)
        gate = sb("gate", [P, 2, NT])
        more = per_expert(3, bf16).rearrange("p t e -> p (t e)").rearrange("p (e t) -> p e t", e=E)
        tiles_of = sb("tiles_of", [P, E])
        before_e = pick[:, 0, 0:E, :]
        zero_dram = nc.dram_tensor("zero_scratch", (2, H, T), fp16, kind="Internal").ap()
        tbase = sb("tbase", [P, E])
        tend = sb("tend", [P, E])
        jge = attended[:, 0:NST * E].rearrange("p (j e) -> p j e", e=E)
        jcol = pl_words[:, 0:8 * NST].rearrange("p (r j) -> p r j", j=NST)
        src_i = sb("src_i", [P, NST], i32)
        dst_i = sb("dst_i", [P, NST], i32)
        tab = sb("tab", [1, NST], i32)

        ps = ctx.enter_context(nc.psum_tensor("ps", [P, 8 * 512], fp32))

        def bank(k, n=512):
            return ps[:, 512 * k:512 * k + n]

        s_ws = sem("wtok_in"); s_img = [sem(f"image_in{c}") for c in range(C)]; s_par = sem("params_in"); s_col = sem("columns_in"); s_row = sem("rows_in"); s_wt2 = sem("weights_in")
        s_txt = sem("text_in"); s_wf = sem("wf_in"); s_zero = sem("zeros_out"); s_vout = [sem("v_out0"), sem("v_out1")]; s_qkout = [sem("q_out"), sem("k_out")]
        s_stack = [sem(f"stack_in{z}") for z in range(NS)]; s_v = [sem(f"values_in{z}") for z in range(NS)]; s_mrow = [sem("mrow_in0"), sem("mrow_in1")]
        s_we = [sem("expert_w_in0"), sem("expert_w_in1")]; s_out = [sem("out_done0"), sem("out_done1")]
        s_x2 = sem("x2_out"); s_xg = [sem(f"xg_in{z}") for z in range(NX)]; s_y = [sem("y_out0"), sem("y_out1")]
        s_gy = [sem(f"outputs_in{g}") for g in range(3)]
        c_const = sem("consts_ready"); c_id = sem("ident_ready"); c_i0 = sem("consts_step"); c_hb = sem("h_plus_bp"); c_hf = sem("h_plus_bf")
        c_w = sem("w_split"); c_x2l = sem("x2_lo"); c_br = sem("brow_step")
        d_ = sem("vector_steps"); d_h0 = sem("h_tail_zeroed")
        d_ve = sem("var_ready"); d_wg = sem("wT_scaled");
        d_tok = sem("patch_normed"); d_emb = sem("embed_taken"); d_xn = sem("xn_ready"); d_xT = sem("xnT_lo"); d_w16 = sem("wqkv_lo"); d_v = sem("v_ready")
        d_lo = sem("qk_lo"); d_pl = sem("exp_lo"); d_bp = sem("bp_ready"); d_g = sem("image_scaled"); d_mx = sem("max_taken"); d_ml = sem("last_max_taken"); d_mc = sem("max_rows_split")
        d_mT = sem("mT_ready"); d_at = sem("attn_normed"); d_pr = sem("residual_measured"); d_r = sem("residual_added"); d_x2 = sem("xn2_ready")
        d_lg = sem("logits_shifted"); d_ch = sem("choice_ready"); d_tab = sem("table_ready"); d_oh = sem("pairs_marked"); d_xi = sem("rows_known")
        d_u = sem("u_ready"); d_sl = sem("s_lo"); d_sT = sem("sT_copied"); d_y = sem("y_ready")
        d_mt = sem("mixed_ready"); d_o = sem("o_ready")
        a_wt = sem("wT_copied"); a_sd = sem("std_ready"); a_tT = sem("patchT_copied"); a_xT = sem("xnT_copied")
        a_hi = sem("qk_hi"); a_vh = sem("v_hi"); a_w16 = sem("wqkv_hi"); a_ph = sem("exp_hi"); a_ex = sem("exp_done"); a_aT = sem("attnT_copied"); a_wh = sem("w_hi")
        a_x2 = sem("x2f_copied"); a_x2h = sem("x2_hi"); a_ge = sem("gate_exp"); a_xh = sem("x_hi"); a_t3 = sem("h3_copied")
        a_s = sem("silu_done"); a_sh = sem("s_hi"); a_b = sem("biases_copied"); a_m = sem("first_weighed"); a_fT = sem("mixT_copied")
        p_wt = sem("wT_done"); p_cr = sem("crow_done"); p_tT = sem("patchT_done"); p_emb = sem("embed_done")
        p_xT = sem("xnT_done"); p_v = sem("v_done"); p_qk = sem("qk_done"); p_S = sem("S_done"); p_St = sem("St_done")
        p_mT = sem("mT_done"); p_pv = sem("pv_done"); p_aT = sem("attnT_done"); p_pj = sem("proj_done")
        p_x2 = sem("x2T_done"); p_lg = sem("logits_done"); p_inv = sem("slots_inverted"); p_cnt = sem("counts_done")
        p_X = sem("xT_done"); p_H3 = sem("h3_done"); p_H1 = sem("h1_done"); p_T = sem("sT_done"); p_O = sem("y_done")
        p_b = sem("biasT_done"); p_bv = sem("bvWp_done"); p_fT = sem("mixT_done"); p_f = sem("final_done")

        NPAR = 9

        def at_least(eng, s, n):
            if not (isinstance(n, int) and n <= 0):
                eng.wait_ge(s, n)

        def step(j):
            return Step(j, j // 2, j // 4, j % 2, j % 4)

        def shifted_step(t, n):
            return Step(t.j + n, t.half + (t.z + n) // 2, t.quarter + (t.x + n) // 4, (t.z + n) % 2, (t.x + n) % 4)

        def over_tiles(eng, body):
            for j in range(3):
                body(step(j))
            with eng.Fori(0, (NST - 7) // 4) as i:
                for c in range(4):
                    body(Step(i * 4 + (3 + c), i * 2 + (3 + c) // 2, i + (3 + c) // 4, (3 + c) % 2, (3 + c) % 4))
            for j in range(NST - 4, NST):
                body(step(j))

        def is_step(t, *js):
            return isinstance(t.j, int) and t.j in js

        block = ctx.enter_context(nc.Block())

        def qk_bank(u):
            part, _, n = QG[u % len(QG)]
            m = PART[part][1] - PART[part][0]
            return bank(u % 4, n * m).rearrange("p (b t) -> p b t", b=n)

        @block.sync
        def _(sp):
            sp.dma_start(wtok[:, :, :], A["L0_tok_W"].rearrange("(m p) f -> p m f", p=P)).then_inc(s_ws, 16)
            for c in range(C):
                sp.dma_start(shared_a[:, 2048 * c:2048 * (c + 1)],
                             A["x"][:, c, :, :].rearrange("b (hh y) x -> b hh (y x)", y=PS)).then_inc(s_img[c], 16)
            sp.wait_ge(d_h0, 1)
            for j in range(NT - NI):
                i = NI + j
                sp.dma_start(h[0:tile_rows(i), i, :], A["txt"][:, 8 * j:min(8 * j + 8, TXT), :]).then_inc(s_txt, 16)
            for w, name in enumerate(("wq", "wk", "wv", "wp")):
                sp.dma_start(wqkv[:, w, :, :] if w < 3 else wp[:, :, :], A["L0_attn_" + name].rearrange("(k p) n -> p k n", p=P)).then_inc(s_wt2, 16)
            sp.dma_start(wg[:, :, :], A["L0_ffn_Wg"].rearrange("(k p) n -> p k n", p=P)).then_inc(s_wt2, 16)
            for n, i in enumerate(ORDER):
                sp.wait_ge(d_v, n + 1)
                sp.dma_start(dram_tile(v_dram, i), vt[0:tile_rows(i), n % 2, :, :, :].rearrange("p s h d -> p (s h d)")
                             ).then_inc(s_vout[n % 2], 16)
            sp.wait_ge(c_br, 4)
            sp.dma_start(zero_dram[:, :, :], Qs[SROWS:SROWS + 2, 0, :, 0:T]).then_inc(s_zero, 16)

            def load_side(b, w):
                for r, s in enumerate(((0, 1, 0), (0, 0, 1))[w]):
                    sp.dma_start(stack((Qs, Ks)[w], b, slice(0, H), slice(0, T), HD * r, HD * (r + 1)),
                                 qk_dram[w, s, :, b * T:(b + 1) * T].rearrange("(h d) t -> d h t", d=HD)
                                 ).then_inc(s_stack[b % NS], 16)

            def load_values(b):
                z = b % NS
                sp.dma_start(Vm[:, z, :, :, :].rearrange("p s h d -> p (s h d)"), v_dram[b, 0:P, :]).then_inc(s_v[z], 16)
                sp.dma_start(Vl[0:TL, z, :, :, :].rearrange("p s h d -> p (s h d)"), v_dram[b, P:T, :]).then_inc(s_v[z], 16)

            def load_stack(b):
                sp.wait_ge(p_St, 3 * (b - NS) + 3)
                sp.dma_start(stack(Qs, b, slice(0, H), slice(0, T), SROWS, SROWS + 2), zero_dram[:, :, :]).then_inc(s_stack[b % NS], 16)
                load_side(b, 0)
                load_side(b, 1)
                sp.wait_ge(p_pv, b - NS + 1)
                load_values(b)

            for w in range(4):
                if w == 3:
                    sp.wait_ge(s_qkout[0], 16 * 4)
                    load_side(0, 0)
                    load_side(1, 0)
                sp.wait_ge(d_lo, len(QG) * (w + 1))
                for k in range(2):
                    sp.dma_start(qk_dram[w // 2, k, P * (w % 2):P * (w % 2) + P, :], qk[:, w, k, :]).then_inc(s_qkout[w // 2], 16)
            sp.wait_ge(s_vout[0], 16 * (NT // 2))
            sp.wait_ge(s_vout[1], 16 * (NT // 2))
            load_values(0)
            load_values(1)
            load_side(2, 0)
            sp.wait_ge(s_zero, 16)
            sp.wait_ge(s_qkout[1], 16 * 4)

            def load_mrow(b):
                sp.wait_ge(d_mT, b + 1)
                sp.wait_ge(p_S, 3 * b + 3)
                sp.dma_start(stack(Qs, b, slice(0, H), slice(0, T), SROWS, SROWS + 2), mT[:, b % 2, :]).then_inc(s_mrow[b % 2], 16)

            load_side(0, 1)
            load_side(1, 1)
            load_mrow(0)
            load_side(2, 1)
            load_values(2)
            for b in range(B):
                if b + 1 < B:
                    load_mrow(b + 1)
                if b + NS < B:
                    load_stack(b + NS)

            sp.wait_ge(d_pl, 5 * B)
            sp.dma_start(wf[:, :, :], A["L0_ffn_Wf"].rearrange("(k p) n -> p k n", p=P)).then_inc(s_wf, 16)
            for g, (t0, n) in enumerate(GG):
                sp.wait_ge(c_x2l, g + 1)
                sp.dma_start(x2_dram[P * t0:P * (t0 + n), :].rearrange("(t p) n -> p t n", p=P),
                             x2hl[:, t0:t0 + n, :, :].rearrange("p t s d -> p t (s d)")).then_inc(s_x2, 16)
            sp.wait_ge(d_y, NST)
            sp.wait_ge(s_y[0], 16 * ((NST + 1) // 2))
            sp.wait_ge(s_y[1], 16 * (NST // 2))
            for g, (t0, n) in enumerate(GG):
                full = n if t0 + n < NT else n - 1
                for k in range(2):
                    o = NP * k + P * t0
                    sp.dma_start(gy[k][:, t0:t0 + full, :], y_dram[o:o + P * full, :].rearrange("(t p) d -> p t d", p=P)
                                 ).then_inc(s_gy[g], 16)
                    if full < n:
                        o += P * full
                        sp.dma_start(gy[k][0:tile_rows(NT - 1), NT - 1, :], y_dram[o:o + tile_rows(NT - 1), :]).then_inc(s_gy[g], 16)
            for i in range(NT):
                sp.wait_ge(d_o, i + 1)
                sp.dma_start(dram_tile(out, i), ot[0:tile_rows(i), i % 2, :]).then_inc(s_out[i % 2], 16)
            sp.wait_ge(s_out[0], 16 * (NT // 2))
            sp.wait_ge(s_out[1], 16 * (NT // 2))

        @block.gpsimd
        def _(pool):
            nc.gpsimd.memset(ones[:, :], 1.0)
            nc.gpsimd.memset(ident[:, :], 0.0).then_inc(c_i0, 1)
            pool.wait_ge(c_i0, 1)
            nc.gpsimd.affine_select(out=ident[:, :], in_=ident[:, :], compare_op=ALU.not_equal, fill=1.0, base=0,
                                    pattern=[[-1, P]], channel_multiplier=1).then_inc(c_id, 1)
            for k, name in ((BP, "L0_attn_bp"), (BF, "L0_ffn_bf")):
                pool.dma_start(rows_h[:, k, :], A[name].rearrange("(o n) -> o n", o=1).to_broadcast([P, D])).then_inc(s_par, 16)
            pool.dma_start(bg_row[:, :], A["L0_ffn_bg"].rearrange("(o n) -> o n", o=1).to_broadcast([P, E])).then_inc(s_par, 16)
            for p0 in (0, 32):
                for name, o, n in (("b1", 0, HID), ("b3", HID, HID), ("b2", 2 * HID, D)):
                    pool.dma_start(braw[p0:p0 + E, o:o + n], A["L0_ffn_" + name]).then_inc(s_par, 16)
            for t, v in ((identb, 0.0), (identh, 0.0), (mask_q, 0.0), (mask_k, 0.0), (mask_l, 0.0),
                         (onesb, 1.0), (before, 0.0), (jmask, 1.0), (qsel, 0.0), (bmask, 1.0), (brow, 0.0)):
                nc.gpsimd.memset(t[:, :], v)
            for t, v in ((tri, 1.0), (sel, 0.0), (qtmp, 0.0)):
                nc.gpsimd.memset(t[:, :, :], v)
            nc.gpsimd.memset(vt[:, :, 0, :, :], 1.0)
            nc.gpsimd.memset(vt[:, :, 1, :, :], 0.0)
            nc.gpsimd.memset(pl_words[:, :], 0.0)
            nc.gpsimd.memset(shift[:, :], 10.0 * math.log(2.0))
            o = P + NT
            nc.gpsimd.iota(iota_i[:, 0:P], [[1, P]], base=0, channel_multiplier=0)
            nc.gpsimd.iota(iota_i[:, P:o], [[P, NT]], base=0, channel_multiplier=0)
            nc.gpsimd.iota(iota_i[:, o:o + NST], [[P, NST]], base=2 * NP + P, channel_multiplier=1)
            nc.gpsimd.iota(iota_i[:, o + NST:o + 2 * NST], [[0, NST]], base=0, channel_multiplier=1).then_inc(c_i0, 1)
            pool.wait_ge(c_i0, 2)

            def select(t, op, fill, base, pattern, cm):
                return nc.gpsimd.affine_select(out=t, in_=t, compare_op=op, fill=fill, base=base, pattern=pattern,
                                               channel_multiplier=cm)

            for m in (identb, identh):
                select(m[:, :], ALU.not_equal, 1.0, 0, [[-1, P]], 1)
            select(mask_q[:, :], ALU.is_ge, BIG, 0, [[-1, P]], 1)
            select(mask_k[:, :], ALU.is_ge, BIG, 0, [[1, P]], -1)
            select(mask_l[:, :], ALU.is_ge, BIG, P, [[-1, T]], 1)
            select(before[:, :], ALU.is_ge, 1.0, 0, [[-1, P]], 1)
            select(tri[:, :, :], ALU.is_gt, 0.0, 0, [[-1, E], [1, E]], 0)
            select(sel[:, :, :], ALU.not_equal, 1.0, 0, [[-1, E], [0, P]], 1)
            select(bmask[:, :], ALU.is_ge, 0.0, 0, [[-TL, H // KD]], 1)
            select(qtmp[:, :, :], ALU.not_equal, 1.0, 0, [[-TL, H // KD], [-1, TL]], 1)
            select(jmask[:, :], ALU.is_ge, 0.0, 0, [[-32, 4]], 1)
            select(qsel[:, :], ALU.not_equal, 1.0, 0, [[-1, TL]], 1)
            nc.gpsimd.tensor_copy(iota_f[:, :], iota_i[:, :]).then_inc(c_i0, 1)
            pool.wait_ge(c_i0, 3)
            select(sel[:, :, :], ALU.not_equal, 1.0, -32, [[-1, E], [0, P]], 1)
            select(bmask[:, :], ALU.is_ge, 0.0, TL - 1, [[TL, H // KD]], -1)
            nc.gpsimd.tensor_copy(posv[:, :], iota_f[:, 0:P])
            nc.gpsimd.tensor_copy(jh[:, :], jv)
            nc.gpsimd.tensor_scalar(place[:, 0, :], jv[:, 0:NT], 1.0, 1.0, ALU.mult, ALU.add)
            nc.gpsimd.tensor_scalar(place[:, 1, :], jv[:, 0:NT], 1.0, 1.0 + NT, ALU.mult, ALU.add)
            select(jmask[:, :], ALU.is_ge, 0.0, 31, [[32, 4]], -1)
            select(qsel[:, :], ALU.not_equal, 1.0, -32, [[-1, TL]], 1).then_inc(c_i0, 1)
            pool.wait_ge(c_i0, 4)
            select(qsel[:, :], ALU.not_equal, 1.0, -64, [[-1, TL]], 1).then_inc(c_i0, 1)
            pool.wait_ge(c_i0, 5)
            select(qsel[:, :], ALU.not_equal, 1.0, -96, [[-1, TL]], 1).then_inc(c_const, 1)
            pool.wait_ge(s_par, 16 * NPAR)
            nc.gpsimd.tensor_copy(brow[0:E, :], braw[0:E, :]).then_inc(c_br, 1)
            pool.wait_ge(c_br, 1)
            nc.gpsimd.tensor_copy(brow[32:32 + E, :], braw[32:32 + E, :]).then_inc(c_br, 1)
            pool.wait_ge(c_br, 2)
            nc.gpsimd.tensor_tensor(brow[32:32 + E, :], braw[32:32 + E, :], brow[32:32 + E, :], ALU.subtract).then_inc(c_br, 1)
            pool.wait_ge(c_br, 3)
            pool.wait_ge(p_emb, NI)
            nc.gpsimd.memset(Qs, 0.0)
            nc.gpsimd.memset(Ks, 1.0).then_inc(c_br, 1)
            pool.wait_ge(d_xn, NT)
            pool.wait_ge(d_bp, 1)
            nc.gpsimd.tensor_tensor(h[:, :, :], h[:, :, :], rows_h[:, BP:BP + 1, :].to_broadcast([P, NT, D]), ALU.add).then_inc(c_hb, 1)

            def load_w(u):
                m = u // 2
                w = A["L0_ffn_W" + "132"[m % 3]][m // 3].rearrange("(k p) n -> p k n", p=P)
                k = w.shape[1] // 2
                pool.dma_start(stage[:, u % 2, :].rearrange("p (k n) -> p k n", k=k), w[:, k * (u % 2):k * (u % 2 + 1), :]
                               ).then_inc(s_we[u % 2], 16)

            load_w(0)
            load_w(1)
            for u in range(6 * E):
                pool.wait_ge(a_wh, u + 1)
                o = WU * (u % 6)
                nc.gpsimd.tensor_tensor(wres[:, 1, u // 6, o:o + WU], stage[:, u % 2, :], wres[:, 0, u // 6, o:o + WU],
                                        ALU.subtract).then_inc(c_w, 1)
                if u + 2 < 6 * E:
                    pool.wait_ge(c_w, u + 1)
                    load_w(u + 2)
            def gather(j):
                pool.indirect_dma_start(out=xg[:, j % NX, :], out_offset=None, in_=x2_dram[:, :],
                                        in_offset=bass.IndirectOffsetOnAxis(ap=src_i[:, j:j + 1], axis=0)).then_inc(s_xg[j % NX], 16)

            for g, (t0, n) in enumerate(GG):
                pool.wait_ge(a_x2h, g + 1)
                nc.gpsimd.tensor_tensor(x2hl[:, t0:t0 + n, 1, :], xn2[:, t0:t0 + n, :], x2hl[:, t0:t0 + n, 0, :], ALU.subtract
                                        ).then_inc(c_x2l, 1)
            pool.wait_ge(s_x2, 16 * len(GG))
            pool.wait_ge(d_xi, 1)
            for j in range(NX):
                gather(j)
            pool.wait_ge(d_x2, NT)
            nc.gpsimd.tensor_tensor(h[:, :, :], h[:, :, :], rows_h[:, BF:BF + 1, :].to_broadcast([P, NT, D]), ALU.add).then_inc(c_hf, 1)
            for j in range(NST):
                if j + NX < NST:
                    pool.wait_ge(p_X, j + 1)
                    gather(j + NX)
                pool.wait_ge(d_y, j + 1)
                pool.indirect_dma_start(out=y_dram[:, :], out_offset=bass.IndirectOffsetOnAxis(ap=dst_i[:, j:j + 1], axis=0),
                                        in_=yt[:, j % 2, :], in_offset=None).then_inc(s_y[j % 2], 16)

        @block.scalar
        def _(act):
            for w, name in enumerate(("L0_tok_ln1_g", "L0_tok_ln1_b")):
                act.dma_start(lnraw[2 * w:2 * w + 2, :], A[name].rearrange("(hf n) -> hf n", hf=2)).then_inc(s_col, 16)
            for w, name in enumerate(("L0_attn_bq", "L0_attn_bk", "L0_attn_bv")):
                act.dma_start(bqkv_raw[2 * w:2 * w + 2, :], A[name].rearrange("(m p) -> m p", p=P)).then_inc(s_col, 16)
            for k, name in ((BTOK, "L0_tok_b"), (G2, "L0_tok_ln2_g"), (B2, "L0_tok_ln2_b")):
                act.dma_start(rows[:, k, :], A[name].rearrange("(o n) -> o n", o=1).to_broadcast([P, D])).then_inc(s_row, 16)
            for g in range(3):
                act.wait_ge(p_wt, g + 1)
                nc.scalar.copy(wT[:, 2 * g:2 * g + 2, :].rearrange("p a b -> p (a b)"), bank(g)).then_inc(a_wt, 1)
            act.wait_ge(p_b, 1)
            nc.scalar.copy(cols[:, :], bank(3)[:, 256:256 + NB + 4 * C]).then_inc(a_b, 1)
            for k, (lo, hi) in enumerate(((0, 2), (2, NI))):
                act.wait_ge(d_ve, k + 1)
                nc.scalar.activation(sd[:, lo:hi], ve[:, lo:hi], ACT.Sqrt).then_inc(a_sd, 1)
            for i in range(NI):
                if i == 3:
                    act.wait_ge(d_ve, 3)
                    nc.scalar.activation(sd[:, NI:NT], ve[:, NI:NT], ACT.Sqrt).then_inc(a_sd, 1)
                if i == 5:
                    act.wait_ge(c_br, 3)
                    act.wait_ge(s_wt2, 16 * 5)
                    nc.scalar.copy(w16[:, 0, :, :, :], wqkv[:, :, :, :]).then_inc(a_w16, 1)
                act.wait_ge(p_tT, i + 1)
                if i >= 2:
                    act.wait_ge(p_emb, i - 1)
                nc.scalar.copy(tT[:, i % 2, :], ps[:, 2048 + 1024 * (i % 2):2048 + 1024 * (i % 2) + FC * P]).then_inc(a_tT, 1)

            def values_hi(n):
                act.wait_ge(p_v, n + 1)
                if n >= 2:
                    act.wait_ge(s_vout[n % 2], 16 * (n // 2))
                m = tile_rows(ORDER[n])
                nc.scalar.copy(vt[0:m, n % 2, 0, :, 0:HD], bank(6 + n % 2, D)[0:m, :].rearrange("p (h d) -> p h d", h=H)).then_inc(a_vh, 1)

            act.wait_ge(c_const, 1)
            for n, i in enumerate(ORDER):
                if n == 2:
                    act.wait_ge(d_ve, 4)
                    nc.scalar.activation(sd[:, 0:NI], ve[:, 0:NI], ACT.Sqrt).then_inc(a_sd, 1)
                if n == 7:
                    act.wait_ge(d_ve, 5)
                    nc.scalar.activation(sd[:, 0:NI], ve[:, 0:NI], ACT.Sqrt).then_inc(a_sd, 1)
                act.wait_ge(p_xT, n + 1)
                r = tile_rows(i)
                nc.scalar.copy(xnT[:, 0, :, P * i:P * i + r], bank(4 + n % 2, D).rearrange("p (k t) -> p k t", k=KD)[:, :, 0:r]
                               ).then_inc(a_xT, 1)
                if n:
                    values_hi(n - 1)
            values_hi(NT - 1)
            for u in range(4 * len(QG)):
                w, g = u // len(QG), QG[u % len(QG)]
                act.wait_ge(p_qk, u + 1)
                nc.scalar.activation(flat_cols(qk[:, w, 0, :], g), qk_bank(u), ACT.Identity,
                                     bias=bqk[:, w:w + 1]).then_inc(a_hi, 1)

            def keep_attended(b):
                act.wait_ge(p_aT, b + 1)
                o = bank(7, KD * T).rearrange("p (k t) -> p k t", k=KD)
                nc.scalar.copy(tile_order(aT, b, 0), o[:, :, 0:IMG].rearrange("p k (hh w) -> p k hh w", w=G))
                nc.scalar.copy(tile_order(aT, b, 1), o[:, :, IMG:T - LAST].rearrange("p k (j t) -> p k j t", t=8))
                nc.scalar.copy(tile_order(aT, b, 2), o[:, :, T - LAST:T]).then_inc(a_aT, 1)

            for b in range(B):
                for hf in range(2):
                    act.wait_ge(p_St, 3 * b + hf + 1)
                    for q in range(2):
                        if 4 * b + 2 * hf >= 2:
                            act.wait_ge(d_pl, 5 * b + 2 * hf + q - 1 if hf else 5 * b - 2 + q)
                        nc.scalar.activation(pm[q], bank(2 + q), ACT.Exp, bias=shift[:, 0:1], scale=SCALE).then_inc(a_ex, 1)
                    if b and not hf:
                        act.wait_ge(p_pv, b)
                    for q in range(2):
                        act.wait_ge(a_ex, 5 * b + 2 * hf + q + 1)
                        nc.scalar.copy(pw[:, 0, HQ * (2 * hf + q):HQ * (2 * hf + q + 1), :].rearrange("p h q -> p (h q)"), pm[q]
                                       ).then_inc(a_ph, 1)
                act.wait_ge(p_St, 3 * b + 3)
                if b:
                    act.wait_ge(d_pl, 5 * b)
                nc.scalar.activation(pl_words[:, 0:H * TL], bank(4, H * TL), ACT.Exp, bias=shift[:, 0:1], scale=SCALE)
                nc.scalar.activation(pl_words[0:TL, H * TL:2 * H * TL], ps[0:TL, 2048 + H * TL:2048 + 2 * H * TL],
                                     ACT.Exp, bias=shift[0:TL, 0:1], scale=SCALE).then_inc(a_ex, 1)
                act.wait_ge(a_ex, 5 * b + 5)
                nc.scalar.copy(plw[:, 0, :, :, :].rearrange("p k h q -> p (k h q)"), pl_words[:, :]).then_inc(a_ph, 1)
                if b:
                    keep_attended(b - 1)
                for u in range(3 * b, 3 * (b + 1)):
                    act.wait_ge(s_we[u % 2], 16 * (u // 2 + 1))
                    o = WU * (u % 6)
                    nc.scalar.copy(wres[:, 0, u // 6, o:o + WU], stage[:, u % 2, :]).then_inc(a_wh, 1)
            keep_attended(B - 1)
            def norm_root(g):
                t0, n = GG[g]
                act.wait_ge(d_ve, 6 + g)
                nc.scalar.activation(sd[:, t0:t0 + n], ve[:, t0:t0 + n], ACT.Sqrt).then_inc(a_sd, 1)

            norm_root(0)
            for i in range(NT):
                if i in (3, 9):
                    norm_root((i + 3) // 6)
                act.wait_ge(p_x2, i + 1)
                if i >= 2:
                    act.wait_ge(p_lg, i - 1)
                nc.scalar.copy(x2f[:, i % 2, :, :].rearrange("p k n -> p (k n)"), bank(2 + i % 2, D)).then_inc(a_x2, 1)
                if i in (9, 12, 17):
                    t0, n = GG[(9, 12, 17).index(i)]
                    act.wait_ge(d_x2, t0 + n)
                    act.wait_ge(p_pj, NT)
                    nc.scalar.copy(x2hl[:, t0:t0 + n, 0, :], xn2[:, t0:t0 + n, :]).then_inc(a_x2h, 1)
                if i == 14:
                    act.wait_ge(d_lg, 1)
                    t0, n = GR[0]
                    nc.scalar.activation(lg[:, t0:t0 + n, :], lg[:, t0:t0 + n, :], ACT.Exp).then_inc(a_ge, 1)
            act.wait_ge(d_lg, 2)
            t0, n = GR[1]
            nc.scalar.activation(lg[:, t0:t0 + n, :], lg[:, t0:t0 + n, :], ACT.Exp).then_inc(a_ge, 1)

            def take_x(t):
                act.wait_ge(p_X, t.j + 1)
                at_least(act, p_H1, t.j - 1)
                nc.scalar.copy(xt[:, t.z, :, :, :].rearrange("p s k n -> p (s k n)"), bank(3, D).bitcast(fp16)).then_inc(a_xh, 1)

            def expert(t):
                act.wait_ge(p_H3, t.j + 1)
                at_least(act, d_u, t.j)
                nc.scalar.copy(t3, bank(0)).then_inc(a_t3, 1)
                if not is_step(t, NST - 1):
                    take_x(shifted_step(t, 1))
                act.wait_ge(d_u, t.j + 1)
                at_least(act, d_sl, t.j - 1)
                nc.scalar.activation(ss[:, t.z, :], uu, ACT.Silu).then_inc(a_s, 1)
                act.wait_ge(a_s, t.j + 1)
                at_least(act, p_T, t.j - 1)
                nc.scalar.copy(sh[:, t.z, :], ss[:, t.z, :]).then_inc(a_sh, 1)

            take_x(step(0))
            over_tiles(act, expert)

            def weigh_first(i):
                act.wait_ge(s_gy[i // 6], 64 if i // 6 == 2 else 32)
                if i >= NM:
                    act.wait_ge(p_fT, i - NM + 1)
                m = tile_rows(i)
                nc.scalar.activation(mt[0:m, i % NM, :], gy[0][0:m, i, :], ACT.Copy, scale=gate[0:m, 0, i:i + 1]).then_inc(a_m, 1)

            for i in range(NM):
                weigh_first(i)
            for i in range(NT):
                act.wait_ge(p_fT, i + 1)
                if i >= 2:
                    act.wait_ge(p_f, i - 1)
                m = tile_rows(i)
                nc.scalar.copy(fT[:, i % 2, :, 0:m], bank(i % 2, D).rearrange("p (k n) -> p k n", k=KD)[:, :, 0:m]).then_inc(a_fT, 1)
                if i + NM < NT:
                    weigh_first(i + NM)

        @block.vector
        def _(dve):
            V = nc.vector
            steps = [0]

            def link(ins):
                steps[0] += 1
                ins.then_inc(d_, 1)
                dve.wait_ge(d_, steps[0])

            V.memset(h[:, NT - 1, :], 0.0).then_inc(d_h0, 1)
            for c in range(C - 1):
                dve.wait_ge(s_img[c], 16)
                for i in range(NI):
                    V.bn_stats(st[:, i, c, :], img[:, c, :, PS * i:PS * (i + 1)])
            dve.wait_ge(s_img[C - 1], 16)

            def patch_stats(lo, hi, wait):
                for i in range(lo, hi):
                    last = V.bn_stats(st[:, i, C - 1, :], img[:, C - 1, :, PS * i:PS * (i + 1)])
                link(last)
                for i in range(lo, hi):
                    last = V.bn_aggr(mv[:, i, :], st[:, i, :, :].rearrange("p a b -> p (a b)"))
                link(last)
                V.tensor_scalar(ve[:, lo:hi], mv[:, lo:hi, 1], EPS, None, ALU.add).then_inc(d_ve, 1)
                dve.wait_ge(a_sd, wait)
                link(V.reciprocal(rstd[:, lo:hi], sd[:, lo:hi]))

            def patch_norm(i):
                if i >= 2:
                    dve.wait_ge(p_tT, i - 1)
                V.tensor_scalar(tokn[:, i % 2, :].rearrange("p (c y x) -> p c y x", c=C, y=PS),
                                img[:, :, :, PS * i:PS * (i + 1)],
                                mv[:, i, 0:1], rstd[:, i:i + 1], ALU.subtract, ALU.mult).then_inc(d_tok, 1)

            def take_embed(i):
                dve.wait_ge(p_emb, i + 1)
                link(V.tensor_tensor(h[:, i, :], bank(i % 2, D), crow[:, :], ALU.add))
                V.bn_stats(st[:, i, 0, :], h[:, i, :]).then_inc(d_emb, 1)

            def norm_begin(lo, hi):
                for i in range(lo, hi):
                    last = V.bn_aggr(mv[:, i, :], st[:, i, 0, :])
                link(last)
                V.tensor_scalar(ve[:, lo:hi], mv[:, lo:hi, 1], EPS, None, ALU.add).then_inc(d_ve, 1)

            def norm_end(lo, hi, wait):
                dve.wait_ge(a_sd, wait)
                link(V.reciprocal(rstd[:, lo:hi], sd[:, lo:hi]))

            patch_stats(0, 2, 1)
            patch_norm(0)
            patch_norm(1)
            dve.wait_ge(a_wt, 3)
            dve.wait_ge(a_b, 1)
            for f in range(FC):
                V.tensor_scalar(wTg[:, f, :], wT[:, f, :], ln1(f, 0), None, ALU.mult).then_inc(d_wg, 1)
                V.tensor_scalar(wTb[:, f, :], wT[:, f, :], ln1(f, 1), None, ALU.mult).then_inc(d_wg, 1)
            patch_stats(2, NI, 2)
            dve.wait_ge(p_cr, 1)
            dve.wait_ge(s_row, 16 * 3)
            link(V.tensor_tensor(crow[:, :], bank(3, D), rows[:, BTOK, :], ALU.add))
            dve.wait_ge(s_txt, 16 * (NT - NI))
            for i in range(NI):
                if i + 2 < NI:
                    patch_norm(i + 2)
                if i == 1:
                    for j in range(NI, NT):
                        last = V.bn_stats(st[:, j, 0, :], h[:, j, :])
                    link(last)
                    norm_begin(NI, NT)
                if i == 2:
                    norm_end(NI, NT, 3)
                if i == 5:
                    dve.wait_ge(a_w16, 1)
                    V.tensor_tensor(w16[:, 1, :, :, :], wqkv[:, :, :, :], w16[:, 0, :, :, :], ALU.subtract).then_inc(d_w16, 1)
                take_embed(i)

            def take_v(n):
                dve.wait_ge(a_vh, n + 1)
                m = tile_rows(ORDER[n])
                V.tensor_tensor(vt[0:m, n % 2, 1, :, 0:HD], bank(6 + n % 2, D)[0:m, :].rearrange("p (h d) -> p h d", h=H),
                                vt[0:m, n % 2, 0, :, 0:HD], ALU.subtract).then_inc(d_v, 1)

            def block_norm(n):
                i = ORDER[n]
                if n >= 2:
                    dve.wait_ge(p_xT, n - 1)
                V.tensor_scalar(xn[:, n % 2, :], h[:, i, :], mv[:, i, 0:1], rstd[:, i:i + 1],
                                ALU.subtract, ALU.mult).then_inc(d_xn, 1)

            def image_norms(n):
                if n == 0:
                    dve.wait_ge(d_emb, NI)
                    norm_begin(0, NI)
                if n == 1:
                    norm_end(0, NI, 4)
                    for i in range(NI):
                        last = V.tensor_scalar(h[:, i, :], h[:, i, :], mv[:, i, 0:1], rstd[:, i:i + 1], ALU.subtract, ALU.mult)
                    link(last)
                half = slice(0, NI // 2) if n % 2 == 0 else slice(NI // 2, NI)
                if n in (2, 3):
                    V.tensor_tensor(h[:, half, :], h[:, half, :], rows[:, G2:G2 + 1, :].to_broadcast([P, NI // 2, D]), ALU.mult).then_inc(d_g, 1)
                if n in (4, 5):
                    dve.wait_ge(d_g, 2)
                    V.tensor_tensor(h[:, half, :], h[:, half, :], rows[:, B2:B2 + 1, :].to_broadcast([P, NI // 2, D]), ALU.add).then_inc(d_g, 1)
                if n == 5:
                    dve.wait_ge(d_g, 4)
                    for i in range(NI):
                        last = V.bn_stats(st[:, i, 0, :], h[:, i, :])
                    link(last)
                    norm_begin(0, NI)
                if n == 6:
                    norm_end(0, NI, 5)

            def take_xT(n):
                dve.wait_ge(a_xT, n + 1)
                i, m = ORDER[n], tile_rows(ORDER[n])
                V.tensor_tensor(xnT[:, 1, :, P * i:P * i + m], bank(4 + n % 2, D).rearrange("p (k t) -> p k t", k=KD)[:, :, 0:m],
                                xnT[:, 0, :, P * i:P * i + m], ALU.subtract).then_inc(d_xT, 1)

            block_norm(0)
            block_norm(1)
            take_xT(0)
            for n in range(NT):
                if n + 2 < NT:
                    block_norm(n + 2)
                if n + 1 < NT:
                    take_xT(n + 1)
                image_norms(n)
                take_v(n)
            for u in range(4 * len(QG)):
                w, g = u // len(QG), QG[u % len(QG)]
                dve.wait_ge(a_hi, u + 1)
                V.scalar_tensor_tensor(out=flat_cols(qk[:, w, 1, :], g), in0=qk_bank(u), scalar=bqk[:, w:w + 1],
                                       in1=flat_cols(qk[:, w, 0, :], g), op0=ALU.add, op1=ALU.subtract).then_inc(d_lo, 1)

            dve.wait_ge(p_bv, 1)
            dve.wait_ge(s_par, 16 * NPAR)
            V.tensor_tensor(rows_h[:, BP, :], bank(6, D), rows_h[:, BP, :], ALU.add).then_inc(d_bp, 1)

            def maxima(b, part, lo_of=None):
                dve.wait_ge(p_S, 3 * b + part + 1)
                if b and part == 0:
                    dve.wait_ge(d_mc, b)
                if part < 2:
                    V.reduce_max(mx[:, 0, 8 * part:8 * part + 8], ps[:, 0:1024].rearrange("p (h k) -> p h k", h=8), AX.X
                                 ).then_inc(d_mx, 1)
                    return
                dve.wait_ge(d_mx, 2 * b + 2)
                V.reduce_max(mxl[:, 0:3], bank(0, 3 * T).rearrange("p (h k) -> p h k", h=3), AX.X)
                V.reduce_max(mxl[:, 3:4], bank(1, T), AX.X).then_inc(d_ml, 1)
                dve.wait_ge(d_ml, b + 1)
                link(V.tensor_tensor(mx[:, 1, :].rearrange("p (a j) -> p a j", j=4), mxl[:, :].unsqueeze(2).to_broadcast([P, 4, 4]),
                                     jmask[:, :].unsqueeze(1).to_broadcast([P, 4, 4]), ALU.mult))
                if b:
                    dve.wait_ge(p_mT, b)
                link(V.tensor_scalar(mall[:, :, 0, :], mx[:, :, :], -1.0, None, ALU.mult))
                V.scalar_tensor_tensor(out=mall[:, :, 1, :], in0=mx[:, :, :], scalar=-1.0, in1=mall[:, :, 0, :],
                                       op0=ALU.mult, op1=ALU.subtract).then_inc(d_mc, 1)
                if lo_of is not None:
                    exp_lo(lo_of, 2)
                    exp_lo(lo_of, 3)
                dve.wait_ge(p_mT, b + 1)
                if b >= 2:
                    dve.wait_ge(s_mrow[b % 2], 16 * (b // 2))
                V.tensor_copy(mT[:, b % 2, :], bank(5)[0:2 * H, 512 - T:512]).then_inc(d_mT, 1)

            def normalise(b):
                dve.wait_ge(p_pv, b + 1)
                main = bank(5, H * (HD + 1)).rearrange("p (h d) -> p h d", h=H)
                rest = bank(6, H * (HD + 1))[0:QR, :].rearrange("p (k h d) -> p k h d", k=KD, d=HD + 1)
                V.reciprocal(rd[:, :], main[:, :, HD])
                link(V.reciprocal(rdl[0:QR, :], rest[:, :, 0, HD]))
                if b:
                    dve.wait_ge(p_aT, b)
                V.tensor_tensor(at[:, :, :], main[:, :, 0:HD], rd[:, :].unsqueeze(2).to_broadcast([P, H, HD]), ALU.mult)
                for k in range(KD):
                    last = V.scalar_tensor_tensor(out=atl[0:QR, k, :].rearrange("p (h d) -> p h d", d=HD), in0=rest[:, k, :, 0:HD],
                                                  scalar=rdl[0:QR, k:k + 1],
                                                  in1=bmask[0:QR, :].unsqueeze(2).to_broadcast([QR, H // KD, HD]),
                                                  op0=ALU.mult, op1=ALU.mult)
                last.then_inc(d_at, 1)

            def exp_lo(b, u):
                dve.wait_ge(a_ph, 5 * b + u + 1)
                if u < 4:
                    hs = slice(HQ * u, HQ * (u + 1))
                    V.tensor_tensor(pw[:, 1, hs, :].rearrange("p h q -> p (h q)"), pm[u % 2],
                                    pw[:, 0, hs, :].rearrange("p h q -> p (h q)"), ALU.subtract).then_inc(d_pl, 1)
                else:
                    V.tensor_tensor(plw[:, 1, :, :, :].rearrange("p k h q -> p (k h q)"), pl_words[:, :],
                                    plw[:, 0, :, :, :].rearrange("p k h q -> p (k h q)"), ALU.subtract).then_inc(d_pl, 1)

            dve.wait_ge(c_const, 1)
            link(V.reduce_sum(qsel2[:, :], qtmp[:, :, :].rearrange("p h q -> p q h"), AX.X))
            for part in range(3):
                maxima(0, part)
            for b in range(B):
                if b + 1 < B:
                    maxima(b + 1, 0)
                if b:
                    normalise(b - 1)
                if b + 1 < B:
                    maxima(b + 1, 1)
                exp_lo(b, 0)
                exp_lo(b, 1)
                if b + 1 < B:
                    maxima(b + 1, 2, lo_of=b)
                for u in range(2 if b + 1 == B else 4, 5):
                    exp_lo(b, u)
            normalise(B - 1)

            dve.wait_ge(c_hb, 1)
            def residual_stats(i):
                dve.wait_ge(d_r, i + 1)
                V.bn_stats(st[:, i, 0, :], h[:, i, :]).then_inc(d_pr, 1)

            for g, (t0, n) in enumerate(GG):
                for i in range(t0, t0 + n):
                    dve.wait_ge(p_pj, i + 1)
                    m = tile_rows(i)
                    V.tensor_tensor(h[0:m, i, :], bank((0, 1, 6, 7)[i % 4], D)[0:m, :], h[0:m, i, :], ALU.add).then_inc(d_r, 1)
                    if i > t0:
                        residual_stats(i - 1)
                residual_stats(t0 + n - 1)
                dve.wait_ge(d_pr, t0 + n)
                norm_begin(t0, t0 + n)
                norm_end(t0, t0 + n, 6 + g)
                for i in range(t0, t0 + n):
                    V.tensor_scalar(xn2[:, i, :], h[:, i, :], mv[:, i, 0:1], rstd[:, i:i + 1],
                                    ALU.subtract, ALU.mult).then_inc(d_x2, 1)

            for g, (t0, n) in enumerate(GR):
                t1 = t0 + n
                ln = lg[:, t0:t1, :]
                gn = gs[:, t0:t1]
                dve.wait_ge(p_lg, t1)
                link(V.tensor_tensor(ln, bank(4 + g % 2, n * E).rearrange("p (t e) -> p t e", e=E),
                                     bg_row[:, :].unsqueeze(1).to_broadcast([P, n, E]), ALU.add))
                link(V.reduce_max(gn, ln, AX.X))
                V.tensor_tensor(ln, ln, gn.unsqueeze(2).to_broadcast([P, n, E]), ALU.subtract).then_inc(d_lg, 1)
                dve.wait_ge(a_ge, g + 1)
                link(V.reduce_sum(gn, ln, AX.X))
                link(V.reciprocal(gn, gn))
                link(V.tensor_tensor(ln, ln, gn.unsqueeze(2).to_broadcast([P, n, E]), ALU.mult))
                this = ln.unsqueeze(3).to_broadcast([P, n, E, E])
                other = ln.unsqueeze(2).to_broadcast([P, n, E, E])
                c1, c2 = cmp1[:, 0:n, :, :], cmp2[:, 0:n, :, :]
                V.tensor_tensor(c1, other, this, ALU.is_gt)
                link(V.tensor_tensor(c2, other, this, ALU.is_equal))
                link(V.tensor_tensor(c2, c2, tri[:, :, :].unsqueeze(1).to_broadcast([P, n, E, E]), ALU.mult))
                link(V.tensor_tensor(c1, c1, c2, ALU.add))
                link(V.reduce_sum(rk[:, t0:t1, :], c1, AX.X))
                V.tensor_scalar(chosen[:, t0:t1, :], rk[:, t0:t1, :], 2.0, None, ALU.is_lt).then_inc(d_ch, 1)

            dve.wait_ge(p_cnt, 1)
            counts = bank(6, (NT + 1) * E)[:, NT * E:]
            link(V.tensor_tensor(more[:, :, :], counts.unsqueeze(2).to_broadcast([P, E, NT]),
                                 tv.unsqueeze(1).to_broadcast([P, E, NT]), ALU.is_gt))
            link(V.reduce_sum(tiles_of[:, :], more[:, :, :], AX.X))
            link(V.tensor_tensor(before_e, tiles_of[:, :].unsqueeze(1).to_broadcast([P, E, E]),
                                 tri[:, :, :].rearrange("p a b -> p b a"), ALU.mult))
            link(V.reduce_sum(tbase[:, :], before_e, AX.X))
            link(V.tensor_tensor(tend[:, :], tbase[:, :], tiles_of[:, :], ALU.add))
            link(V.tensor_scalar(tbase[:, :], tbase[:, :], float(P), None, ALU.mult))
            link(V.tensor_tensor(slots[:, :, :], bank(6, NT * E).rearrange("p (t e) -> p t e", e=E),
                                 tbase[:, :].unsqueeze(1).to_broadcast([P, NT, E]), ALU.add))
            for k in range(2):
                last = V.scalar_tensor_tensor(out=pick[:, k, :, :], in0=rk[:, :, :], scalar=float(k), in1=slots[:, :, :],
                                              op0=ALU.is_equal, op1=ALU.mult)
            link(last)
            link(V.reduce_sum(slot_f[:, :, :], pick[:, :, :, :], AX.X))
            link(V.tensor_copy(slot_i[:, :, :], slot_f[:, :, :]))
            link(V.tensor_scalar(slot_i[:, :, :], slot_i[:, :, :], 7, None, ALU.logical_shift_right))
            V.tensor_copy(tile_h[:, :, :], slot_i[:, :, :])
            link(V.tensor_copy(tile_f[:, :, :], slot_i[:, :, :]))
            link(V.scalar_tensor_tensor(out=slot_f[:, :, :], in0=tile_f[:, :, :], scalar=-float(P), in1=slot_f[:, :, :],
                                        op0=ALU.mult, op1=ALU.add))
            M = 2 * NT
            th = tile_h[:, :, :].rearrange("p k t -> p (k t)").unsqueeze(2).to_broadcast([P, M, NST])
            dve.wait_ge(p_x2, NT)
            dve.wait_ge(c_x2l, len(GG))
            link(V.tensor_tensor(tile_of[:, :, 1, :], th, jh[:, :].unsqueeze(1).to_broadcast([P, M, NST]), ALU.is_equal))
            V.tensor_tensor(tile_of[:, :, 0, :], tile_of[:, :, 1, :],
                            place[:, :, :].rearrange("p k t -> p (k t)").unsqueeze(2).to_broadcast([P, M, NST]), ALU.mult
                            ).then_inc(d_, 1)
            steps[0] += 1
            dve.wait_ge(d_, steps[0])
            V.tensor_scalar(tile_of[:, :, 1, :], tile_of[:, :, 1, :], pv, None, ALU.mult).then_inc(d_oh, 1)
            for m in range(M):
                V.tensor_scalar(pos_of[:, m, :], posv[:, :], slot_f[:, m // NT, m % NT:m % NT + 1], None, ALU.is_equal).then_inc(d_oh, 1)
            dve.wait_ge(p_inv, 1)
            pair, part = bank(1, NST), bank(1, 2 * NST)[:, NST:2 * NST]
            link(V.tensor_copy(jcol[:, 0, :], pair))
            V.scalar_tensor_tensor(out=jcol[:, 1, :], in0=jcol[:, 0, :], scalar=float(P), in1=part, op0=ALU.mult, op1=ALU.add)
            V.tensor_scalar(jcol[:, 2, :], jcol[:, 0, :], float(NT + 1), -float(NP), ALU.is_ge, ALU.mult)
            link(V.scalar_tensor_tensor(out=jcol[:, 3, :], in0=jcol[:, 0, :], scalar=1.0, in1=empty, op0=ALU.is_lt, op1=ALU.mult))
            V.tensor_tensor(jcol[:, 4, :], jcol[:, 1, :], jcol[:, 2, :], ALU.add)
            link(V.tensor_tensor(jcol[:, 5, :], jcol[:, 1, :], jcol[:, 3, :], ALU.add))
            V.tensor_scalar(src_i[:, :], jcol[:, 4, :], -float(P), 0.0, ALU.add, ALU.max)
            V.tensor_scalar(dst_i[:, :], jcol[:, 5, :], -float(P), None, ALU.add).then_inc(d_xi, 1)
            one = slice(0, 1)
            link(V.tensor_tensor(jge[one, :, :], jv[one, :].unsqueeze(2).to_broadcast([1, NST, E]),
                                 tend[one, :].unsqueeze(1).to_broadcast([1, NST, E]), ALU.is_ge))
            link(V.reduce_sum(jcol[one, 7, :], jge[one, :, :], AX.X))
            V.tensor_scalar(tab[:, :], jcol[one, 7, :], float(E - 1), None, ALU.min).then_inc(d_tab, 1)
            for k in range(2):
                last = V.scalar_tensor_tensor(out=pick[:, k, :, :], in0=rk[:, :, :], scalar=float(k), in1=lg[:, :, :],
                                              op0=ALU.is_equal, op1=ALU.mult)
            link(last)
            link(V.reduce_sum(gate[:, :, :], pick[:, :, :, :], AX.X))

            def split_s(t):
                dve.wait_ge(a_sh, t.j + 1)
                at_least(dve, p_T, t.j - 1)
                V.tensor_tensor(sl[:, t.z, :], ss[:, t.z, :], sh[:, t.z, :], ALU.subtract).then_inc(d_sl, 1)

            def keep_sT(t):
                dve.wait_ge(p_T, t.j + 1)
                at_least(dve, p_O, t.j - 1)
                V.tensor_copy(sT[:, t.z, :, :, :].rearrange("p s m n -> p (s m n)"), bank(2).bitcast(fp16)).then_inc(d_sT, 1)

            def take_y(t):
                dve.wait_ge(p_O, t.j + 1)
                at_least(dve, s_y[t.z], t.half * 16)
                V.tensor_copy(yt[:, t.z, :], bank(4 + t.z, D)).then_inc(d_y, 1)

            def expert(t):
                if not is_step(t, 0):
                    keep_sT(shifted_step(t, -1))
                dve.wait_ge(a_t3, t.j + 1)
                dve.wait_ge(p_H1, t.j + 1)
                at_least(dve, a_s, t.j)
                V.tensor_tensor(uu, bank(1), t3, ALU.mult).then_inc(d_u, 1)
                if not is_step(t, 0):
                    take_y(shifted_step(t, -1))
                split_s(t)

            over_tiles(dve, expert)
            keep_sT(step(NST - 1))
            take_y(step(NST - 1))

            dve.wait_ge(c_hf, 1)

            def finish(i):
                dve.wait_ge(p_f, i + 1)
                if i >= 2:
                    dve.wait_ge(s_out[i % 2], 16 * (i // 2))
                m = tile_rows(i)
                V.tensor_tensor(ot[0:m, i % 2, :], bank(2 + i % 2, D)[0:m, :], h[0:m, i, :], ALU.add).then_inc(d_o, 1)

            def weigh_second(i):
                m = tile_rows(i)
                dve.wait_ge(a_m, i + 1)
                V.scalar_tensor_tensor(out=mt[0:m, i % NM, :], in0=gy[1][0:m, i, :], scalar=gate[0:m, 1, i:i + 1],
                                       in1=mt[0:m, i % NM, :], op0=ALU.mult, op1=ALU.add).then_inc(d_mt, 1)

            for i in range(3):
                weigh_second(i)
            for i in range(NT):
                if i + 3 < NT:
                    weigh_second(i + 3)
                finish(i)

        @block.tensor
        def _(pe):
            mm = nc.tensor.matmul
            TERMS = ((0, 0), (0, 1), (1, 0))
            tr = nc.tensor.transpose
            pe.wait_ge(c_id, 1)
            pe.wait_ge(s_ws, 16)
            for g in range(3):
                for f in (2 * g, 2 * g + 1):
                    off = (f // C) * (C * P) + f % C
                    for m in range(KD):
                        last = tr(bank(g)[:, D * (f % 2) + P * m:D * (f % 2) + P * (m + 1)],
                                  wtok[:, m, off:off + C * (P - 1) + 1:C], ident[:, :])
                last.then_inc(p_wt, 1)
            pe.wait_ge(s_col, 16 * 5)
            tr(bank(3)[:, 256:256 + NB], bqkv_raw, ident[0:NB, 0:NB])
            for c in range(C):
                o = 256 + NB + 4 * c
                last = tr(bank(3)[:, o:o + 4], lnraw[:, c:c + C * (P - 1) + 1:C], ident[0:4, 0:4])
            last.then_inc(p_b, 1)
            def bias_through_weights():
                pe.wait_ge(d_wg, 2 * FC)
                for f in range(FC):
                    last = mm(bank(3, D), ones[:, :], wTb[:, f, :], start=(f == 0), stop=(f == FC - 1))
                last.then_inc(p_cr, 1)

            def embed(i):
                pe.wait_ge(a_tT, i + 1)
                if i >= 2:
                    pe.wait_ge(d_emb, i - 1)
                for f in range(FC):
                    ch = f * P
                    last = mm(bank(i % 2, D), tT[:, i % 2, ch:ch + P], wTg[:, f, :], start=(f == 0), stop=(f == FC - 1))
                last.then_inc(p_emb, 1)

            for i in range(NI):
                pe.wait_ge(d_tok, i + 1)
                if i >= 2:
                    pe.wait_ge(a_tT, i - 1)
                for f in range(FC):
                    src = (f % C) * (PS * PS) + (f // C) * P
                    o = 2048 + 1024 * (i % 2) + P * f
                    last = tr(ps[:, o:o + P], tokn[:, i % 2, src:src + P], ident[:, :])
                last.then_inc(p_tT, 1)
                if i == 1:
                    bias_through_weights()
                if i:
                    embed(i - 1)
            embed(NI - 1)

            pe.wait_ge(s_wt2, 16 * 5)

            def values(n):
                i = ORDER[n]
                pe.wait_ge(d_xT, n + 1)
                if n >= 2:
                    pe.wait_ge(d_v, n - 1)
                r = tile_rows(i)
                for k in range(KD):
                    for x, y in TERMS:
                        last = mm(bank(6 + n % 2, D)[0:r, :], xnT[:, x, k, P * i:P * i + r], w16[:, y, 2, k, :],
                                  start=(k + x + y == 0), stop=(k == KD - 1 and x == 1))
                last.then_inc(p_v, 1)

            pe.wait_ge(a_tT, NI)
            pe.wait_ge(d_w16, 1)
            for n in range(NT):
                pe.wait_ge(d_xn, n + 1)
                if n >= 2:
                    pe.wait_ge(d_xT, n - 1)
                for k in range(KD):
                    last = tr(bank(4 + n % 2)[:, P * k:P * (k + 1)], xn[:, n % 2, P * k:P * (k + 1)], ident[:, :])
                last.then_inc(p_xT, 1)
                if n:
                    values(n - 1)
            values(NT - 1)
            pe.wait_ge(d_v, NT - 1)
            pe.wait_ge(a_b, 1)
            for k in range(KD):
                last = mm(bank(6, D), bv[:, k:k + 1].to_broadcast([P, P]), wp[:, k, :], start=(k == 0), stop=(k == KD - 1))
            last.then_inc(p_bv, 1)
            for u in range(4 * len(QG)):
                w, g = u // len(QG), QG[u % len(QG)]
                o = qk_bank(u)
                if g[0] < 2:
                    o = o.rearrange("p b (x y) -> p b x y", y=8)
                if u >= 4:
                    pe.wait_ge(d_lo, u - 3)
                for k in range(KD):
                    for x, y in TERMS:
                        last = mm(o, w16[:, y, w // 2, k, P * (w % 2):P * (w % 2) + P], tile_cols(xnT[:, x, k, :], g),
                                  start=(k + x + y == 0), stop=(k == KD - 1 and x == 1))
                last.then_inc(p_qk, 1)

            def scores(b, part):
                z = b % NS
                if part == 0:
                    pe.wait_ge(s_stack[z], 16 * (6 + 7 * (b // NS)))
                if part:
                    pe.wait_ge(d_mx, 2 * b + part)
                elif b:
                    pe.wait_ge(d_ml, b)
                else:
                    pe.wait_ge(d_lo, 4 * len(QG))
                if part < 2:
                    for q in range(2):
                        for j in range(4):
                            hd = 8 * part + 4 * q + j
                            mm(bank(q)[:, P * j:P * (j + 1)], stack(Qs, b, hd, slice(0, P)), stack(Ks, b, hd, slice(0, P)),
                               start=(j == 0), stop=False)
                        last = mm(bank(q), identb[:, :], mask_q[:, :].unsqueeze(1).to_broadcast([P, 4, P]), start=False, stop=True)
                    last.then_inc(p_S, 1)
                    return
                for g, (s0, sn) in enumerate(((0, 3), (3, 1))):
                    for j in range(4):
                        o = ps[32 * j:32 * j + 32, 512 * g:512 * g + sn * T]
                        for s in range(sn):
                            hd = 4 * (s0 + s) + j
                            mm(o[:, T * s:T * (s + 1)], stack(Qs, b, hd, slice(P, P + 32)),
                               stack(Ks, b, hd, slice(0, T)), start=(s == 0), stop=False, tile_position=(0, 32 * j))
                        last = mm(o.rearrange("p (s t) -> p s t", t=T)[:, :, P:T], identb[0:32, 0:32],
                                  mask_l[:, P:T].unsqueeze(1).to_broadcast([32, sn, TL]), start=False, stop=True,
                                  tile_position=(0, 32 * j))
                last.then_inc(p_S, 1)

            def shifted(b, part):
                if part == 0:
                    pe.wait_ge(s_mrow[b % 2], 16 * (b // 2 + 1))
                if b or part == 1:
                    pe.wait_ge(a_ex, 5 * b + (-1, 2, 0)[part])
                if part < 2:
                    for q in range(2):
                        for j in range(4):
                            hd = 8 * part + 4 * q + j
                            mm(bank(2 + q)[:, P * j:P * (j + 1)], stack(Ks, b, hd, slice(0, P)), stack(Qs, b, hd, slice(0, P)),
                               start=(j == 0), stop=False)
                        last = mm(bank(2 + q), identb[:, :], mask_k[:, :].unsqueeze(1).to_broadcast([P, 4, P]), start=False, stop=True)
                    last.then_inc(p_St, 1)
                    return
                for hd in range(H):
                    mm(bank(4)[:, TL * hd:TL * (hd + 1)], stack(Ks, b, hd, slice(0, P)), stack(Qs, b, hd, slice(P, T)),
                       start=(hd == 0), stop=(hd == H - 1))
                o = ps[0:TL, 2048 + H * TL:2048 + 2 * H * TL]
                for hd in range(H):
                    mm(o[:, TL * hd:TL * (hd + 1)], stack(Ks, b, hd, slice(P, T)), stack(Qs, b, hd, slice(P, T)),
                       start=(hd == 0), stop=False)
                last = mm(o, identb[0:TL, 0:TL], mask_k[0:TL, 0:TL].unsqueeze(1).to_broadcast([TL, H, TL]), start=False, stop=True)
                last.then_inc(p_St, 1)

            def maxrows(b):
                pe.wait_ge(d_mc, b + 1)
                if b >= 2:
                    pe.wait_ge(d_at, b - 1)
                o = bank(5)[0:2 * H, 512 - T:512]
                mm(o[:, 0:P], mall[:, 0, :, :].rearrange("p s h -> p (s h)"), identh[:, :], start=True, stop=True)
                mm(o[:, P:T], mall[:, 1, :, :].rearrange("p s h -> p (s h)"), qsel[:, :], start=True, stop=True).then_inc(p_mT, 1)

            def weigh_main(b):
                z = b % NS
                if b:
                    pe.wait_ge(d_at, b)
                pe.wait_ge(d_mT, min(b + 2, B))
                pe.wait_ge(s_v[z], 32 * (b // NS + 1))
                main = bank(5, H * (HD + 1)).rearrange("p (h d) -> p h d", h=H)
                for hd in range(H):
                    if hd % (H // 2) == 0:
                        pe.wait_ge(d_pl, 5 * b + 2 + 2 * (hd // (H // 2)))
                    for x, y in TERMS:
                        mm(main[:, hd, :], pw[:, x, hd, :], Vm[:, z, y, hd, :], start=(hd == 0 and x + y == 0),
                           stop=(hd == H - 1 and x == 1))

            def weigh_rest(b):
                z = b % NS
                HK = H // KD
                pe.wait_ge(d_pl, 5 * b + 5)
                for k in range(KD):
                    o = bank(6)[0:QR, HK * (HD + 1) * k:HK * (HD + 1) * (k + 1)]
                    hs = slice(HK * k, HK * (k + 1))
                    for x, y in TERMS:
                        mm(o, plw[:, x, 0, hs, :].rearrange("p h q -> p (h q)"),
                           Vm[:, z, y, hs, :].rearrange("p h d -> p (h d)"), start=(x + y == 0), stop=False)
                        last = mm(o, plw[0:TL, x, 1, hs, :].rearrange("p h q -> p (h q)"),
                                  Vl[:, z, y, hs, :].rearrange("p h d -> p (h d)"), start=False, stop=(x == 1))
                last.then_inc(p_pv, 1)

            def attended(b):
                pe.wait_ge(d_at, b + 1)
                if b:
                    pe.wait_ge(a_aT, b)
                o = bank(7, KD * T).rearrange("p (k t) -> p k t", k=KD)
                for k in range(KD):
                    tr(o[:, k, 0:P], at[:, :, :].rearrange("p h d -> p (h d)")[:, P * k:P * (k + 1)], ident[:, :])
                    last = mm(o[:, k, P:T], atl[0:QR, k, :], qsel2[0:QR, :], start=True, stop=True)
                last.then_inc(p_aT, 1)

            for part in range(3):
                scores(0, part)
            scores(1, 0)
            maxrows(0)
            for b in range(B):
                if b:
                    weigh_main(b - 1)
                    weigh_rest(b - 1)
                shifted(b, 0)
                if b + 1 < B:
                    scores(b + 1, 1)
                if b:
                    attended(b - 1)
                shifted(b, 1)
                if b + 1 < B:
                    scores(b + 1, 2)
                shifted(b, 2)
                if b + 2 < B:
                    scores(b + 2, 0)
                if b + 1 < B:
                    maxrows(b + 1)
            weigh_main(B - 1)
            weigh_rest(B - 1)
            attended(B - 1)

            pe.wait_ge(a_aT, B)
            def project(i):
                if i >= 4:
                    pe.wait_ge(d_r, i - 3)
                m = tile_rows(i)
                for k in range(KD):
                    last = mm(bank((0, 1, 6, 7)[i % 4], D)[0:m, :], aT[:, k, P * i:P * i + m], wp[:, k, :], start=(k == 0),
                              stop=(k == KD - 1))
                last.then_inc(p_pj, 1)

            def logits(i):
                pe.wait_ge(a_x2, i + 1)
                g = i // GR[0][1]
                c = E * (i - GR[g][0])
                for k in range(KD):
                    last = mm(bank(4 + g)[:, c:c + E], x2f[:, i % 2, k, :], wg[:, k, :], start=(k == 0),
                              stop=(k == KD - 1))
                last.then_inc(p_lg, 1)

            def rows_of(g):
                pe.wait_ge(d_ch, g + 1)
                o = bank(6, (NT + 1) * E).rearrange("p (t e) -> p t e", e=E)
                t0, n = GR[g]
                for i in range(t0, t0 + n):
                    m = tile_rows(i)
                    mm(o[:, i, :], before[0:m, :], chosen[0:m, i, :], start=(i == 0), stop=False)
                    last = mm(o[:, i + 1:NT + 1, :], onesb[0:m, :], chosen[0:m, i, :].unsqueeze(1).to_broadcast([m, NT - i, E]),
                              start=False, stop=(i == NT - 1))
                if g == len(GR) - 1:
                    last.then_inc(p_cnt, 1)

            def norm_logits(g):
                t0, n = GG[g]
                for i in range(t0, t0 + n):
                    pe.wait_ge(d_x2, i + 1)
                    if i >= 2:
                        pe.wait_ge(a_x2, i - 1)
                    for k in range(KD):
                        last = tr(bank(2 + i % 2)[:, P * k:P * (k + 1)], xn2[:, i, P * k:P * (k + 1)], ident[:, :])
                    last.then_inc(p_x2, 1)
                    if i:
                        logits(i - 1)

            for i in range(GG[2][0]):
                project(i)
            norm_logits(0)
            for i in range(GG[2][0], NT):
                project(i)
            norm_logits(1)
            norm_logits(2)
            logits(NT - 1)
            rows_of(0)
            rows_of(1)

            for i in range(2 * NT):
                pe.wait_ge(d_oh, i + 2)
                m = tile_rows(i % NT)
                last = mm(bank(1, 2 * NST), pos_of[0:m, i, :], tile_of[0:m, i, :, :].rearrange("p v j -> p (v j)"), start=(i == 0),
                          stop=(i == 2 * NT - 1))
            last.then_inc(p_inv, 1)

            def transpose_x(t):
                pe.wait_ge(s_xg[t.x], t.quarter * 16 + 16)
                for c in range(2 * KD):
                    last = tr(bank(3, D).bitcast(fp16)[:, P * c:P * (c + 1)], xg[:, t.x, P * c:P * (c + 1)], identh[:, :])
                last.then_inc(p_X, 1)

            def hidden(o, e, w, z, done):
                mm(o, sel[:, bass.ds(e, 1), :].rearrange("p e n -> p (e n)"), brow[:, HID * w:HID * (w + 1)], start=True, stop=False)
                for k in range(KD):
                    c = KD * HID * w + HID * k
                    for x, s in ((0, 0), (0, 1), (1, 0)):
                        last = mm(o, xt[:, z, x, k, :], wres[:, s, bass.ds(e, 1), c:c + HID].rearrange("p e n -> p (e n)"),
                                  start=False, stop=(k == KD - 1 and x == 1))
                last.then_inc(done, 1)

            def transpose_s(t):
                pe.wait_ge(d_sl, t.j + 1)
                at_least(pe, d_sT, t.j)
                for s, src in enumerate((sh, sl)):
                    for m in range(MH):
                        o = P * (MH * s + m)
                        last = tr(bank(2).bitcast(fp16)[:, o:o + P], src[:, t.z, P * m:P * (m + 1)], identh[:, :])
                last.then_inc(p_T, 1)

            def expert_out(t, e):
                pe.wait_ge(d_sT, t.j + 1)
                at_least(pe, d_y, t.j - 1)
                o = bank(4 + t.z, D)
                mm(o, sel[:, bass.ds(e, 1), :].rearrange("p e n -> p (e n)"), brow[:, 2 * HID:2 * HID + D], start=True, stop=False)
                for m in range(MH):
                    c = 2 * KD * HID + D * m
                    for x, s in ((0, 0), (0, 1), (1, 0)):
                        last = mm(o, sT[:, t.z, x, m, :], wres[:, s, bass.ds(e, 1), c:c + D].rearrange("p e n -> p (e n)"),
                                  start=False, stop=(m == MH - 1 and x == 1))
                last.then_inc(p_O, 1)

            def expert_of(t):
                return pe.value_load(tab[0:1, bass.ds(t.j, 1)], min_val=0, max_val=E - 1)

            held = {}

            def expert(t):
                if is_step(t, 0, NST - 4) or (not isinstance(t.j, int) and t.x == 3):
                    held["this"] = expert_of(t)
                    held["last"] = None if is_step(t, 0) else expert_of(shifted_step(t, -1))
                e, last_e = held["this"], held["last"]
                pe.wait_ge(a_xh, t.j + 1)
                at_least(pe, a_t3, t.j)
                hidden(bank(0), e, 1, t.z, p_H3)
                if not is_step(t, NST - 1):
                    transpose_x(shifted_step(t, 1))
                if not is_step(t, 0):
                    transpose_s(shifted_step(t, -1))
                at_least(pe, d_u, t.j)
                hidden(bank(1), e, 0, t.z, p_H1)
                if not is_step(t, 2, NST - 1) and (isinstance(t.j, int) or t.x != 2):
                    held["this"] = expert_of(shifted_step(t, 1))
                held["last"] = e
                if not is_step(t, 0):
                    expert_out(shifted_step(t, -1), last_e)

            pe.wait_ge(c_w, 6 * E)
            pe.wait_ge(d_tab, 1)
            transpose_x(step(0))
            over_tiles(pe, expert)
            transpose_s(step(NST - 1))
            expert_out(step(NST - 1), held["last"])

            pe.wait_ge(s_wf, 16)

            def final(i):
                pe.wait_ge(a_fT, i + 1)
                if i >= 2:
                    pe.wait_ge(d_o, i - 1)
                m = tile_rows(i)
                for k in range(KD):
                    last = mm(bank(2 + i % 2, D)[0:m, :], fT[:, i % 2, k, 0:m], wf[:, k, :], start=(k == 0), stop=(k == KD - 1))
                last.then_inc(p_f, 1)

            pe.wait_ge(d_y, NST)
            for i in range(NT):
                m = tile_rows(i)
                pe.wait_ge(d_mt, i + 1)
                if i >= 2:
                    pe.wait_ge(a_fT, i - 1)
                for k in range(KD):
                    last = tr(bank(i % 2)[:, P * k:P * k + m], mt[0:m, i % NM, P * k:P * (k + 1)], ident[0:m, 0:m])
                last.then_inc(p_fT, 1)
                if i:
                    final(i - 1)
            final(NT - 1)


_INS = ['x', 'txt', 'L0_tok_ln1_g', 'L0_tok_ln1_b', 'L0_tok_W', 'L0_tok_b', 'L0_tok_ln2_g', 'L0_tok_ln2_b',
        'L0_attn_wq', 'L0_attn_bq', 'L0_attn_wk', 'L0_attn_bk', 'L0_attn_wv', 'L0_attn_bv', 'L0_attn_wp', 'L0_attn_bp',
        'L0_ffn_W1', 'L0_ffn_b1', 'L0_ffn_W3', 'L0_ffn_b3', 'L0_ffn_W2', 'L0_ffn_b2', 'L0_ffn_Wg', 'L0_ffn_bg',
        'L0_ffn_Wf', 'L0_ffn_bf']


def kernel(**inputs):
    import numpy as _np
    import concourse.bacc as _bacc
    from concourse import mybir as _mybir
    from concourse.bass_utils import run_bass_kernel_spmd as _run

    nc = _bacc.Bacc("TRN2", target_bir_lowering=False, num_devices=1)
    arrays, args = {}, {}
    for name in _INS:
        a = _np.ascontiguousarray(inputs[name])
        arrays[f"in_{name}"] = a
        args[name] = nc.dram_tensor(f"in_{name}", a.shape, _mybir.dt.from_np(a.dtype), kind="ExternalInput").ap()
    out = nc.dram_tensor("out_0", (16, 141, 256), _mybir.dt.float32, kind="ExternalOutput").ap()
    early_fusion_block(nc, args, out)
    r = _run(nc, [arrays], core_ids=[0])
    return r.results[0]["out_0"]
```
